# Optimizing a Trainium2 kernel written in Bass

```python
import numpy as np
import jax
import jax.numpy as jnp

def _softmax(x, axis=-1):
    return jax.nn.softmax(x, axis=axis)

def _gelu(x):
    return jax.nn.gelu(x, approximate=True)

def _silu(x):
    return jax.nn.silu(x)

def _sigmoid(x):
    return jax.nn.sigmoid(x)

def _layernorm(x, axis=-1, eps=1e-05):
    m = jnp.mean(x, axis=axis, keepdims=True)
    v = jnp.var(x, axis=axis, keepdims=True)
    return (x - m) / jnp.sqrt(v + eps)

def _scatter_add(tgt, idx, src, axis=0):
    return tgt.at[idx].add(src)

def _segment_sum(src, seg, n):
    return jax.ops.segment_sum(src, seg, n)
kernel_name = 'mk_adaln_d2_jaxref_r8_1ec53c'

def setup_inputs(seed: int=0):
    np.random.seed(seed)
    _w = jnp.asarray

    def _L0_attn_setup():
        import jax, jax.numpy as jnp
        import numpy as np
        D_MODEL, D_STATE, D_CONV, EXPAND = (128, 16, 4, 2)
        D_INNER = EXPAND * D_MODEL
        BATCH, SEQ = (2, 256)

        def _forward(x, in_proj_w, conv_w, conv_b, dt_w, dt_b, A_log, D, B_w, C_w, out_w):
            xz = x @ in_proj_w.T
            xc, z = jnp.split(xz, 2, axis=-1)
            h = jnp.transpose(xc, (0, 2, 1))
            h = jnp.pad(h, ((0, 0), (0, 0), (D_CONV - 1, 0)))
            h = jax.lax.conv_general_dilated(h, conv_w, (1,), 'VALID', dimension_numbers=('NCH', 'OIH', 'NCH'))
            h = h + conv_b[None, :, None]
            u = jnp.transpose(h, (0, 2, 1))
            dt = jnp.clip(jax.nn.sigmoid(u @ dt_w.T + dt_b), 0.0001, 1.0)
            A = -jnp.exp(A_log)
            Bm = u @ B_w.T
            Cm = u @ C_w.T
            u_t = jnp.transpose(u, (1, 0, 2))
            dt_t = jnp.transpose(dt, (1, 0, 2))
            B_t = jnp.transpose(Bm, (1, 0, 2))
            C_t = jnp.transpose(Cm, (1, 0, 2))

            def step(state, inp):
                ut, dtt, bt, ct = inp
                dA = jnp.exp(jnp.clip(dtt[:, :, None] * A, -5.0, 5.0))
                dB = dtt[:, :, None] * bt[:, None, :] * ut[:, :, None]
                state = dA * state + dB + 1e-06
                y = jnp.sum(state * ct[:, None, :], axis=-1) + D * ut
                return (state, y)
            state0 = jnp.zeros((x.shape[0], D_INNER, D_STATE), x.dtype)
            _, ys = jax.lax.scan(step, state0, (u_t, dt_t, B_t, C_t))
            y = jnp.transpose(ys, (1, 0, 2))
            y = y * jax.nn.silu(z)
            return y @ out_w.T
        key = jax.random.key(seed)
        ks = jax.random.split(key, 10)
        inv = lambda n: 1.0 / np.sqrt(n)
        return {'x': jax.random.normal(ks[0], (BATCH, SEQ, D_MODEL), jnp.float32), 'in_proj_w': jax.random.uniform(ks[1], (2 * D_INNER, D_MODEL), jnp.float32, -inv(D_MODEL), inv(D_MODEL)), 'conv_w': jax.random.uniform(ks[2], (D_INNER, D_INNER, D_CONV), jnp.float32, -inv(D_INNER * D_CONV), inv(D_INNER * D_CONV)), 'conv_b': jax.random.uniform(ks[3], (D_INNER,), jnp.float32, -inv(D_INNER * D_CONV), inv(D_INNER * D_CONV)), 'dt_w': jax.random.uniform(ks[4], (D_INNER, D_INNER), jnp.float32, -inv(D_INNER), inv(D_INNER)), 'dt_b': jax.random.uniform(ks[5], (D_INNER,), jnp.float32, -inv(D_INNER), inv(D_INNER)), 'A_log': jax.random.normal(ks[6], (D_INNER, D_STATE), jnp.float32) * 0.01, 'D': jnp.ones((D_INNER,), jnp.float32), 'B_w': jax.random.uniform(ks[7], (D_STATE, D_INNER), jnp.float32, -inv(D_INNER), inv(D_INNER)), 'C_w': jax.random.uniform(ks[8], (D_STATE, D_INNER), jnp.float32, -inv(D_INNER), inv(D_INNER)), 'out_w': jax.random.uniform(ks[9], (D_MODEL, D_INNER), jnp.float32, -inv(D_INNER), inv(D_INNER))}
    _L0_attn_in = _L0_attn_setup()

    def _L0_ffn_setup():
        import jax, jax.numpy as jnp
        import numpy as np
        B, S, D, O, E, R, TOP_K = (4, 128, 128, 128, 8, 16, 2)
        SCALING = 32.0 / 16.0
        NEG_INF = -1000000000.0
        key = jax.random.key(seed)
        ks = jax.random.split(key, 6)
        return {'x': jax.random.normal(ks[0], (B, S, D), jnp.float32), 'base_w': jax.random.normal(ks[1], (O, D), jnp.float32) * 0.02, 'base_b': jnp.zeros((O,), jnp.float32), 'lora_A': jax.random.normal(ks[2], (E, D, R), jnp.float32) * 0.02, 'lora_B': jax.random.normal(ks[3], (E, R, O), jnp.float32) * 0.02, 'router_w': jax.random.normal(ks[4], (E, D), jnp.float32) * 0.02, 'router_b': jnp.zeros((E,), jnp.float32)}
    _L0_ffn_in = _L0_ffn_setup()
    _L0_c = _w((lambda *s: np.random.randn(*s).astype(np.float32) * 0.05)(8, 128))
    _L0_wmod = _w((lambda *s: np.random.randn(*s).astype(np.float32) * 0.05)(128, 6 * 128) * 128 ** (-0.5))

    def _L1_attn_setup():
        import jax, jax.numpy as jnp
        import numpy as np
        B, L, HID = (8, 1025, 128)
        H, KV, DH = (16, 4, 64)
        EPS = 1e-06
        ROPE_BASE = 10000.0

        def _rms_norm(x, w):
            var = jnp.mean(jnp.square(x), axis=-1, keepdims=True)
            return x * jax.lax.rsqrt(var + EPS) * w

        def _rotate_half(x):
            x1, x2 = jnp.split(x, 2, axis=-1)
            return jnp.concatenate([-x2, x1], axis=-1)

        def _rope_cache(seq_len, dim):
            inv_freq = 1.0 / ROPE_BASE ** (jnp.arange(0, dim, 2, dtype=jnp.float32) / dim)
            pos = jnp.arange(seq_len, dtype=jnp.float32)
            freqs = pos[:, None] * inv_freq[None, :]
            emb = jnp.concatenate([freqs, freqs], axis=-1)
            return (jnp.cos(emb), jnp.sin(emb))
        key = jax.random.key(seed)
        ks = jax.random.split(key, 5)
        s_in = 1.0
        s_q = float(np.sqrt(2.0 / (HID + H * DH)))
        s_kv = float(np.sqrt(2.0 / (HID + KV * DH)))
        s_o = float(np.sqrt(2.0 / (H * DH + HID)) / np.sqrt(2.0))
        return {'inputs': jax.random.normal(ks[0], (B, L, HID), jnp.float32) * s_in, 'Wq': jax.random.normal(ks[1], (H * DH, HID), jnp.float32) * s_q, 'Wk': jax.random.normal(ks[2], (KV * DH, HID), jnp.float32) * s_kv, 'Wv': jax.random.normal(ks[3], (KV * DH, HID), jnp.float32) * s_kv, 'Wo': jax.random.normal(ks[4], (HID, H * DH), jnp.float32) * s_o, 'q_norm_w': jnp.ones((DH,), jnp.float32), 'k_norm_w': jnp.ones((DH,), jnp.float32)}
    _L1_attn_in = _L1_attn_setup()

    def _L1_ffn_setup():
        import jax, jax.numpy as jnp
        import numpy as np
        DIM = 128

        def _reference_tuple_inner(x, W_r, W_k, W_v, mu_r, mu_k):
            B, T, C = x.shape
            x_prev = jnp.concatenate([jnp.zeros((B, 1, C), x.dtype), x[:, :-1, :]], axis=1)
            xr = mu_r * x + (1.0 - mu_r) * x_prev
            xk = mu_k * x + (1.0 - mu_k) * x_prev
            r = jax.nn.sigmoid(jnp.einsum('btc,dc->btd', xr, W_r))
            k = jnp.einsum('btc,dc->btd', xk, W_k)
            k_act = jnp.square(jax.nn.relu(k))
            out = r * jnp.einsum('btc,dc->btd', k_act, W_v)
            new_state = x[:, -1, :]
            return (out, new_state)
        key = jax.random.key(seed)
        ks = jax.random.split(key, 6)
        B, T, C = (8, 256, DIM)
        x = jax.random.normal(ks[0], (B, T, C), dtype=jnp.float32)
        s = 1.0 / np.sqrt(C)
        W_r = jax.random.uniform(ks[1], (C, C), jnp.float32, -s, s)
        W_k = jax.random.uniform(ks[2], (C, C), jnp.float32, -s, s)
        W_v = jax.random.uniform(ks[3], (C, C), jnp.float32, -s, s)
        mu_r = jax.random.uniform(ks[4], (C,), jnp.float32)
        mu_k = jax.random.uniform(ks[5], (C,), jnp.float32)
        return {'x': x, 'W_r': W_r, 'W_k': W_k, 'W_v': W_v, 'mu_r': mu_r, 'mu_k': mu_k}
    _L1_ffn_in = _L1_ffn_setup()
    _L1_c = _w((lambda *s: np.random.randn(*s).astype(np.float32) * 0.05)(8, 128))
    _L1_wmod = _w((lambda *s: np.random.randn(*s).astype(np.float32) * 0.05)(128, 6 * 128) * 128 ** (-0.5))
    _d = {'L0_attn_x': _L0_attn_in['x'], 'L0_attn_in_proj_w': _L0_attn_in['in_proj_w'], 'L0_attn_conv_w': _L0_attn_in['conv_w'], 'L0_attn_conv_b': _L0_attn_in['conv_b'], 'L0_attn_dt_w': _L0_attn_in['dt_w'], 'L0_attn_dt_b': _L0_attn_in['dt_b'], 'L0_attn_A_log': _L0_attn_in['A_log'], 'L0_attn_D': _L0_attn_in['D'], 'L0_attn_B_w': _L0_attn_in['B_w'], 'L0_attn_C_w': _L0_attn_in['C_w'], 'L0_attn_out_w': _L0_attn_in['out_w'], 'L0_ffn_base_w': _L0_ffn_in['base_w'], 'L0_ffn_base_b': _L0_ffn_in['base_b'], 'L0_ffn_lora_A': _L0_ffn_in['lora_A'], 'L0_ffn_lora_B': _L0_ffn_in['lora_B'], 'L0_ffn_router_w': _L0_ffn_in['router_w'], 'L0_ffn_router_b': _L0_ffn_in['router_b'], 'L0_c': _L0_c, 'L0_wmod': _L0_wmod, 'L1_attn_Wq': _L1_attn_in['Wq'], 'L1_attn_Wk': _L1_attn_in['Wk'], 'L1_attn_Wv': _L1_attn_in['Wv'], 'L1_attn_Wo': _L1_attn_in['Wo'], 'L1_attn_q_norm_w': _L1_attn_in['q_norm_w'], 'L1_attn_k_norm_w': _L1_attn_in['k_norm_w'], 'L1_ffn_W_r': _L1_ffn_in['W_r'], 'L1_ffn_W_k': _L1_ffn_in['W_k'], 'L1_ffn_W_v': _L1_ffn_in['W_v'], 'L1_ffn_mu_r': _L1_ffn_in['mu_r'], 'L1_ffn_mu_k': _L1_ffn_in['mu_k'], 'L1_c': _L1_c, 'L1_wmod': _L1_wmod}
    _x0 = _d['L0_attn_x']
    _d['L0_attn_x'] = jax.random.normal(jax.random.fold_in(jax.random.key(seed), 1), (8, 256, 128), dtype=_x0.dtype)
    del _x0
    return _d

def reference(L0_attn_x, L0_attn_in_proj_w, L0_attn_conv_w, L0_attn_conv_b, L0_attn_dt_w, L0_attn_dt_b, L0_attn_A_log, L0_attn_D, L0_attn_B_w, L0_attn_C_w, L0_attn_out_w, L0_ffn_base_w, L0_ffn_base_b, L0_ffn_lora_A, L0_ffn_lora_B, L0_ffn_router_w, L0_ffn_router_b, L0_c, L0_wmod, L1_attn_Wq, L1_attn_Wk, L1_attn_Wv, L1_attn_Wo, L1_attn_q_norm_w, L1_attn_k_norm_w, L1_ffn_W_r, L1_ffn_W_k, L1_ffn_W_v, L1_ffn_mu_r, L1_ffn_mu_k, L1_c, L1_wmod):

    def _L0_attn_ref(x, in_proj_w, conv_w, conv_b, dt_w, dt_b, A_log, D, B_w, C_w, out_w):
        import jax, jax.numpy as jnp
        import numpy as np
        D_MODEL, D_STATE, D_CONV, EXPAND = (128, 16, 4, 2)
        D_INNER = EXPAND * D_MODEL
        BATCH, SEQ = (2, 256)

        def _forward(x, in_proj_w, conv_w, conv_b, dt_w, dt_b, A_log, D, B_w, C_w, out_w):
            xz = x @ in_proj_w.T
            xc, z = jnp.split(xz, 2, axis=-1)
            h = jnp.transpose(xc, (0, 2, 1))
            h = jnp.pad(h, ((0, 0), (0, 0), (D_CONV - 1, 0)))
            h = jax.lax.conv_general_dilated(h, conv_w, (1,), 'VALID', dimension_numbers=('NCH', 'OIH', 'NCH'))
            h = h + conv_b[None, :, None]
            u = jnp.transpose(h, (0, 2, 1))
            dt = jnp.clip(jax.nn.sigmoid(u @ dt_w.T + dt_b), 0.0001, 1.0)
            A = -jnp.exp(A_log)
            Bm = u @ B_w.T
            Cm = u @ C_w.T
            u_t = jnp.transpose(u, (1, 0, 2))
            dt_t = jnp.transpose(dt, (1, 0, 2))
            B_t = jnp.transpose(Bm, (1, 0, 2))
            C_t = jnp.transpose(Cm, (1, 0, 2))

            def step(state, inp):
                ut, dtt, bt, ct = inp
                dA = jnp.exp(jnp.clip(dtt[:, :, None] * A, -5.0, 5.0))
                dB = dtt[:, :, None] * bt[:, None, :] * ut[:, :, None]
                state = dA * state + dB + 1e-06
                y = jnp.sum(state * ct[:, None, :], axis=-1) + D * ut
                return (state, y)
            state0 = jnp.zeros((x.shape[0], D_INNER, D_STATE), x.dtype)
            _, ys = jax.lax.scan(step, state0, (u_t, dt_t, B_t, C_t))
            y = jnp.transpose(ys, (1, 0, 2))
            y = y * jax.nn.silu(z)
            return y @ out_w.T
        return _forward(x, in_proj_w, conv_w, conv_b, dt_w, dt_b, A_log, D, B_w, C_w, out_w)

    def _L0_ffn_ref(x, base_w, base_b, lora_A, lora_B, router_w, router_b):
        import jax, jax.numpy as jnp
        import numpy as np
        B, S, D, O, E, R, TOP_K = (4, 128, 128, 128, 8, 16, 2)
        SCALING = 32.0 / 16.0
        NEG_INF = -1000000000.0
        result = jnp.einsum('bsd,od->bso', x, base_w) + base_b
        ax = jnp.einsum('bsd,edr->bser', x, lora_A)
        bax = jnp.einsum('bser,ero->bseo', ax, lora_B)
        logits = jnp.einsum('bsd,ed->bse', x, router_w) + router_b
        kth = jax.lax.top_k(logits, TOP_K)[0][..., -1:]
        masked = jnp.where(logits < kth, NEG_INF, logits)
        expert_weights = jax.nn.softmax(masked, axis=-1)
        return result + SCALING * jnp.einsum('bse,bseo->bso', expert_weights, bax)

    def _L1_attn_ref(inputs, Wq, Wk, Wv, Wo, q_norm_w, k_norm_w):
        import jax, jax.numpy as jnp
        import numpy as np
        B, L, HID = (8, 1025, 128)
        H, KV, DH = (16, 4, 64)
        EPS = 1e-06
        ROPE_BASE = 10000.0

        def _rms_norm(x, w):
            var = jnp.mean(jnp.square(x), axis=-1, keepdims=True)
            return x * jax.lax.rsqrt(var + EPS) * w

        def _rotate_half(x):
            x1, x2 = jnp.split(x, 2, axis=-1)
            return jnp.concatenate([-x2, x1], axis=-1)

        def _rope_cache(seq_len, dim):
            inv_freq = 1.0 / ROPE_BASE ** (jnp.arange(0, dim, 2, dtype=jnp.float32) / dim)
            pos = jnp.arange(seq_len, dtype=jnp.float32)
            freqs = pos[:, None] * inv_freq[None, :]
            emb = jnp.concatenate([freqs, freqs], axis=-1)
            return (jnp.cos(emb), jnp.sin(emb))
        b, l, _ = inputs.shape
        q = (inputs @ Wq.T).reshape(b, l, H, DH)
        k = (inputs @ Wk.T).reshape(b, l, KV, DH)
        v = (inputs @ Wv.T).reshape(b, l, KV, DH)
        q = _rms_norm(q, q_norm_w).transpose(0, 2, 1, 3)
        k = _rms_norm(k, k_norm_w).transpose(0, 2, 1, 3)
        v = v.transpose(0, 2, 1, 3)
        l_img = l - 1
        cos, sin = _rope_cache(l_img, DH)
        cos = cos[None, None].astype(q.dtype)
        sin = sin[None, None].astype(q.dtype)
        q_img = q[:, :, 1:]
        k_img = k[:, :, 1:]
        q = jnp.concatenate([q[:, :, :1], q_img * cos + _rotate_half(q_img) * sin], axis=2)
        k = jnp.concatenate([k[:, :, :1], k_img * cos + _rotate_half(k_img) * sin], axis=2)
        rep = H // KV
        k = jnp.repeat(k, rep, axis=1)
        v = jnp.repeat(v, rep, axis=1)
        scores = jnp.einsum('bhqd,bhkd->bhqk', q, k)
        attn = jax.nn.softmax(scores.astype(jnp.float32), axis=-1).astype(q.dtype)
        out = jnp.einsum('bhqk,bhkd->bhqd', attn, v)
        out = out.transpose(0, 2, 1, 3).reshape(b, l, H * DH)
        return out @ Wo.T

    def _L1_ffn_ref(x, W_r, W_k, W_v, mu_r, mu_k):
        import jax, jax.numpy as jnp
        import numpy as np
        DIM = 128

        def _reference_tuple_inner(x, W_r, W_k, W_v, mu_r, mu_k):
            B, T, C = x.shape
            x_prev = jnp.concatenate([jnp.zeros((B, 1, C), x.dtype), x[:, :-1, :]], axis=1)
            xr = mu_r * x + (1.0 - mu_r) * x_prev
            xk = mu_k * x + (1.0 - mu_k) * x_prev
            r = jax.nn.sigmoid(jnp.einsum('btc,dc->btd', xr, W_r))
            k = jnp.einsum('btc,dc->btd', xk, W_k)
            k_act = jnp.square(jax.nn.relu(k))
            out = r * jnp.einsum('btc,dc->btd', k_act, W_v)
            new_state = x[:, -1, :]
            return (out, new_state)
        return _reference_tuple_inner(x, W_r, W_k, W_v, mu_r, mu_k)[0]
    x = L0_attn_x
    mod = (_silu(L0_c) @ L0_wmod).reshape(L0_c.shape[0], 6, 1, -1)
    sa, ca, ga, sb, cb, gb = (mod[:, 0], mod[:, 1], mod[:, 2], mod[:, 3], mod[:, 4], mod[:, 5])
    ga = (2 * (ga >= 0) - 1) * jnp.maximum(jnp.abs(ga), 0.25)
    gb = (2 * (gb >= 0) - 1) * jnp.maximum(jnp.abs(gb), 0.25)
    h = _layernorm(x, axis=-1) * (1 + ca) + sa
    x = x + ga * _L0_attn_ref(h, L0_attn_in_proj_w, L0_attn_conv_w, L0_attn_conv_b, L0_attn_dt_w, L0_attn_dt_b, L0_attn_A_log, L0_attn_D, L0_attn_B_w, L0_attn_C_w, L0_attn_out_w)
    h = _layernorm(x, axis=-1) * (1 + cb) + sb
    x = x + gb * _L0_ffn_ref(h, L0_ffn_base_w, L0_ffn_base_b, L0_ffn_lora_A, L0_ffn_lora_B, L0_ffn_router_w, L0_ffn_router_b)
    mod = (_silu(L1_c) @ L1_wmod).reshape(L1_c.shape[0], 6, 1, -1)
    sa, ca, ga, sb, cb, gb = (mod[:, 0], mod[:, 1], mod[:, 2], mod[:, 3], mod[:, 4], mod[:, 5])
    ga = (2 * (ga >= 0) - 1) * jnp.maximum(jnp.abs(ga), 0.25)
    gb = (2 * (gb >= 0) - 1) * jnp.maximum(jnp.abs(gb), 0.25)
    h = _layernorm(x, axis=-1) * (1 + ca) + sa
    x = x + ga * _L1_attn_ref(h, L1_attn_Wq, L1_attn_Wk, L1_attn_Wv, L1_attn_Wo, L1_attn_q_norm_w, L1_attn_k_norm_w)
    h = _layernorm(x, axis=-1) * (1 + cb) + sb
    x = x + gb * _L1_ffn_ref(h, L1_ffn_W_r, L1_ffn_W_k, L1_ffn_W_v, L1_ffn_mu_r, L1_ffn_mu_k)
    return x

_drawn_inputs = setup_inputs


def setup_inputs(seed=0):
    import zlib

    import numpy as np

    out = dict(_drawn_inputs(seed))
    spreads = {'L0_attn_D': (1.0, 0.6),
     'L0_ffn_base_b': (0.0, 2.0),
     'L0_ffn_router_b': (0.0, 2.0),
     'L1_attn_q_norm_w': (1.0, 0.6),
     'L1_attn_k_norm_w': (1.0, 0.6)}
    factors = {'L0_attn_in_proj_w': 2.816,
     'L0_attn_conv_b': 8.0,
     'L0_attn_dt_w': 8.0,
     'L0_attn_dt_b': 8.0,
     'L0_attn_A_log': 8.0,
     'L0_attn_B_w': 8.0,
     'L0_attn_C_w': 8.0,
     'L0_attn_out_w': 2.679,
     'L0_ffn_lora_A': 7.373,
     'L0_ffn_lora_B': 7.359,
     'L0_ffn_router_w': 24.027,
     'L1_ffn_W_r': 8.0,
     'L1_ffn_W_k': 3.005,
     'L1_ffn_W_v': 2.773,
     'L1_ffn_mu_r': 8.0,
     'L1_ffn_mu_k': 4.696,
     'L0_ffn_base_w': 8.0,
     'L1_attn_Wq': 5.998,
     'L1_attn_Wk': 6.199,
     'L1_attn_Wv': 6.03,
     'L1_attn_Wo': 5.825}
    for name, (base, spread) in spreads.items():
        noise = np.random.default_rng([zlib.crc32(name.encode()), seed]).standard_normal(out[name].shape)
        drawn = base * np.exp(spread * noise) if base else spread * noise
        out[name] = jnp.asarray(drawn.astype(out[name].dtype))
    for name, factor in factors.items():
        out[name] = (out[name] * factor).astype(out[name].dtype)
    return out
```

```python
from contextlib import ExitStack

import concourse.bass as bass
from concourse import mybir

F32 = mybir.dt.float32
BF16 = mybir.dt.bfloat16
I32 = mybir.dt.int32
ALU = mybir.AluOpType
ACT = mybir.ActivationFunctionType
AX = mybir.AxisListType

P = 128
B, T = 8, 256
NT = T // P
DI = 256
ND = DI // P
NS = 16
TAPS = 4
PAD = TAPS - 1
E, R = 8, 16
H, KV, DH = 16, 4, 64
REP = H // KV
HK = H + KV
NF = H * DH // P
LN_EPS, RMS_EPS, STATE_EPS = 1e-5, 1e-6, 1e-6
EXP5, EXPM5 = 148.4131591025766, 0.006737946999085467
RSQRT_SEED = 0x5F3759DF
NEWTON = 3
LN_STEPS = 4 + 3 * NEWTON

EVENTS = dict(
    x_in=16, ln0=LN_STEPS, ln1=LN_STEPS, ln2=LN_STEPS, ln3=LN_STEPS, rms=2 + 3 * NEWTON,
    xn0=1, xn1=1, xn2=1, xn3=1, h_ps0=1, h_ps1=1, h_ps2=1, h_ps3=1, h1=1, h2=1, h3=1, h4=1,
    u_ps=1, z_ps=1, uT=1, thz=1, gz=1, dt_ps=1, thd=1, dt=3, bc_ps=1, bc_hi=1, bc_rest=3, bc3=1,
    bb_ps=8, cb_ps=8, dA=8, db=8, dbe=8, dac=8, scan=8, ys=8, y_ps=8, y1=1, yT=1,
    o0_ps=1, g0=1, x1=1, ax_ps=1, lg_ps=1, top=6, el=1, wx=1, wt_ps=1, wT=1, axw=1, f0_ps=1, g1=1, x2=1,
    qkv_ps=6, qs=6, sq=6, va=2, ssq=2, rotc=2, rots=2, rsum=2, qr=4, qT_ps=6, qT=6, qTb=6,
    ms_ps=16, mx=16, mn=2, mn_ps=1, negm=1,
    sc_ps=16, pt=16, av=16, rinv=8, on=8, ot_ps=4, ot=4, o1_ps=1, g2=1, x3=1,
    dd=1, xk=1, xr=1, kk_ps=1, rr_ps=1, kr=1, ka=1, thr=1, vv_ps=1, t4=2, x4=1, out=16,
)


def build(nc, d, out):
    ctx = ExitStack()
    with ctx:
        def sb(name, shape, dt=F32):
            return ctx.enter_context(nc.sbuf_tensor(name, shape, dt))

        def sem(name):
            return ctx.enter_context(nc.semaphore(name))

        w_inx = sb("w_inx", [P, ND, P])
        w_cin = sb("w_cin", [P, TAPS, DI])
        w_z = sb("w_z", [P, DI])
        w_dt = sb("w_dt", [P, ND, DI])
        w_bc = sb("w_bc", [P, ND, 96])
        w_out = sb("w_out", [P, ND, P])
        w_base = sb("w_base", [P, P])
        w_la = sb("w_la", [P, E * R])
        w_lb = sb("w_lb", [E * R, P])
        w_rt = sb("w_rt", [P, E])
        w_qkv = sb("w_qkv", [P, (H + 2 * KV) * DH])
        w_o = sb("w_o", [P, NF, P])
        w_r = sb("w_r", [P, P])
        w_k = sb("w_k", [P, P])
        w_v = sb("w_v", [P, P])
        cT = sb("cT", [P, 2, B])
        cols = sb("cols", [P, 3 * ND + 2])
        a_log = sb("a_log", [P, ND, NS])
        neg_a = sb("neg_a", [P, ND, NS])
        hdtb = sb("hdtb", [P, ND])
        rows = sb("rows", [1, P + E])
        norm_w = sb("norm_w", [P, 2, DH])
        cs = sb("cs", [P, NT, 2, DH])
        rot_c = sb("rot_c", [P, NT, HK, DH])
        rot_s = sb("rot_s", [P, NT, HK, DH])
        ident = sb("ident", [P, P])
        identb = sb("identb", [P, P], BF16)
        sel = sb("sel", [96, 2 * NS, P], BF16)
        onehot = sb("onehot", [P, H, P], BF16)
        pick = sb("pick", [P, 32 + H])
        ones_row = sb("ones_row", [1, P])
        cth = sb("cth", [P, 2, B])
        csil = sb("csil", [P, 2, B])
        mod_t = sb("mod_t", [P, 2, 4, B])
        gate = sb("gate", [B, 2, 2, P])
        gabs = sb("gabs", [B, 2, 2, P])
        gates = sb("gates", [P, B, 2, 2, P])
        gate_dram = nc.dram_tensor("gate_scratch", (B, 2, 2, P), F32, kind="Internal").ap()

        x0 = sb("x0", [P, NT, P])
        x1 = sb("x1", [P, NT, P])
        x2 = sb("x2", [P, NT, P])
        x3 = sb("x3", [P, NT, P])
        x4 = sb("x4", [P, NT, P])
        tmp_g = sb("tmp_g", [P, NT, P])
        stats = sb("stats", [P, NT, 6])
        mv = sb("mv", [P, NT, 2])
        lnv = sb("lnv", [P, 3, NT])
        xn = [sb(f"xn{n}", [P, NT, P]) for n in range(4)]
        h1 = sb("h1", [P, PAD + T])
        h2 = sb("h2", [P, T])
        h3 = sb("h3", [P, T])
        h4 = sb("h4", [P, 1 + T])
        uT = sb("uT", [P, ND, T])
        thz = sb("thz", [P, ND, T])
        gz = sb("gz", [P, ND, T])
        thd = sb("thd", [P, ND, T])
        dt = sb("dt", [P, ND, T])
        dtu = sb("dtu", [P, ND, T])
        bc3 = sb("bc3", [96, T], BF16)
        bc_r = sb("bc_r", [96, T])
        bc_m = sb("bc_m", [96, T], BF16)
        scan_mem = sb("scan_mem", [P, 6, ND * 2 * T])
        dA, dB, st = ([scan_mem[:, 2 * k + n, :].rearrange("p (c m t) -> p c m t", c=ND, m=2) for n in range(2)]
                      for k in range(3))
        scan_flat = scan_mem[:].rearrange("p k x -> p (k x)")
        qn = scan_flat[:, 0:NT * HK * DH].rearrange("p (t h f) -> p t h f", t=NT, h=HK)
        sq = scan_flat[:, NT * HK * DH:2 * NT * HK * DH].rearrange("p (t h f) -> p t h f", t=NT, h=HK)
        w_conv = scan_flat[:, 0:ND * TAPS * DI].rearrange("p (c j o) -> p c j o", c=ND, j=TAPS)
        w_mod = scan_flat[:, ND * TAPS * DI:ND * TAPS * DI + 12 * P].rearrange("p (l j f) -> p l j f", l=2, j=6)
        y1 = sb("y1", [P, ND, T])
        yT = sb("yT", [P, ND, T])
        lg = sb("lg", [P, NT, E])
        m8 = sb("m8", [P, NT, 8])
        nm = sb("nm", [P, NT])
        el = sb("el", [P, NT, E])
        em = sb("em", [P, NT, E])
        es = sb("es", [P, NT])
        er = sb("er", [P, NT])
        wx = sb("wx", [P, NT, E, R])
        wT = sb("wT", [P, T])
        axw = sb("axw", [P, T])
        qs = sb("qs", [P, NT, HK, DH])
        qc = sb("qc", [P, NT * HK * DH])
        oT = qc[:, 0:NF * T].rearrange("p (f t) -> p f t", f=NF)
        qc = qc[:].rearrange("p (t h f) -> p t h f", t=NT, h=HK)
        rv = sb("rv", [P, 4, NT, HK])
        qr = sb("qr", [P, NT, H + 2 * KV, DH])
        on = qr[:, :, 0:H, :]
        qT = sb("qT", [P, NF + KV, T])
        qTb = sb("qTb", [P, NF + KV, T], BF16)
        va = sb("va", [P, NT, KV, DH + 1])
        mx = sb("mx", [P, NT, H])
        mn = sb("mn", [P, NT, P], BF16)
        negm = sb("negm", [P, T], BF16)
        pt = [sb(f"pt{n}", [P, NT, T]) for n in range(2)]
        rinv = sb("rinv", [P, 2, 4])
        dd = sb("dd", [P, T])
        xk = sb("xk", [P, T])
        xr = sb("xr", [P, T])
        kr = sb("kr", [P, T])
        ka = sb("ka", [P, T])
        thr = sb("thr", [P, NT, P])
        t4 = sb("t4", [P, NT, P])

        bank = {n: ctx.enter_context(nc.psum_tensor(f"ps_{n}", [P, 512], F32))
                for n in ("B", "C", "Y", "S0", "S1", "O0", "O1", "M")}
        S = {name: sem(f"s_{name}") for name in EVENTS}
        s_w0, s_w1, s_w2, s_const, s_consts, s_pick = (sem(n) for n in ("s_w0", "s_w1", "s_w2", "s_const", "s_consts", "s_pick"))
        s_pre_act, s_pre_dve, s_pre_pe, s_gate, s_gates, s_rot = (
            sem(n) for n in ("s_pre_act", "s_pre_dve", "s_pre_pe", "s_gate", "s_gates", "s_rot"))

        s_passed = sem("s_passed")

        def at(name, i, k=None):
            n = EVENTS[name]
            return i * n + (n if k is None else k)

        def wait_apart(eng, name, value):
            eng.wait_ge(S[name], value)
            eng.sem_inc(s_passed, 1)

        def halves(bk, n=256):
            return bank[bk][:, 0:2 * n].rearrange("p (a b) -> p a b", a=2)

        loads_early = [
            (cT[:], d["cT"]), (w_mod, d["wmod"]), (w_inx[:], d["w_inx"]), (w_conv, d["w_conv"]),
            (w_z[:], d["w_z"]), (cols[:], d["cols"]), (a_log[:], d["a_log"]), (pick[:], d["pick"]),
            (w_dt[:], d["w_dt"]), (w_bc[:], d["w_bc"]), (cs[:], d["cs"]),
        ]
        loads_late = [
            (w_out[:], d["w_out"]), (w_base[:], d["w_base"]), (w_la[:], d["w_la"]), (w_lb[:], d["w_lb"]),
            (w_rt[:], d["w_rt"]), (rows[:], d["rows"]), (norm_w[:], d["norm_w"]), (w_qkv[:], d["w_qkv"]),
            (w_o[:], d["w_o"]), (w_r[:], d["w_r"]), (w_k[:], d["w_k"]), (w_v[:], d["w_v"]),
        ]
        EARLY, LATE = 16 * len(loads_early), 16 * len(loads_late)
        x_view = d["x"].rearrange("b (t p) f -> b p t f", p=P)
        out_view = out.rearrange("b (t p) f -> b p t f", p=P)
        block = ctx.enter_context(nc.Block())

        @block.sync
        def _(sp):
            sp.dma_start(x0[:], x_view[0]).then_inc(S["x_in"], 16)
            for dst, src in loads_early:
                sp.dma_start(dst, src).then_inc(s_w0, 16)
            for dst, src in loads_late:
                sp.dma_start(dst, src).then_inc(s_w1, 16)
            sp.wait_ge(s_gate, 1)
            sp.dma_start(gate_dram, gate[:]).then_inc(s_gates, 16)
            sp.wait_ge(s_gates, 16)
            sp.dma_start(gates[:].rearrange("p b l g f -> p (b l g f)"),
                         gate_dram.rearrange("b l g f -> (b l g f)").partition_broadcast(P)).then_inc(s_gates, 16)

            def turn(i, load, store):
                if load:
                    sp.wait_ge(S["x1"], at("x1", i, 0))
                    sp.dma_start(x0[:], x_view[i]).then_inc(S["x_in"], 16)
                if store:
                    sp.wait_ge(S["x4"], at("x4", i - 1))
                    sp.dma_start(out_view[i - 1], x4[:]).then_inc(S["out"], 16)

            with sp.Fori(1, B) as i:
                turn(i, True, True)
            turn(B, False, True)
            sp.wait_ge(S["out"], 16 * B)

        @block.gpsimd
        def _(pool):
            nc.gpsimd.memset(ident[:], 0.0).then_inc(s_const, 1)
            nc.gpsimd.memset(ones_row[:], 1.0).then_inc(s_consts, 1)
            nc.gpsimd.memset(h1[:, 0:PAD], 0.0).then_inc(s_consts, 1)
            nc.gpsimd.memset(h4[:, 0:1], 0.0).then_inc(s_consts, 1)
            nc.gpsimd.memset(va[:, :, :, DH:DH + 1], 1.0).then_inc(s_consts, 1)
            nc.gpsimd.memset(mn[:], 0.0).then_inc(s_consts, 1)
            pool.wait_ge(s_const, 1)
            nc.gpsimd.affine_select(out=ident[:], in_=ident[:], compare_op=ALU.not_equal, fill=1.0, base=0,
                                    pattern=[[-1, P]], channel_multiplier=1).then_inc(s_const, 1)
            pool.wait_ge(s_const, 2)
            nc.gpsimd.tensor_copy(identb[:], ident[:]).then_inc(s_consts, 1)
            pool.wait_ge(s_w0, EARLY)
            nc.gpsimd.tensor_copy(sel[:], pick[0:96, 0:32].unsqueeze(2).broadcast_to((96, 32, P))).then_inc(s_consts, 1)
            nc.gpsimd.tensor_copy(onehot[:], pick[:, 32:32 + H].unsqueeze(2).broadcast_to((P, H, P))).then_inc(s_consts, 1)
            pool.wait_ge(s_w1, LATE)
            for which, (lo, n) in enumerate(((0, H), (H, KV))):
                for t in range(NT):
                    nc.gpsimd.tensor_tensor(
                        rot_c[:, t, lo:lo + n, :], cs[:, t, 0, :].unsqueeze(1).broadcast_to((P, n, DH)),
                        norm_w[:, which, :].unsqueeze(1).broadcast_to((P, n, DH)), ALU.mult).then_inc(s_rot, 1)
                    for a, b in ((0, DH // 2), (DH // 2, 0)):
                        m = DH // 2
                        nc.gpsimd.tensor_tensor(
                            rot_s[:, t, lo:lo + n, a:a + m], cs[:, t, 1, a:a + m].unsqueeze(1).broadcast_to((P, n, m)),
                            norm_w[:, which, b:b + m].unsqueeze(1).broadcast_to((P, n, m)), ALU.mult).then_inc(s_rot, 1)

            def pairs(i):
                for p in range(8):
                    wait_apart(pool, "db", at("db", i, p + 1))
                    nc.gpsimd.tensor_scalar(dB[p % 2], dB[p % 2], 1.0, STATE_EPS, ALU.mult, ALU.add)\
                        .then_inc(S["dbe"], 1)

            def rotate(i):
                for t in range(NT):
                    pool.wait_ge(S["qs"], at("qs", i, 3 * t + 3))
                    if t == 0:
                        pool.wait_ge(s_rot, 12)
                    m = DH // 2
                    pool.wait_ge(S["rsum"], at("rsum", i, 0))
                    nc.gpsimd.tensor_tensor(qn[:, t, :, 0:m], qs[:, t, :, m:DH], rot_s[:, t, :, 0:m], ALU.mult)
                    nc.gpsimd.tensor_tensor(qn[:, t, :, m:DH], qs[:, t, :, 0:m], rot_s[:, t, :, m:DH], ALU.mult)\
                        .then_inc(S["rots"], 1)

            pairs(0)
            rotate(0)
            with pool.Fori(1, B) as i:
                pairs(i)
                rotate(i)

        @block.scalar
        def _(act):
            act.wait_ge(s_w0, EARLY)
            nc.scalar.activation(cth[:], cT[:], ACT.Tanh, scale=0.5).then_inc(s_pre_act, 1)
            nc.scalar.activation(neg_a[:], a_log[:], ACT.Exp).then_inc(s_pre_act, 1)
            nc.scalar.mul(hdtb[:], cols[:, ND:2 * ND], 0.5).then_inc(s_pre_act, 1)
            act.wait_ge(s_pre_act, 2)
            nc.scalar.mul(neg_a[:], neg_a[:], -1.0).then_inc(s_pre_act, 1)
            act.wait_ge(s_pre_act, 4)
            for j in range(2):
                act.wait_ge(s_pre_pe, 2 + j)
                nc.scalar.copy(w_cin[:, 2 * j:2 * j + 2, :], halves(("S0", "S1")[j])).then_inc(s_pre_act, 1)

            def modulate(i, n, dst, done):
                l, j = n // 2, 2 * (n % 2)
                act.wait_ge(S[f"h_ps{n}"], at(f"h_ps{n}", i))
                nc.scalar.activation(dst, bank["M"][:, 0:T], ACT.Identity, scale=mod_t[:, l, j + 1, bass.ds(i, 1)],
                                     bias=mod_t[:, l, j, bass.ds(i, 1)]).then_inc(S[done], 1)

            def before_scan(i):
                if isinstance(i, int):
                    act.wait_ge(s_pre_dve, 4)
                    act.wait_ge(s_consts, 8)
                modulate(i, 0, h1[:, PAD:PAD + T], "h1")
                act.wait_ge(S["u_ps"], at("u_ps", i))
                for c in range(ND):
                    last = nc.scalar.activation(uT[:, c, :], halves("O0")[:, c, :], ACT.Identity, bias=cols[:, c:c + 1])
                last.then_inc(S["uT"], 1)
                act.wait_ge(S["z_ps"], at("z_ps", i))
                nc.scalar.activation(thz[:], halves("O1"), ACT.Tanh, scale=0.5).then_inc(S["thz"], 1)
                act.wait_ge(S["bc_ps"], at("bc_ps", i))
                nc.scalar.copy(bc3[:], bank["S1"][0:96, 0:T]).then_inc(S["bc_hi"], 1)
                act.wait_ge(S["dt_ps"], at("dt_ps", i))
                for c in range(ND):
                    last = nc.scalar.activation(thd[:, c, :], halves("S0")[:, c, :], ACT.Tanh, scale=0.5, bias=hdtb[:, c:c + 1])
                last.then_inc(S["thd"], 1)

            def decay(i, p):
                if p == 0:
                    act.wait_ge(S["dt"], at("dt", i, 2))
                if p >= 2:
                    act.wait_ge(S["scan"], at("scan", i, p - 1))
                else:
                    act.wait_ge(S["scan"], at("scan", i, 0))
                for c in range(ND):
                    for m in range(2):
                        n = 2 * p + m
                        last = nc.scalar.activation(dA[p % 2][:, c, m, :], dt[:, c, :], ACT.Exp, scale=neg_a[:, c, n:n + 1])
                last.then_inc(S["dA"], 1)

            def probs(j, h):
                act.wait_ge(S["sc_ps"], at("sc_ps", j, h + 1))
                if h >= 2:
                    act.wait_ge(S["av"], at("av", j, h - 1))
                nc.scalar.activation(pt[h % 2][:], halves(f"S{h % 2}"), ACT.Exp).then_inc(S["pt"], 1)

            def heads_to_T(j, g):
                act.wait_ge(S["ot_ps"], at("ot_ps", j, g + 1))
                nc.scalar.copy(oT[:, 2 * g:2 * g + 2, :], halves("M")).then_inc(S["ot"], 1)

            def mix(j):
                modulate(j, 3, h4[:, 1:1 + T], "h4")
                act.wait_ge(S["rr_ps"], at("rr_ps", j))
                nc.scalar.activation(thr[:].rearrange("p t f -> p (t f)"), bank["S1"][:, 0:T], ACT.Tanh, scale=0.5)\
                    .then_inc(S["thr"], 1)

            def experts(i):
                modulate(i, 1, h2[:], "h2")
                act.wait_ge(S["top"], at("top", i, 3))
                for t in range(NT):
                    last = nc.scalar.activation(el[:, t, :], lg[:, t, :], ACT.Exp, bias=nm[:, t:t + 1])
                last.then_inc(S["el"], 1)
                act.wait_ge(S["wt_ps"], at("wt_ps", i))
                nc.scalar.copy(wT[:], bank["S1"][:, 0:T]).then_inc(S["wT"], 1)

            def qkv(i):
                modulate(i, 2, h3[:], "h3")
                for t in range(NT):
                    for n in range(3):
                        act.wait_ge(S["qkv_ps"], at("qkv_ps", i, 3 * t + n + 1))
                        src = bank[QKV_BANKS[t][n]]
                        w = 512 if n < 2 else KV * DH
                        a = 8 * n
                        nc.scalar.copy(qs[:, t, a:a + w // DH, :], src[:, 0:w].rearrange("p (h f) -> p h f", f=DH))\
                            .then_inc(S["qs"], 1)
                        nc.scalar.activation(sq[:, t, a:a + w // DH, :], src[:, 0:w].rearrange("p (h f) -> p h f", f=DH),
                                             ACT.Square).then_inc(S["sq"], 1)
                    nc.scalar.copy(va[:, t, :, 0:DH], src[:, KV * DH:2 * KV * DH].rearrange("p (h f) -> p h f", f=DH))\
                        .then_inc(S["va"], 1)
                for n in range(6):
                    act.wait_ge(S["qT_ps"], at("qT_ps", i, n + 1))
                    nc.scalar.copy(qT[:, 2 * n:2 * n + 2, :], halves(QT_BANKS[n])).then_inc(S["qT"], 1)
                act.wait_ge(S["mn_ps"], at("mn_ps", i))
                nc.scalar.copy(negm[:], bank["M"][:, 0:T // 2].bitcast(BF16)).then_inc(S["negm"], 1)

            def turn(i, prev, cur):
                if cur:
                    before_scan(i)
                for p in range(8):
                    if cur:
                        decay(i, p)
                    if prev:
                        probs(i - 1, 2 * p)
                        probs(i - 1, 2 * p + 1)
                        if p in (3, 5, 7):
                            heads_to_T(i - 1, (p - 3) // 2)
                if prev:
                    heads_to_T(i - 1, 3)
                    mix(i - 1)
                if cur:
                    experts(i)
                    qkv(i)

            turn(0, False, True)
            with act.Fori(1, B) as i:
                turn(i, True, True)
            turn(B, True, False)

        @block.vector
        def _(dve):
            dve.wait_ge(s_w0, EARLY)
            dve.wait_ge(s_pre_act, 1)
            nc.vector.scalar_tensor_tensor(out=csil[:], in0=cth[:], scalar=1.0, in1=cT[:], op0=ALU.add, op1=ALU.mult)\
                .then_inc(s_pre_dve, 1)
            dve.wait_ge(s_pre_dve, 1)
            nc.vector.tensor_scalar(csil[:], csil[:], 0.5, None, ALU.mult).then_inc(s_pre_dve, 1)
            dve.wait_ge(s_pre_pe, 1)
            mod_ps = bank["M"][:, 0:64].rearrange("p (l j b) -> p l j b", l=2, j=4)
            for l in range(2):
                nc.vector.tensor_copy(mod_t[:, l, 0:4:2, :], mod_ps[:, l, 0:4:2, :])
                nc.vector.tensor_scalar(mod_t[:, l, 1:4:2, :], mod_ps[:, l, 1:4:2, :], 1.0, None, ALU.add)\
                    .then_inc(s_pre_dve, 1)
            gate_ps = bank["B"][0:B, :].rearrange("p (l g f) -> p l g f", l=2, g=2)
            nc.vector.tensor_copy(gate[:], gate_ps).then_inc(s_pre_dve, 1)
            dve.wait_ge(s_pre_dve, 5)
            nc.vector.scalar_tensor_tensor(out=gabs[:], in0=gate[:], scalar=-1.0, in1=gate[:], op0=ALU.mult, op1=ALU.max)\
                .then_inc(s_pre_dve, 1)
            dve.wait_ge(s_pre_dve, 6)
            nc.vector.tensor_scalar(gabs[:], gabs[:], 0.25, None, ALU.max).then_inc(s_pre_dve, 1)
            nc.vector.tensor_scalar(gate[:], gate[:], 0.0, 2.0, ALU.is_ge, ALU.mult).then_inc(s_pre_dve, 1)
            dve.wait_ge(s_pre_dve, 8)
            nc.vector.scalar_tensor_tensor(out=gate[:], in0=gate[:], scalar=-1.0, in1=gabs[:], op0=ALU.add, op1=ALU.mult)\
                .then_inc(s_gate, 1)

            def rsqrt(y, v, a, s, i, k):
                nc.vector.tensor_scalar(y.bitcast(I32), v.bitcast(I32), -0.5, float(RSQRT_SEED), ALU.mult, ALU.add)\
                    .then_inc(S[s], 1)
                for _ in range(NEWTON):
                    dve.wait_ge(S[s], at(s, i, k + 1))
                    nc.vector.tensor_tensor(a, y, y, ALU.mult).then_inc(S[s], 1)
                    dve.wait_ge(S[s], at(s, i, k + 2))
                    nc.vector.scalar_tensor_tensor(out=a, in0=a, scalar=-0.5, in1=v, op0=ALU.mult, op1=ALU.mult)\
                        .then_inc(S[s], 1)
                    dve.wait_ge(S[s], at(s, i, k + 3))
                    nc.vector.scalar_tensor_tensor(out=y, in0=a, scalar=1.5, in1=y, op0=ALU.add, op1=ALU.mult)\
                        .then_inc(S[s], 1)
                    k += 3
                dve.wait_ge(S[s], at(s, i, k + 1))

            def layer_norm(i, n, x):
                ln = f"ln{n}"
                for t in range(NT):
                    last = nc.vector.bn_stats(stats[:, t, :], x[:, t, :])
                last.then_inc(S[ln], 1)
                wait_apart(dve, ln, at(ln, i, 1))
                for t in range(NT):
                    last = nc.vector.bn_aggr(mv[:, t, :], stats[:, t, :])
                last.then_inc(S[ln], 1)
                dve.wait_ge(S[ln], at(ln, i, 2))
                nc.vector.tensor_scalar(lnv[:, 0, :], mv[:, :, 1], LN_EPS, None, ALU.add).then_inc(S[ln], 1)
                dve.wait_ge(S[ln], at(ln, i, 3))
                rsqrt(lnv[:, 1, :], lnv[:, 0, :], lnv[:, 2, :], ln, i, 3)
                for t in range(NT):
                    last = nc.vector.tensor_scalar(xn[n][:, t, :], x[:, t, :], mv[:, t, 0:1], lnv[:, 1, t:t + 1],
                                                   ALU.subtract, ALU.mult)
                last.then_inc(S[f"xn{n}"], 1)

            def residual(i, ps, l, g, x, y, step, done):
                gt = gates[:, bass.ds(i, 1), l, g, :].broadcast_to((P, NT, P))
                nc.vector.tensor_tensor(tmp_g[:], ps, gt, ALU.mult).then_inc(S[step], 1)
                dve.wait_ge(S[step], at(step, i))
                nc.vector.tensor_tensor(y[:], tmp_g[:], x[:], ALU.add).then_inc(S[done], 1)
                dve.wait_ge(S[done], at(done, i))

            def before_scan(i):
                dve.wait_ge(S["x_in"], at("x_in", i))
                layer_norm(i, 0, x0)
                dve.wait_ge(S["bc_hi"], at("bc_hi", i))
                nc.vector.tensor_tensor(bc_r[:], bank["S1"][0:96, 0:T], bc3[:], ALU.subtract).then_inc(S["bc_rest"], 1)
                dve.wait_ge(S["thd"], at("thd", i))
                nc.vector.tensor_scalar(dt[:], thd[:], 0.5, 0.5, ALU.mult, ALU.add).then_inc(S["dt"], 1)
                dve.wait_ge(S["bc_rest"], at("bc_rest", i, 1))
                nc.vector.tensor_copy(bc_m[:], bc_r[:]).then_inc(S["bc_rest"], 1)
                dve.wait_ge(S["dt"], at("dt", i, 1))
                nc.vector.tensor_scalar(dt[:], dt[:], 1e-4, 1.0, ALU.max, ALU.min).then_inc(S["dt"], 1)
                dve.wait_ge(S["bc_rest"], at("bc_rest", i, 2))
                nc.vector.tensor_copy(bc3[32:64, :], bc_m[32:64, :]).then_inc(S["bc_rest"], 1)
                nc.vector.tensor_tensor(bc3[64:96, :], bc_r[64:96, :], bc_m[64:96, :], ALU.subtract).then_inc(S["bc3"], 1)
                dve.wait_ge(S["dt"], at("dt", i, 2))
                dve.wait_ge(S["uT"], at("uT", i))
                nc.vector.tensor_tensor(dtu[:], dt[:], uT[:], ALU.mult).then_inc(S["dt"], 1)
                dve.wait_ge(S["thz"], at("thz", i))
                nc.vector.scalar_tensor_tensor(out=gz[:], in0=thz[:], scalar=1.0, in1=halves("O1"), op0=ALU.add, op1=ALU.mult)\
                    .then_inc(S["gz"], 1)
                dve.wait_ge(S["dt"], at("dt", i, 3))

            def inject(i, p):
                dve.wait_ge(S["bb_ps"], at("bb_ps", i, p + 1))
                nc.vector.tensor_tensor(dB[p % 2], halves("B").unsqueeze(1).broadcast_to((P, ND, 2, T)),
                                        dtu[:].unsqueeze(2).broadcast_to((P, ND, 2, T)), ALU.mult).then_inc(S["db"], 1)

            def scan(i, p):
                dve.wait_ge(S["dA"], at("dA", i, p + 1))
                nc.vector.tensor_scalar(dA[p % 2], dA[p % 2], EXPM5, EXP5, ALU.max, ALU.min).then_inc(S["dac"], 1)
                dve.wait_ge(S["dac"], at("dac", i, p + 1))
                dve.wait_ge(S["dbe"], at("dbe", i, p + 1))
                if p >= 2:
                    dve.wait_ge(S["y_ps"], at("y_ps", i, p - 1))
                for c in range(ND):
                    for m in range(2):
                        last = nc.vector.tensor_tensor_scan(st[p % 2][:, c, m, :], dA[p % 2][:, c, m, :],
                                                            dB[p % 2][:, c, m, :], 0.0, ALU.mult, ALU.add)
                last.then_inc(S["scan"], 1)
                dve.wait_ge(S["scan"], at("scan", i, p + 1))
                dve.wait_ge(S["cb_ps"], at("cb_ps", i, p + 1))
                nc.vector.tensor_tensor(st[p % 2], halves("C").unsqueeze(1).broadcast_to((P, ND, 2, T)), st[p % 2],
                                        ALU.mult).then_inc(S["ys"], 1)

            def weigh(j, n):
                dve.wait_ge(S["av"], at("av", j, 2 * n + 2))
                o = bank[f"O{n % 2}"][:, 0:4 * (DH + 1)].rearrange("p (a f) -> p a f", a=4)
                nc.vector.reciprocal(rinv[:, n % 2, :], o[:, :, DH]).then_inc(S["rinv"], 1)
                dve.wait_ge(S["rinv"], at("rinv", j, n + 1))
                for hh in range(2):
                    last = nc.vector.tensor_tensor(on[:, :, 2 * n + hh, :], o[:, 2 * hh:2 * hh + 2, 0:DH],
                                                   rinv[:, n % 2, 2 * hh:2 * hh + 2].unsqueeze(2).broadcast_to((P, NT, DH)), ALU.mult)
                last.then_inc(S["on"], 1)

            def mix(j):
                dve.wait_ge(S["o1_ps"], at("o1_ps", j))
                residual(j, halves("M", P), 1, 0, x2, x3, "g2", "x3")
                layer_norm(j, 3, x3)
                dve.wait_ge(S["h4"], at("h4", j))
                nc.vector.tensor_tensor(dd[:], h4[:, 1:1 + T], h4[:, 0:T], ALU.subtract).then_inc(S["dd"], 1)
                dve.wait_ge(S["dd"], at("dd", j))
                mu_r, mu_k = cols[:, 3 * ND:3 * ND + 1], cols[:, 3 * ND + 1:3 * ND + 2]
                nc.vector.scalar_tensor_tensor(out=xk[:], in0=dd[:], scalar=mu_k, in1=h4[:, 0:T], op0=ALU.mult, op1=ALU.add)\
                    .then_inc(S["xk"], 1)
                nc.vector.scalar_tensor_tensor(out=xr[:], in0=dd[:], scalar=mu_r, in1=h4[:, 0:T], op0=ALU.mult, op1=ALU.add)\
                    .then_inc(S["xr"], 1)
                dve.wait_ge(S["kk_ps"], at("kk_ps", j))
                nc.vector.tensor_scalar(kr[:], bank["S0"][:, 0:T], 0.0, None, ALU.max).then_inc(S["kr"], 1)
                dve.wait_ge(S["kr"], at("kr", j))
                nc.vector.tensor_tensor(ka[:], kr[:], kr[:], ALU.mult).then_inc(S["ka"], 1)
                dve.wait_ge(S["thr"], at("thr", j))
                dve.wait_ge(S["vv_ps"], at("vv_ps", j))
                nc.vector.scalar_tensor_tensor(out=t4[:], in0=thr[:], scalar=1.0, in1=halves("O0", P), op0=ALU.add, op1=ALU.mult)\
                    .then_inc(S["t4"], 1)
                dve.wait_ge(S["t4"], at("t4", j, 1))
                gt = gates[:, bass.ds(j, 1), 1, 1, :].broadcast_to((P, NT, P))
                nc.vector.scalar_tensor_tensor(out=t4[:], in0=t4[:], scalar=0.5, in1=gt, op0=ALU.mult, op1=ALU.mult)\
                    .then_inc(S["t4"], 1)
                dve.wait_ge(S["t4"], at("t4", j, 2))
                dve.wait_ge(S["out"], at("out", j, 0))
                nc.vector.tensor_tensor(x4[:], t4[:], x3[:], ALU.add).then_inc(S["x4"], 1)

            def after_scan(i):
                dve.wait_ge(S["y_ps"], at("y_ps", i))
                for c in range(ND):
                    last = nc.vector.scalar_tensor_tensor(out=y1[:, c, :], in0=uT[:, c, :], scalar=cols[:, 2 * ND + c:2 * ND + c + 1],
                                                          in1=halves("Y")[:, c, :], op0=ALU.mult, op1=ALU.add)
                last.then_inc(S["y1"], 1)
                dve.wait_ge(S["y1"], at("y1", i))
                nc.vector.scalar_tensor_tensor(out=yT[:], in0=y1[:], scalar=0.5, in1=gz[:], op0=ALU.mult, op1=ALU.mult)\
                    .then_inc(S["yT"], 1)
                dve.wait_ge(S["o0_ps"], at("o0_ps", i))
                if isinstance(i, int):
                    dve.wait_ge(s_gates, 32)
                residual(i, halves("M", P), 0, 0, x0, x1, "g0", "x1")
                layer_norm(i, 1, x1)
                dve.wait_ge(S["lg_ps"], at("lg_ps", i))
                nc.vector.tensor_copy(lg[:], bank["S1"][:, 0:NT * E].rearrange("p (t e) -> p t e", t=NT)).then_inc(S["top"], 1)
                wait_apart(dve, "top", at("top", i, 1))
                for t in range(NT):
                    last = nc.vector.max(m8[:, t, :], lg[:, t, :])
                last.then_inc(S["top"], 1)
                dve.wait_ge(S["top"], at("top", i, 2))
                nc.vector.tensor_scalar(nm[:], m8[:, :, 0], -1.0, None, ALU.mult).then_inc(S["top"], 1)
                dve.wait_ge(S["el"], at("el", i))
                for t in range(NT):
                    last = nc.vector.scalar_tensor_tensor(out=em[:, t, :], in0=lg[:, t, :], scalar=m8[:, t, 1:2], in1=el[:, t, :],
                                                          op0=ALU.is_ge, op1=ALU.mult)
                last.then_inc(S["top"], 1)
                dve.wait_ge(S["top"], at("top", i, 4))
                nc.vector.tensor_reduce(es[:], em[:], AX.X, ALU.add).then_inc(S["top"], 1)
                dve.wait_ge(S["top"], at("top", i, 5))
                nc.vector.reciprocal(er[:], es[:]).then_inc(S["top"], 1)
                dve.wait_ge(S["top"], at("top", i, 6))
                for t in range(NT):
                    last = nc.vector.tensor_scalar(wx[:, t, :, :], em[:, t, :].unsqueeze(2).broadcast_to((P, E, R)),
                                                   er[:, t:t + 1], 2.0, ALU.mult, ALU.mult)
                last.then_inc(S["wx"], 1)
                dve.wait_ge(S["wT"], at("wT", i))
                nc.vector.tensor_tensor(axw[:], bank["S0"][:, 0:T], wT[:], ALU.mult).then_inc(S["axw"], 1)
                dve.wait_ge(S["f0_ps"], at("f0_ps", i))
                residual(i, halves("O0", P), 0, 1, x1, x2, "g1", "x2")
                layer_norm(i, 2, x2)

            def qkv(i):
                for t in range(NT):
                    dve.wait_ge(S["sq"], at("sq", i, 3 * t + 3))
                    nc.vector.tensor_reduce(rv[:, 0, t, :], sq[:, t, :, :], AX.X, ALU.add).then_inc(S["ssq"], 1)
                    nc.vector.tensor_tensor(qc[:, t, :, :], qs[:, t, :, :], rot_c[:, t, :, :], ALU.mult).then_inc(S["rotc"], 1)
                dve.wait_ge(S["ssq"], at("ssq", i))
                v, y, a = rv[:, 1, :, :], rv[:, 2, :, :], rv[:, 3, :, :]
                nc.vector.tensor_scalar(v, rv[:, 0, :, :], 1.0 / DH, RMS_EPS, ALU.mult, ALU.add).then_inc(S["rms"], 1)
                dve.wait_ge(S["rms"], at("rms", i, 1))
                rsqrt(y, v, a, "rms", i, 1)
                for t in range(NT):
                    dve.wait_ge(S["rots"], at("rots", i, t + 1))
                    nc.vector.tensor_tensor(qc[:, t, :, :], qc[:, t, :, :], qn[:, t, :, :], ALU.add).then_inc(S["rsum"], 1)
                for t in range(NT):
                    dve.wait_ge(S["rsum"], at("rsum", i, t + 1))
                    nc.vector.tensor_tensor(qr[:, t, 0:H, :], qc[:, t, 0:H, :], y[:, t, 0:H].unsqueeze(2).broadcast_to((P, H, DH)),
                                            ALU.mult).then_inc(S["qr"], 1)
                    dst = qr[:, t, H:, :].rearrange("p (k c) f -> p c k f", c=2)
                    for c in range(2):
                        last = nc.vector.tensor_tensor(dst[:, c, :, :], qc[:, t, H:HK, :],
                                                       y[:, t, H:HK].unsqueeze(2).broadcast_to((P, KV, DH)), ALU.mult)
                    last.then_inc(S["qr"], 1)
                for n in range(6):
                    dve.wait_ge(S["qT"], at("qT", i, n + 1))
                    nc.vector.tensor_copy(qTb[:, 2 * n:2 * n + 2, :], qT[:, 2 * n:2 * n + 2, :]).then_inc(S["qTb"], 1)
                for n, (hp, q, t) in enumerate(MAX_STEPS):
                    dve.wait_ge(S["ms_ps"], at("ms_ps", i, n + 1))
                    dst = mx[:, t, :].rearrange("p (f c) -> p c f", c=2)[:, hp, 2 * q:2 * q + 2]
                    nc.vector.tensor_reduce(dst, halves(MAX_BANKS[n % 4]), AX.X, ALU.max).then_inc(S["mx"], 1)
                dve.wait_ge(S["mx"], at("mx", i))
                for a in (0, 64):
                    nc.vector.tensor_scalar(mn[:, :, a:a + H], mx[:], -1.0, None, ALU.mult).then_inc(S["mn"], 1)

            def turn(i, prev, cur):
                if cur:
                    before_scan(i)
                    inject(i, 0)
                for p in range(8):
                    if cur:
                        if p < 7:
                            inject(i, p + 1)
                        scan(i, p)
                    if prev and p >= 1:
                        weigh(i - 1, p - 1)
                if prev:
                    weigh(i - 1, 7)
                    mix(i - 1)
                if cur:
                    after_scan(i)
                    qkv(i)

            turn(0, False, True)
            with dve.Fori(1, B) as i:
                turn(i, True, True)
            turn(B, True, False)

        @block.tensor
        def _(pe):
            pe.wait_ge(s_pre_dve, 2)
            pe.wait_ge(s_w0, EARLY)
            mod_ps = bank["M"][:, 0:64].rearrange("p (l j b) -> p l j b", l=2, j=4)
            for l in range(2):
                nc.tensor.matmul(bank["B"][0:B, 256 * l:256 * l + 256], csil[:, l, :],
                                 w_mod[:, l, 2:6:3, :], start=True, stop=True)
                for j, part in enumerate((0, 1, 3, 4)):
                    last = nc.tensor.matmul(mod_ps[:, l, j, :], w_mod[:, l, part, :], csil[:, l, :], start=True, stop=True)
            last.then_inc(s_pre_pe, 1)
            for j in range(2):
                for tap in (2 * j, 2 * j + 1):
                    for c in range(ND):
                        last = nc.tensor.matmul(halves(("S0", "S1")[j])[:, tap % 2, :], w_inx[:, c, :], w_conv[:, c, tap, :],
                                                start=(c == 0), stop=(c == ND - 1))
                last.then_inc(s_pre_pe, 1)
            pe.wait_ge(s_consts, 8)

            def turn_xn(i, n):
                pe.wait_ge(S[f"xn{n}"], at(f"xn{n}", i))
                for t in range(NT):
                    last = nc.tensor.transpose(bank["M"][:, t * P:(t + 1) * P], xn[n][:, t, :], ident[:])
                last.then_inc(S[f"h_ps{n}"], 1)

            def before_scan(i):
                pe.wait_ge(S["negm"], at("negm", i, 0))
                if isinstance(i, int):
                    pe.wait_ge(s_pre_dve, 4)
                    pe.wait_ge(s_pre_act, 6)
                turn_xn(i, 0)
                pe.wait_ge(S["h1"], at("h1", i))
                pe.wait_ge(S["mx"], at("mx", i, 0))
                for c in range(ND):
                    for tap in range(TAPS):
                        last = nc.tensor.matmul(halves("O0")[:, c, :], w_cin[:, tap, c * P:(c + 1) * P], h1[:, tap:tap + T],
                                                start=(tap == 0), stop=(tap == TAPS - 1))
                last.then_inc(S["u_ps"], 1)
                for c in range(ND):
                    last = nc.tensor.matmul(halves("O1")[:, c, :], w_z[:, c * P:(c + 1) * P], h1[:, PAD:PAD + T], start=True, stop=True)
                last.then_inc(S["z_ps"], 1)
                pe.wait_ge(S["uT"], at("uT", i))
                for k in range(ND):
                    last = nc.tensor.matmul(bank["S1"][0:96, 0:T], w_bc[:, k, :], uT[:, k, :], start=(k == 0), stop=(k == ND - 1))
                last.then_inc(S["bc_ps"], 1)
                for c in range(ND):
                    for k in range(ND):
                        last = nc.tensor.matmul(halves("S0")[:, c, :], w_dt[:, k, c * P:(c + 1) * P], uT[:, k, :],
                                                start=(k == 0), stop=(k == ND - 1))
                last.then_inc(S["dt_ps"], 1)

            def spread(i, p):
                if p == 0:
                    pe.wait_ge(S["bc3"], at("bc3", i))
                else:
                    pe.wait_ge(S["db"], at("db", i, p))
                for m in range(2):
                    last = nc.tensor.matmul(halves("B")[:, m, :], sel[:, 2 * p + m, :], bc3[:], start=True, stop=True)
                last.then_inc(S["bb_ps"], 1)
                if p > 0:
                    pe.wait_ge(S["ys"], at("ys", i, p))
                for m in range(2):
                    last = nc.tensor.matmul(halves("C")[:, m, :], sel[:, NS + 2 * p + m, :], bc3[:], start=True, stop=True)
                last.then_inc(S["cb_ps"], 1)

            def sum_states(i, p):
                pe.wait_ge(S["ys"], at("ys", i, p + 1))
                for m in range(2):
                    last = nc.tensor.matmul(halves("Y"), ident[:], st[p % 2][:, :, m, :],
                                            start=(p == 0 and m == 0), stop=(p == 7 and m == 1))
                last.then_inc(S["y_ps"], 1)

            def scores(j, h):
                f, a, g = h // 2, DH * (h % 2), h // REP
                if h >= 2:
                    pe.wait_ge(S["pt"], at("pt", j, h - 1))
                if h == 0:
                    pe.wait_ge(S["negm"], at("negm", j))
                for kt in range(NT):
                    dst = halves(f"S{h % 2}")[:, kt, :]
                    nc.tensor.matmul(dst, qT[a:a + DH, NF + g, kt * P:(kt + 1) * P], qT[a:a + DH, f, :], start=True, stop=False)
                    last = nc.tensor.matmul(dst, onehot[a:a + DH, h, :], negm[a:a + DH, :], start=False, stop=True)
                last.then_inc(S["sc_ps"], 1)

            def weighted(j, h):
                pe.wait_ge(S["pt"], at("pt", j, h + 1))
                if h % 2 == 0 and h >= 4:
                    pe.wait_ge(S["on"], at("on", j, h // 2 - 1))
                for qt in range(NT):
                    c = (DH + 1) * (2 * (h % 2) + qt)
                    for kt in range(NT):
                        last = nc.tensor.matmul(bank[f"O{h // 2 % 2}"][:, c:c + DH + 1], pt[h % 2][:, kt, qt * P:(qt + 1) * P],
                                                va[:, kt, h // REP, :], start=(kt == 0), stop=(kt == NT - 1))
                last.then_inc(S["av"], 1)

            def heads_to_T(j, g):
                pe.wait_ge(S["on"], at("on", j, 2 * g + 2))
                if g > 0:
                    pe.wait_ge(S["ot"], at("ot", j, g))
                for f in range(2):
                    for t in range(NT):
                        src = on[:, t, 4 * g + 2 * f:4 * g + 2 * f + 2, :].rearrange("p h f -> p (h f)")
                        last = nc.tensor.transpose(halves("M")[:, f, t * P:(t + 1) * P], src, ident[:])
                last.then_inc(S["ot_ps"], 1)

            def mix(j):
                pe.wait_ge(S["ot"], at("ot", j))
                for t in range(NT):
                    for f in range(NF):
                        last = nc.tensor.matmul(halves("M", P)[:, t, :], oT[:, f, t * P:(t + 1) * P], w_o[:, f, :],
                                                start=(f == 0), stop=(f == NF - 1))
                last.then_inc(S["o1_ps"], 1)
                turn_xn(j, 3)
                pe.wait_ge(S["xk"], at("xk", j))
                nc.tensor.matmul(bank["S0"][:, 0:T], w_k[:], xk[:], start=True, stop=True).then_inc(S["kk_ps"], 1)
                pe.wait_ge(S["xr"], at("xr", j))
                for t in range(NT):
                    last = nc.tensor.matmul(halves("S1", P)[:, t, :], xr[:, t * P:(t + 1) * P], w_r[:], start=True, stop=True)
                last.then_inc(S["rr_ps"], 1)
                pe.wait_ge(S["ka"], at("ka", j))
                for t in range(NT):
                    last = nc.tensor.matmul(halves("O0", P)[:, t, :], ka[:, t * P:(t + 1) * P], w_v[:], start=True, stop=True)
                last.then_inc(S["vv_ps"], 1)

            def after_scan(i):
                pe.wait_ge(S["yT"], at("yT", i))
                if isinstance(i, int):
                    pe.wait_ge(s_w1, LATE)
                if not isinstance(i, int):
                    pe.wait_ge(S["h4"], at("h4", i, 0))
                for t in range(NT):
                    for k in range(ND):
                        last = nc.tensor.matmul(halves("M", P)[:, t, :], yT[:, k, t * P:(t + 1) * P], w_out[:, k, :],
                                                start=(k == 0), stop=(k == ND - 1))
                last.then_inc(S["o0_ps"], 1)
                turn_xn(i, 1)
                pe.wait_ge(S["h2"], at("h2", i))
                if not isinstance(i, int):
                    pe.wait_ge(S["thr"], at("thr", i, 0))
                    pe.wait_ge(S["t4"], at("t4", i, 0))
                for t in range(NT):
                    dst = bank["S1"][:, t * E:(t + 1) * E]
                    nc.tensor.matmul(dst, h2[:, t * P:(t + 1) * P], w_rt[:], start=True, stop=False)
                    last = nc.tensor.matmul(dst, ones_row[:], rows[:, P:P + E], start=False, stop=True)
                last.then_inc(S["lg_ps"], 1)
                nc.tensor.matmul(bank["S0"][:, 0:T], w_la[:], h2[:], start=True, stop=True).then_inc(S["ax_ps"], 1)
                pe.wait_ge(S["wx"], at("wx", i))
                for t in range(NT):
                    last = nc.tensor.transpose(bank["S1"][:, t * P:(t + 1) * P], wx[:, t, :, :].rearrange("p e r -> p (e r)"), ident[:])
                last.then_inc(S["wt_ps"], 1)
                pe.wait_ge(S["axw"], at("axw", i))
                for t in range(NT):
                    dst = halves("O0", P)[:, t, :]
                    nc.tensor.matmul(dst, h2[:, t * P:(t + 1) * P], w_base[:], start=True, stop=False)
                    nc.tensor.matmul(dst, ones_row[:], rows[:, 0:P], start=False, stop=False)
                    last = nc.tensor.matmul(dst, axw[:, t * P:(t + 1) * P], w_lb[:], start=False, stop=True)
                last.then_inc(S["f0_ps"], 1)

            def qkv(i):
                turn_xn(i, 2)
                pe.wait_ge(S["h3"], at("h3", i))
                pe.wait_ge(S["x2"], at("x2", i))
                for t in range(NT):
                    for n in range(3):
                        nc.tensor.matmul(bank[QKV_BANKS[t][n]][:], h3[:, t * P:(t + 1) * P], w_qkv[:, 512 * n:512 * n + 512],
                                         start=True, stop=True).then_inc(S["qkv_ps"], 1)
                pe.wait_ge(S["qr"], at("qr", i))
                pe.wait_ge(S["va"], at("va", i))
                for n in range(6):
                    for f in range(2):
                        for t in range(NT):
                            src = qr[:, t, 2 * (2 * n + f):2 * (2 * n + f) + 2, :].rearrange("p h f -> p (h f)")
                            last = nc.tensor.transpose(halves(QT_BANKS[n])[:, f, t * P:(t + 1) * P], src, ident[:])
                    last.then_inc(S["qT_ps"], 1)
                pe.wait_ge(S["qTb"], at("qTb", i))
                for n, (hp, q, t) in enumerate(MAX_STEPS):
                    if n >= 4:
                        pe.wait_ge(S["mx"], at("mx", i, n - 3))
                    for m in range(2):
                        f, a = 2 * q + m, DH * hp
                        last = nc.tensor.matmul(halves(MAX_BANKS[n % 4])[:, m, :], qTb[a:a + DH, f, t * P:(t + 1) * P],
                                                qTb[a:a + DH, NF + 2 * f // REP, :], start=True, stop=True)
                    last.then_inc(S["ms_ps"], 1)
                pe.wait_ge(S["mn"], at("mn", i))
                for t in range(NT):
                    last = nc.tensor.transpose(bank["M"][:, t * P // 2:(t + 1) * P // 2].bitcast(BF16), mn[:, t, :], identb[:])
                last.then_inc(S["mn_ps"], 1)

            def turn(i, prev, cur):
                if cur:
                    before_scan(i)
                    spread(i, 0)
                if prev:
                    scores(i - 1, 0)
                for p in range(8):
                    if prev:
                        if cur and p == 1:
                            pe.wait_ge(S["gz"], at("gz", i))
                        scores(i - 1, 2 * p + 1)
                        weighted(i - 1, 2 * p)
                        if p < 7:
                            scores(i - 1, 2 * p + 2)
                        weighted(i - 1, 2 * p + 1)
                    if cur:
                        if p < 7:
                            spread(i, p + 1)
                        sum_states(i, p)
                    if prev and p in (3, 5, 7):
                        heads_to_T(i - 1, (p - 3) // 2)
                if prev:
                    heads_to_T(i - 1, 3)
                    mix(i - 1)
                if cur:
                    after_scan(i)
                    qkv(i)

            turn(0, False, True)
            with pe.Fori(1, B) as i:
                turn(i, True, True)
            turn(B, True, False)


QKV_BANKS = (("B", "C", "S0"), ("S1", "O0", "O1"))
QT_BANKS = ("B", "C", "S0", "S1", "O0", "O1")
MAX_BANKS = ("S0", "S1", "O0", "O1")
MAX_STEPS = [(hp, q, t) for q in range(NF // 2) for t in range(NT) for hp in range(2)]


def kernel(**inputs):
    import numpy as np
    import concourse.bacc as bacc
    from concourse.bass_utils import run_bass_kernel_spmd as run

    a = {k: np.asarray(v) for k, v in inputs.items()}
    m0, m1, f0, f1 = "L0_attn_", "L1_attn_", "L0_ffn_", "L1_ffn_"

    def tiles(w):
        w = w.reshape((w.shape[0] // P, P) + w.shape[1:])
        return np.moveaxis(w, 0, 1)

    in_w = a[m0 + "in_proj_w"]
    bc = np.concatenate([a[m0 + "B_w"], a[m0 + "C_w"]]).T
    mod = np.stack([a["L0_wmod"], a["L1_wmod"]]).reshape(2, P, 6, P)
    pos = np.maximum(np.arange(T, dtype=np.float32) - 1, 0)
    inv_freq = (1.0 / np.float32(10000.0) ** (np.arange(0, DH, 2, dtype=np.float32) / DH)).astype(np.float32)
    angle = np.concatenate([pos[:, None] * inv_freq[None, :]] * 2, axis=1).astype(np.float32)
    sign = np.where(np.arange(DH) < DH // 2, -1.0, 1.0).astype(np.float32)
    cs = np.stack([np.cos(angle), np.sin(angle) * sign], axis=1).astype(np.float32)
    pick = np.zeros((P, 32 + H), np.float32)
    for p in range(P):
        pick[p, p % 32] = 1.0
        if p % 64 < H:
            pick[p, 32 + p % 64] = 1.0
    arrays = {
        "x": a[m0 + "x"],
        "cT": np.stack([a["L0_c"].T, a["L1_c"].T], axis=1),
        "wmod": np.moveaxis(mod, 0, 1),
        "w_inx": tiles(in_w[:DI]),
        "w_conv": tiles(a[m0 + "conv_w"].transpose(1, 2, 0)),
        "w_z": in_w[DI:].T,
        "cols": np.concatenate([tiles(a[m0 + "conv_b"]), tiles(a[m0 + "dt_b"]), tiles(a[m0 + "D"]),
                                a[f1 + "mu_r"][:, None], a[f1 + "mu_k"][:, None]], axis=1),
        "a_log": tiles(a[m0 + "A_log"]),
        "pick": pick,
        "w_dt": tiles(a[m0 + "dt_w"].T),
        "w_bc": tiles(np.concatenate([bc, bc, bc], axis=1)),
        "cs": tiles(cs),
        "w_out": tiles(a[m0 + "out_w"].T),
        "w_base": a[f0 + "base_w"].T,
        "w_la": a[f0 + "lora_A"].transpose(1, 0, 2).reshape(P, E * R),
        "w_lb": a[f0 + "lora_B"].reshape(E * R, P),
        "w_rt": a[f0 + "router_w"].T,
        "rows": np.concatenate([a[f0 + "base_b"], a[f0 + "router_b"]])[None, :],
        "norm_w": np.broadcast_to(np.stack([a[m1 + "q_norm_w"], a[m1 + "k_norm_w"]]), (P, 2, DH)),
        "w_qkv": np.concatenate([a[m1 + "Wq"], a[m1 + "Wk"], a[m1 + "Wv"]]).T,
        "w_o": tiles(a[m1 + "Wo"].T),
        "w_r": a[f1 + "W_r"].T,
        "w_k": a[f1 + "W_k"].T,
        "w_v": a[f1 + "W_v"].T,
    }
    arrays = {k: np.ascontiguousarray(v) for k, v in arrays.items()}
    nc = bacc.Bacc("TRN2", target_bir_lowering=False, num_devices=1)
    d = {k: nc.dram_tensor(f"in_{k}", v.shape, mybir.dt.from_np(v.dtype), kind="ExternalInput").ap()
         for k, v in arrays.items()}
    out = nc.dram_tensor("out", (B, T, P), F32, kind="ExternalOutput").ap()
    build(nc, d, out)
    r = run(nc, [{f"in_{k}": v for k, v in arrays.items()}], core_ids=[0])
    return r.results[0]["out"]
```

```python
from contextlib import ExitStack

import concourse.bass as bass
from concourse import mybir

F32 = mybir.dt.float32
BF16 = mybir.dt.bfloat16
I32 = mybir.dt.int32
ALU = mybir.AluOpType
ACT = mybir.ActivationFunctionType
AX = mybir.AxisListType

P = 128
B, T = 8, 256
NT = T // P
DI = 256
ND = DI // P
NS = 16
TAPS = 4
PAD = TAPS - 1
E, R = 8, 16
H, KV, DH = 16, 4, 64
REP = H // KV
HK = H + KV
NF = H * DH // P
LN_EPS, RMS_EPS, STATE_EPS = 1e-5, 1e-6, 1e-6
EXP5, EXPM5 = 148.4131591025766, 0.006737946999085467
RSQRT_SEED = 0x5F3759DF
NEWTON = 3
LN_STEPS = 2 + 3 * NEWTON

EVENTS = dict(
    x_in=16, x0=1, mom0=2, mom1=2, mom2=2, mom3=2, norms=LN_STEPS, ln2=LN_STEPS, rms=2 + 3 * NEWTON,
    xn0=1, xn1=1, xn2=1, xn3=1, h_ps0=1, h_ps1=1, h_ps2=1, h_ps3=1, h1=1, h2=1, h3=1, h4=1,
    u_ps=1, z_ps=1, uT=1, thz=1, gz=1, dt_ps=1, thd=1, dt=3, bc_ps=1, bc_hi=1, bc_rest=3, bc3=1,
    bb_ps=8, cb_ps=8, dA=8, db=8, dbe=8, dac=8, scan=8, ys=8, y_ps=8, y1=1, yT=1,
    o0_ps=1, g0=1, x1=1, ax_ps=1, lg_ps=1, top=6, el=1, wx=1, wt_ps=1, wT=1, axw=1, f0_ps=1, g1=1, x2=1,
    qkv_ps=6, qs=6, sq=6, va=2, ssq=2, rotc=2, rots=2, rsum=2, qr=4, qT_ps=6, qT=6, qTb=6,
    ms_ps=16, mx=16, mn=2, mn_ps=1, negm=1,
    sc_ps=16, pt=16, av=16, rinv=8, on=8, ot_ps=4, ot=4, o1_ps=1, g2=1, x3=1,
    dd=1, xk=1, xr=1, kk_ps=1, rr_ps=1, kr=1, ka=1, thr=1, vv_ps=1, t4=2, x4=1, out=16,
)


def build(nc, d, out):
    ctx = ExitStack()
    with ctx:
        def sb(name, shape, dt=F32):
            return ctx.enter_context(nc.sbuf_tensor(name, shape, dt))

        def sem(name):
            return ctx.enter_context(nc.semaphore(name))

        w_inx = sb("w_inx", [P, ND, P])
        w_cin = sb("w_cin", [P, TAPS, DI])
        w_z = sb("w_z", [P, DI])
        w_dt = sb("w_dt", [P, ND, DI])
        w_bc = sb("w_bc", [P, ND, 96])
        w_out = sb("w_out", [P, ND, P])
        w_base = sb("w_base", [P, P])
        w_la = sb("w_la", [P, E * R])
        w_lb = sb("w_lb", [E * R, P])
        w_rt = sb("w_rt", [P, E])
        w_qkv = sb("w_qkv", [P, (H + 2 * KV) * DH])
        w_o = sb("w_o", [P, NF, P])
        w_r = sb("w_r", [P, P])
        w_k = sb("w_k", [P, P])
        w_v = sb("w_v", [P, P])
        cT = sb("cT", [P, 2, B])
        cols = sb("cols", [P, 3 * ND + 2])
        a_log = sb("a_log", [P, ND, NS])
        neg_a = sb("neg_a", [P, ND, NS])
        hdtb = sb("hdtb", [P, ND])
        rows = sb("rows", [1, P + E])
        norm_w = sb("norm_w", [P, 2, DH])
        cs = sb("cs", [P, NT, 2, DH])
        rot_c = sb("rot_c", [P, NT, HK, DH])
        rot_s = sb("rot_s", [P, NT, HK, DH])
        ident = sb("ident", [P, P])
        identb = sb("identb", [P, P], BF16)
        sel = sb("sel", [96, 2 * NS, P], BF16)
        onehot = sb("onehot", [P, H, P], BF16)
        pick = sb("pick", [P, 32 + H])
        ones_row = sb("ones_row", [1, P])
        cth = sb("cth", [P, 2, B])
        csil = sb("csil", [P, 2, B])
        mod_t = sb("mod_t", [P, 2, 4, B])
        gate = sb("gate", [B, 2, 2, P])
        gabs = sb("gabs", [B, 2, 2, P])
        gates = sb("gates", [P, B, 2, 2, P])
        gate_dram = nc.dram_tensor("gate_scratch", (B, 2, 2, P), F32, kind="Internal").ap()

        xa = sb("xa", [P, NT, P])
        x0 = sb("x0", [P, NT, P])
        x1 = sb("x1", [P, NT, P])
        x2 = sb("x2", [P, NT, P])
        x3 = sb("x3", [P, NT, P])
        x4 = sb("x4", [P, NT, P])
        tmp_g = sb("tmp_g", [P, NT, P])
        stats = sb("stats", [P, 4, NT, 6])
        mv = sb("mv", [P, 4, NT, 2])
        lnv = sb("lnv", [P, 3, 4, NT])
        xn = [sb(f"xn{n}", [P, NT, P]) for n in range(4)]
        h1 = sb("h1", [P, PAD + T])
        h2 = sb("h2", [P, T])
        h3 = sb("h3", [P, T])
        h4 = sb("h4", [P, 1 + T])
        uT = sb("uT", [P, ND, T])
        thz = sb("thz", [P, ND, T])
        gz = sb("gz", [P, ND, T])
        thd = sb("thd", [P, ND, T])
        dt = sb("dt", [P, ND, T])
        dtu = sb("dtu", [P, ND, T])
        bc3 = sb("bc3", [96, T], BF16)
        bc_r = sb("bc_r", [96, T])
        bc_m = sb("bc_m", [96, T], BF16)
        scan_mem = sb("scan_mem", [P, 6, ND * 2 * T])
        dA, dB, st = ([scan_mem[:, 2 * k + n, :].rearrange("p (c m t) -> p c m t", c=ND, m=2) for n in range(2)]
                      for k in range(3))
        scan_flat = scan_mem[:].rearrange("p k x -> p (k x)")
        qn = scan_flat[:, 0:NT * HK * DH].rearrange("p (t h f) -> p t h f", t=NT, h=HK)
        sq = scan_flat[:, NT * HK * DH:2 * NT * HK * DH].rearrange("p (t h f) -> p t h f", t=NT, h=HK)
        w_conv = scan_flat[:, 0:ND * TAPS * DI].rearrange("p (c j o) -> p c j o", c=ND, j=TAPS)
        w_mod = scan_flat[:, ND * TAPS * DI:ND * TAPS * DI + 12 * P].rearrange("p (l j f) -> p l j f", l=2, j=6)
        y1 = sb("y1", [P, ND, T])
        yT = sb("yT", [P, ND, T])
        lg = sb("lg", [P, NT, E])
        m8 = sb("m8", [P, NT, 8])
        nm = sb("nm", [P, NT])
        el = sb("el", [P, NT, E])
        em = sb("em", [P, NT, E])
        es = sb("es", [P, NT])
        er = sb("er", [P, NT])
        wx = sb("wx", [P, NT, E, R])
        wT = sb("wT", [P, T])
        axw = sb("axw", [P, T])
        qs = sb("qs", [P, NT, HK, DH])
        qc = sb("qc", [P, NT * HK * DH])
        oT = qc[:, 0:NF * T].rearrange("p (f t) -> p f t", f=NF)
        qc = qc[:].rearrange("p (t h f) -> p t h f", t=NT, h=HK)
        rv = sb("rv", [P, 4, NT, HK])
        qr = sb("qr", [P, NT, H + 2 * KV, DH])
        on = qr[:, :, 0:H, :]
        qT = sb("qT", [P, NF + KV, T])
        qTb = sb("qTb", [P, NF + KV, T], BF16)
        va = sb("va", [P, NT, KV, DH + 1])
        mx = sb("mx", [P, NT, H])
        mn = sb("mn", [P, NT, P], BF16)
        negm = sb("negm", [P, T], BF16)
        pt = [sb(f"pt{n}", [P, NT, T]) for n in range(2)]
        rinv = sb("rinv", [P, 2, 4])
        dd = sb("dd", [P, T])
        xk = sb("xk", [P, T])
        xr = sb("xr", [P, T])
        kr = sb("kr", [P, T])
        ka = sb("ka", [P, T])
        thr = sb("thr", [P, NT, P])
        t4 = sb("t4", [P, NT, P])

        bank = {n: ctx.enter_context(nc.psum_tensor(f"ps_{n}", [P, 512], F32))
                for n in ("B", "C", "Y", "S0", "S1", "O0", "O1", "M")}
        S = {name: sem(f"s_{name}") for name in EVENTS}
        s_w0, s_w1, s_w2, s_const, s_consts, s_pick = (sem(n) for n in ("s_w0", "s_w1", "s_w2", "s_const", "s_consts", "s_pick"))
        s_pre_act, s_pre_dve, s_pre_pe, s_gate, s_gates, s_rot = (
            sem(n) for n in ("s_pre_act", "s_pre_dve", "s_pre_pe", "s_gate", "s_gates", "s_rot"))

        s_passed = sem("s_passed")

        def at(name, i, k=None):
            n = EVENTS[name]
            return i * n + (n if k is None else k)

        def wait_apart(eng, name, value):
            eng.wait_ge(S[name], value)
            eng.sem_inc(s_passed, 1)

        def halves(bk, n=256):
            return bank[bk][:, 0:2 * n].rearrange("p (a b) -> p a b", a=2)

        loads_early = [
            (cT[:], d["cT"]), (w_mod, d["wmod"]), (w_inx[:], d["w_inx"]), (w_conv, d["w_conv"]),
            (w_z[:], d["w_z"]), (cols[:], d["cols"]), (a_log[:], d["a_log"]), (pick[:], d["pick"]),
            (w_dt[:], d["w_dt"]), (w_bc[:], d["w_bc"]), (cs[:], d["cs"]),
        ]
        loads_late = [
            (w_out[:], d["w_out"]), (w_base[:], d["w_base"]), (w_la[:], d["w_la"]), (w_lb[:], d["w_lb"]),
            (w_rt[:], d["w_rt"]), (rows[:], d["rows"]), (norm_w[:], d["norm_w"]), (w_qkv[:], d["w_qkv"]),
            (w_o[:], d["w_o"]), (w_r[:], d["w_r"]), (w_k[:], d["w_k"]), (w_v[:], d["w_v"]),
        ]
        EARLY, LATE = 16 * len(loads_early), 16 * len(loads_late)
        x_view = d["x"].rearrange("b (t p) f -> b p t f", p=P)
        out_view = out.rearrange("b (t p) f -> b p t f", p=P)
        block = ctx.enter_context(nc.Block())

        @block.sync
        def _(sp):
            sp.dma_start(xa[:], x_view[0]).then_inc(S["x_in"], 16)
            for dst, src in loads_early:
                sp.dma_start(dst, src).then_inc(s_w0, 16)
            for dst, src in loads_late:
                sp.dma_start(dst, src).then_inc(s_w1, 16)
            sp.wait_ge(s_gate, 1)
            sp.dma_start(gate_dram, gate[:]).then_inc(s_gates, 16)
            sp.wait_ge(s_gates, 16)
            sp.dma_start(gates[:].rearrange("p b l g f -> p (b l g f)"),
                         gate_dram.rearrange("b l g f -> (b l g f)").partition_broadcast(P)).then_inc(s_gates, 16)

            def load(b):
                sp.wait_ge(S["x0"], at("x0", b, 0))
                sp.wait_ge(S["xn0"], at("xn0", b, 0))
                sp.dma_start(xa[:], x_view[b]).then_inc(S["x_in"], 16)

            def store(b):
                sp.wait_ge(S["x4"], at("x4", b))
                sp.dma_start(out_view[b], x4[:]).then_inc(S["out"], 16)

            load(1)
            with sp.Fori(1, B - 1) as i:
                load(i + 1)
                store(i - 1)
            store(B - 2)
            store(B - 1)
            sp.wait_ge(S["out"], 16 * B)

        @block.gpsimd
        def _(pool):
            nc.gpsimd.memset(ident[:], 0.0).then_inc(s_const, 1)
            nc.gpsimd.memset(ones_row[:], 1.0).then_inc(s_consts, 1)
            nc.gpsimd.memset(h1[:, 0:PAD], 0.0).then_inc(s_consts, 1)
            nc.gpsimd.memset(h4[:, 0:1], 0.0).then_inc(s_consts, 1)
            nc.gpsimd.memset(va[:, :, :, DH:DH + 1], 1.0).then_inc(s_consts, 1)
            nc.gpsimd.memset(mn[:], 0.0).then_inc(s_consts, 1)
            pool.wait_ge(s_const, 1)
            nc.gpsimd.affine_select(out=ident[:], in_=ident[:], compare_op=ALU.not_equal, fill=1.0, base=0,
                                    pattern=[[-1, P]], channel_multiplier=1).then_inc(s_const, 1)
            pool.wait_ge(s_const, 2)
            nc.gpsimd.tensor_copy(identb[:], ident[:]).then_inc(s_consts, 1)
            pool.wait_ge(s_w0, EARLY)
            nc.gpsimd.tensor_copy(sel[:], pick[0:96, 0:32].unsqueeze(2).broadcast_to((96, 32, P))).then_inc(s_consts, 1)
            nc.gpsimd.tensor_copy(onehot[:], pick[:, 32:32 + H].unsqueeze(2).broadcast_to((P, H, P))).then_inc(s_consts, 1)
            pool.wait_ge(s_w1, LATE)
            for which, (lo, n) in enumerate(((0, H), (H, KV))):
                for t in range(NT):
                    nc.gpsimd.tensor_tensor(
                        rot_c[:, t, lo:lo + n, :], cs[:, t, 0, :].unsqueeze(1).broadcast_to((P, n, DH)),
                        norm_w[:, which, :].unsqueeze(1).broadcast_to((P, n, DH)), ALU.mult).then_inc(s_rot, 1)
                    for a, b in ((0, DH // 2), (DH // 2, 0)):
                        m = DH // 2
                        nc.gpsimd.tensor_tensor(
                            rot_s[:, t, lo:lo + n, a:a + m], cs[:, t, 1, a:a + m].unsqueeze(1).broadcast_to((P, n, m)),
                            norm_w[:, which, b:b + m].unsqueeze(1).broadcast_to((P, n, m)), ALU.mult).then_inc(s_rot, 1)

            def pairs(i):
                for p in range(8):
                    wait_apart(pool, "db", at("db", i, p + 1))
                    nc.gpsimd.tensor_scalar(dB[p % 2], dB[p % 2], 1.0, STATE_EPS, ALU.mult, ALU.add)\
                        .then_inc(S["dbe"], 1)

            def rotate(i):
                for t in range(NT):
                    pool.wait_ge(S["qs"], at("qs", i, 3 * t + 3))
                    if t == 0:
                        pool.wait_ge(s_rot, 12)
                    m = DH // 2
                    pool.wait_ge(S["rsum"], at("rsum", i, 0))
                    nc.gpsimd.tensor_tensor(qn[:, t, :, 0:m], qs[:, t, :, m:DH], rot_s[:, t, :, 0:m], ALU.mult)
                    nc.gpsimd.tensor_tensor(qn[:, t, :, m:DH], qs[:, t, :, 0:m], rot_s[:, t, :, m:DH], ALU.mult)\
                        .then_inc(S["rots"], 1)

            def keep(b):
                pool.wait_ge(S["x_in"], at("x_in", b))
                wait_apart(pool, "x1", at("x1", b, 0))
                nc.gpsimd.tensor_copy(x0[:], xa[:]).then_inc(S["x0"], 1)

            keep(0)
            pairs(0)
            keep(1)
            rotate(0)
            with pool.Fori(1, B - 1) as i:
                pairs(i)
                keep(i + 1)
                rotate(i)
            pairs(B - 1)
            rotate(B - 1)

        @block.scalar
        def _(act):
            act.wait_ge(s_w0, EARLY)
            nc.scalar.activation(cth[:], cT[:], ACT.Tanh, scale=0.5).then_inc(s_pre_act, 1)
            nc.scalar.activation(neg_a[:], a_log[:], ACT.Exp).then_inc(s_pre_act, 1)
            nc.scalar.mul(hdtb[:], cols[:, ND:2 * ND], 0.5).then_inc(s_pre_act, 1)
            act.wait_ge(s_pre_act, 2)
            nc.scalar.mul(neg_a[:], neg_a[:], -1.0).then_inc(s_pre_act, 1)
            act.wait_ge(s_pre_act, 4)
            for j in range(2):
                act.wait_ge(s_pre_pe, 2 + j)
                nc.scalar.copy(w_cin[:, 2 * j:2 * j + 2, :], halves(("S0", "S1")[j])).then_inc(s_pre_act, 1)

            def modulate(i, n, ps, dst, done):
                l, j = n // 2, 2 * (n % 2)
                act.wait_ge(S[f"h_ps{n}"], at(f"h_ps{n}", i))
                nc.scalar.activation(dst, bank[ps][:, 0:T], ACT.Identity, scale=mod_t[:, l, j + 1, bass.ds(i, 1)],
                                     bias=mod_t[:, l, j, bass.ds(i, 1)]).then_inc(S[done], 1)

            def conv_out(b):
                act.wait_ge(S["y1"], at("y1", b, 0))
                act.wait_ge(S["u_ps"], at("u_ps", b))
                for c in range(ND):
                    last = nc.scalar.activation(uT[:, c, :], halves("O1")[:, c, :], ACT.Identity, bias=cols[:, c:c + 1])
                last.then_inc(S["uT"], 1)

            def gate_of_y(b):
                act.wait_ge(S["z_ps"], at("z_ps", b))
                nc.scalar.activation(thz[:], halves("O0"), ACT.Tanh, scale=0.5).then_inc(S["thz"], 1)

            def b_and_c(b):
                act.wait_ge(S["bc_ps"], at("bc_ps", b))
                nc.scalar.copy(bc3[:], bank["O1"][0:96, 0:T]).then_inc(S["bc_hi"], 1)

            def step_size(b):
                act.wait_ge(S["dt_ps"], at("dt_ps", b))
                for c in range(ND):
                    last = nc.scalar.activation(thd[:, c, :], halves("Y")[:, c, :], ACT.Tanh, scale=0.5, bias=hdtb[:, c:c + 1])
                last.then_inc(S["thd"], 1)

            def decay(i, p, c):
                if p == 0 and c == 0:
                    act.wait_ge(S["dt"], at("dt", i, 2))
                    act.wait_ge(S["ssq"], at("ssq", i, 0))
                    act.wait_ge(S["rsum"], at("rsum", i, 0))
                if p >= 2 and c == 0:
                    act.wait_ge(S["scan"], at("scan", i, p - 1))
                for m in range(2):
                    n = 2 * p + m
                    last = nc.scalar.activation(dA[p % 2][:, c, m, :], dt[:, c, :], ACT.Exp, scale=neg_a[:, c, n:n + 1])
                if c == ND - 1:
                    last.then_inc(S["dA"], 1)

            def probs(j, h):
                act.wait_ge(S["sc_ps"], at("sc_ps", j, h + 1))
                if h >= 2:
                    act.wait_ge(S["av"], at("av", j, h - 1))
                nc.scalar.activation(pt[h % 2][:], halves(f"S{h % 2}"), ACT.Exp).then_inc(S["pt"], 1)

            def heads_to_T(j, g):
                act.wait_ge(S["ot_ps"], at("ot_ps", j, g + 1))
                nc.scalar.copy(oT[:, 2 * g:2 * g + 2, :], halves("M")).then_inc(S["ot"], 1)

            def receptance(j):
                act.wait_ge(S["rr_ps"], at("rr_ps", j))
                nc.scalar.activation(thr[:].rearrange("p t f -> p (t f)"), bank["S1"][:, 0:T], ACT.Tanh, scale=0.5)\
                    .then_inc(S["thr"], 1)

            def router_exp(i):
                act.wait_ge(S["top"], at("top", i, 3))
                for t in range(NT):
                    last = nc.scalar.activation(el[:, t, :], lg[:, t, :], ACT.Exp, bias=nm[:, t:t + 1])
                last.then_inc(S["el"], 1)

            def expert_weights(i):
                act.wait_ge(S["wt_ps"], at("wt_ps", i))
                nc.scalar.copy(wT[:], bank["C"][:, 0:T]).then_inc(S["wT"], 1)

            def qkv(i):
                modulate(i, 2, "B", h3[:], "h3")
                for t in range(NT):
                    for n in range(3):
                        act.wait_ge(S["qkv_ps"], at("qkv_ps", i, 3 * t + n + 1))
                        src = bank[QKV_BANKS[t][n]]
                        w = 512 if n < 2 else KV * DH
                        a = 8 * n
                        nc.scalar.copy(qs[:, t, a:a + w // DH, :], src[:, 0:w].rearrange("p (h f) -> p h f", f=DH))\
                            .then_inc(S["qs"], 1)
                        nc.scalar.activation(sq[:, t, a:a + w // DH, :], src[:, 0:w].rearrange("p (h f) -> p h f", f=DH),
                                             ACT.Square).then_inc(S["sq"], 1)
                    nc.scalar.copy(va[:, t, :, 0:DH], src[:, KV * DH:2 * KV * DH].rearrange("p (h f) -> p h f", f=DH))\
                        .then_inc(S["va"], 1)
                for n in range(6):
                    act.wait_ge(S["qT_ps"], at("qT_ps", i, n + 1))
                    nc.scalar.copy(qT[:, 2 * n:2 * n + 2, :], halves(QT_BANKS[n])).then_inc(S["qT"], 1)
                act.wait_ge(S["mn_ps"], at("mn_ps", i))
                nc.scalar.copy(negm[:], bank["M"][:, 0:T // 2].bitcast(BF16)).then_inc(S["negm"], 1)

            def turn(i, prev, cur, nxt):
                if cur:
                    decay(i, 0, 0)
                    decay(i, 0, 1)
                for p in range(8):
                    if prev:
                        probs(i - 1, 2 * p)
                    if cur and p < 7:
                        decay(i, p + 1, 0)
                    if prev:
                        probs(i - 1, 2 * p + 1)
                    if cur and p < 7:
                        decay(i, p + 1, 1)
                    if prev and p in (3, 5, 7):
                        heads_to_T(i - 1, (p - 3) // 2)
                if prev:
                    heads_to_T(i - 1, 3)
                if cur:
                    modulate(i, 1, "B", h2[:], "h2")
                if prev:
                    modulate(i - 1, 3, "M", h4[:, 1:1 + T], "h4")
                if nxt:
                    modulate(i + 1, 0, "O0", h1[:, PAD:PAD + T], "h1")
                if cur:
                    router_exp(i)
                if prev:
                    receptance(i - 1)
                if nxt:
                    conv_out(i + 1)
                if cur:
                    expert_weights(i)
                if nxt:
                    gate_of_y(i + 1)
                    b_and_c(i + 1)
                    step_size(i + 1)
                if cur:
                    qkv(i)

            act.wait_ge(s_pre_dve, 4)
            act.wait_ge(s_consts, 8)
            turn(-1, False, False, True)
            turn(0, False, True, True)
            with act.Fori(1, B - 1) as i:
                turn(i, True, True, True)
            turn(B - 1, True, True, False)
            turn(B, True, False, False)

        @block.vector
        def _(dve):
            dve.wait_ge(s_w0, EARLY)
            dve.wait_ge(s_pre_act, 1)
            nc.vector.scalar_tensor_tensor(out=csil[:], in0=cth[:], scalar=1.0, in1=cT[:], op0=ALU.add, op1=ALU.mult)\
                .then_inc(s_pre_dve, 1)
            dve.wait_ge(s_pre_dve, 1)
            nc.vector.tensor_scalar(csil[:], csil[:], 0.5, None, ALU.mult).then_inc(s_pre_dve, 1)
            dve.wait_ge(s_pre_pe, 1)
            mod_ps = bank["M"][:, 0:64].rearrange("p (l j b) -> p l j b", l=2, j=4)
            for l in range(2):
                nc.vector.tensor_copy(mod_t[:, l, 0:4:2, :], mod_ps[:, l, 0:4:2, :])
                nc.vector.tensor_scalar(mod_t[:, l, 1:4:2, :], mod_ps[:, l, 1:4:2, :], 1.0, None, ALU.add)\
                    .then_inc(s_pre_dve, 1)
            gate_ps = bank["B"][0:B, :].rearrange("p (l g f) -> p l g f", l=2, g=2)
            nc.vector.tensor_copy(gate[:], gate_ps).then_inc(s_pre_dve, 1)
            dve.wait_ge(s_pre_dve, 5)
            nc.vector.scalar_tensor_tensor(out=gabs[:], in0=gate[:], scalar=-1.0, in1=gate[:], op0=ALU.mult, op1=ALU.max)\
                .then_inc(s_pre_dve, 1)
            dve.wait_ge(s_pre_dve, 6)
            nc.vector.tensor_scalar(gabs[:], gabs[:], 0.25, None, ALU.max).then_inc(s_pre_dve, 1)
            nc.vector.tensor_scalar(gate[:], gate[:], 0.0, 2.0, ALU.is_ge, ALU.mult).then_inc(s_pre_dve, 1)
            dve.wait_ge(s_pre_dve, 8)
            nc.vector.scalar_tensor_tensor(out=gate[:], in0=gate[:], scalar=-1.0, in1=gabs[:], op0=ALU.add, op1=ALU.mult)\
                .then_inc(s_gate, 1)

            def rsqrt(y, v, a, s, i, k):
                nc.vector.tensor_scalar(y.bitcast(I32), v.bitcast(I32), -0.5, float(RSQRT_SEED), ALU.mult, ALU.add)\
                    .then_inc(S[s], 1)
                for _ in range(NEWTON):
                    dve.wait_ge(S[s], at(s, i, k + 1))
                    nc.vector.tensor_tensor(a, y, y, ALU.mult).then_inc(S[s], 1)
                    dve.wait_ge(S[s], at(s, i, k + 2))
                    nc.vector.scalar_tensor_tensor(out=a, in0=a, scalar=-0.5, in1=v, op0=ALU.mult, op1=ALU.mult)\
                        .then_inc(S[s], 1)
                    dve.wait_ge(S[s], at(s, i, k + 3))
                    nc.vector.scalar_tensor_tensor(out=y, in0=a, scalar=1.5, in1=y, op0=ALU.add, op1=ALU.mult)\
                        .then_inc(S[s], 1)
                    k += 3
                dve.wait_ge(S[s], at(s, i, k + 1))

            def moments(b, slot, x):
                mom = f"mom{slot}"
                for t in range(NT):
                    last = nc.vector.bn_stats(stats[:, slot, t, :], x[:, t, :])
                last.then_inc(S[mom], 1)
                wait_apart(dve, mom, at(mom, b, 1))
                for t in range(NT):
                    last = nc.vector.bn_aggr(mv[:, slot, t, :], stats[:, slot, t, :])
                last.then_inc(S[mom], 1)
                dve.wait_ge(S[mom], at(mom, b, 2))

            def deviations(lo, hi, s, i):
                v, y, a = (lnv[:, k, lo:hi, :] for k in range(3))
                nc.vector.tensor_scalar(v, mv[:, lo:hi, :, 1], LN_EPS, None, ALU.add).then_inc(S[s], 1)
                dve.wait_ge(S[s], at(s, i, 1))
                rsqrt(y, v, a, s, i, 1)

            def normed(b, n, slot, x):
                for t in range(NT):
                    last = nc.vector.tensor_scalar(xn[n][:, t, :], x[:, t, :], mv[:, slot, t, 0:1], lnv[:, 1, slot, t:t + 1],
                                                   ALU.subtract, ALU.mult)
                last.then_inc(S[f"xn{n}"], 1)

            def residual(i, ps, l, g, x, y, step, done):
                gt = gates[:, bass.ds(i, 1), l, g, :].broadcast_to((P, NT, P))
                nc.vector.tensor_tensor(tmp_g[:], ps, gt, ALU.mult).then_inc(S[step], 1)
                dve.wait_ge(S[step], at(step, i))
                nc.vector.tensor_tensor(y[:], tmp_g[:], x[:], ALU.add).then_inc(S[done], 1)
                dve.wait_ge(S[done], at(done, i))

            def split_bc(b):
                dve.wait_ge(S["bc_hi"], at("bc_hi", b))
                nc.vector.tensor_tensor(bc_r[:], bank["O1"][0:96, 0:T], bc3[:], ALU.subtract).then_inc(S["bc_rest"], 1)
                dve.wait_ge(S["bc_rest"], at("bc_rest", b, 1))
                nc.vector.tensor_copy(bc_m[:], bc_r[:]).then_inc(S["bc_rest"], 1)
                dve.wait_ge(S["bc_rest"], at("bc_rest", b, 2))
                nc.vector.tensor_copy(bc3[32:64, :], bc_m[32:64, :]).then_inc(S["bc_rest"], 1)
                nc.vector.tensor_tensor(bc3[64:96, :], bc_r[64:96, :], bc_m[64:96, :], ALU.subtract).then_inc(S["bc3"], 1)

            def gate_of_y(b):
                dve.wait_ge(S["thz"], at("thz", b))
                nc.vector.scalar_tensor_tensor(out=gz[:], in0=thz[:], scalar=1.0, in1=halves("O0"), op0=ALU.add, op1=ALU.mult)\
                    .then_inc(S["gz"], 1)

            def step_size(b):
                dve.wait_ge(S["thd"], at("thd", b))
                nc.vector.tensor_scalar(dt[:], thd[:], 0.5, 0.5, ALU.mult, ALU.add).then_inc(S["dt"], 1)
                dve.wait_ge(S["dt"], at("dt", b, 1))
                nc.vector.tensor_scalar(dt[:], dt[:], 1e-4, 1.0, ALU.max, ALU.min).then_inc(S["dt"], 1)
                dve.wait_ge(S["dt"], at("dt", b, 2))
                dve.wait_ge(S["uT"], at("uT", b))
                nc.vector.tensor_tensor(dtu[:], dt[:], uT[:], ALU.mult).then_inc(S["dt"], 1)
                dve.wait_ge(S["dt"], at("dt", b, 3))

            def inject(i, p):
                dve.wait_ge(S["bb_ps"], at("bb_ps", i, p + 1))
                nc.vector.tensor_tensor(dB[p % 2], halves("B").unsqueeze(1).broadcast_to((P, ND, 2, T)),
                                        dtu[:].unsqueeze(2).broadcast_to((P, ND, 2, T)), ALU.mult).then_inc(S["db"], 1)

            def scan(i, p):
                dve.wait_ge(S["dA"], at("dA", i, p + 1))
                nc.vector.tensor_scalar(dA[p % 2], dA[p % 2], EXPM5, EXP5, ALU.max, ALU.min).then_inc(S["dac"], 1)
                dve.wait_ge(S["dac"], at("dac", i, p + 1))
                dve.wait_ge(S["dbe"], at("dbe", i, p + 1))
                if p >= 2:
                    dve.wait_ge(S["y_ps"], at("y_ps", i, p - 1))
                for c in range(ND):
                    for m in range(2):
                        last = nc.vector.tensor_tensor_scan(st[p % 2][:, c, m, :], dA[p % 2][:, c, m, :],
                                                            dB[p % 2][:, c, m, :], 0.0, ALU.mult, ALU.add)
                last.then_inc(S["scan"], 1)
                dve.wait_ge(S["scan"], at("scan", i, p + 1))
                dve.wait_ge(S["cb_ps"], at("cb_ps", i, p + 1))
                nc.vector.tensor_tensor(st[p % 2], halves("C").unsqueeze(1).broadcast_to((P, ND, 2, T)), st[p % 2],
                                        ALU.mult).then_inc(S["ys"], 1)

            def weigh(j, n):
                dve.wait_ge(S["av"], at("av", j, 2 * n + 2))
                o = bank[f"O{n % 2}"][:, 0:4 * (DH + 1)].rearrange("p (a f) -> p a f", a=4)
                nc.vector.reciprocal(rinv[:, n % 2, :], o[:, :, DH]).then_inc(S["rinv"], 1)
                dve.wait_ge(S["rinv"], at("rinv", j, n + 1))
                for hh in range(2):
                    last = nc.vector.tensor_tensor(on[:, :, 2 * n + hh, :], o[:, 2 * hh:2 * hh + 2, 0:DH],
                                                   rinv[:, n % 2, 2 * hh:2 * hh + 2].unsqueeze(2).broadcast_to((P, NT, DH)), ALU.mult)
                last.then_inc(S["on"], 1)

            def shift_mix(j):
                dve.wait_ge(S["h4"], at("h4", j))
                nc.vector.tensor_tensor(dd[:], h4[:, 1:1 + T], h4[:, 0:T], ALU.subtract).then_inc(S["dd"], 1)
                dve.wait_ge(S["dd"], at("dd", j))
                mu_r, mu_k = cols[:, 3 * ND:3 * ND + 1], cols[:, 3 * ND + 1:3 * ND + 2]
                nc.vector.scalar_tensor_tensor(out=xk[:], in0=dd[:], scalar=mu_k, in1=h4[:, 0:T], op0=ALU.mult, op1=ALU.add)\
                    .then_inc(S["xk"], 1)
                nc.vector.scalar_tensor_tensor(out=xr[:], in0=dd[:], scalar=mu_r, in1=h4[:, 0:T], op0=ALU.mult, op1=ALU.add)\
                    .then_inc(S["xr"], 1)

            def relu_squared(j):
                dve.wait_ge(S["kk_ps"], at("kk_ps", j))
                nc.vector.tensor_scalar(kr[:], bank["S0"][:, 0:T], 0.0, None, ALU.max).then_inc(S["kr"], 1)
                dve.wait_ge(S["kr"], at("kr", j))
                nc.vector.tensor_tensor(ka[:], kr[:], kr[:], ALU.mult).then_inc(S["ka"], 1)

            def finish(j):
                dve.wait_ge(S["thr"], at("thr", j))
                dve.wait_ge(S["vv_ps"], at("vv_ps", j))
                nc.vector.scalar_tensor_tensor(out=t4[:], in0=thr[:], scalar=1.0, in1=halves("S0", P), op0=ALU.add, op1=ALU.mult)\
                    .then_inc(S["t4"], 1)
                dve.wait_ge(S["t4"], at("t4", j, 1))
                gt = gates[:, bass.ds(j, 1), 1, 1, :].broadcast_to((P, NT, P))
                nc.vector.scalar_tensor_tensor(out=t4[:], in0=t4[:], scalar=0.5, in1=gt, op0=ALU.mult, op1=ALU.mult)\
                    .then_inc(S["t4"], 1)
                dve.wait_ge(S["t4"], at("t4", j, 2))
                dve.wait_ge(S["out"], at("out", j, 0))
                nc.vector.tensor_tensor(x4[:], t4[:], x3[:], ALU.add).then_inc(S["x4"], 1)

            def scan_out(i):
                dve.wait_ge(S["y_ps"], at("y_ps", i))
                for c in range(ND):
                    last = nc.vector.scalar_tensor_tensor(out=y1[:, c, :], in0=uT[:, c, :], scalar=cols[:, 2 * ND + c:2 * ND + c + 1],
                                                          in1=halves("Y")[:, c, :], op0=ALU.mult, op1=ALU.add)
                last.then_inc(S["y1"], 1)
                dve.wait_ge(S["y1"], at("y1", i))
                nc.vector.scalar_tensor_tensor(out=yT[:], in0=y1[:], scalar=0.5, in1=gz[:], op0=ALU.mult, op1=ALU.mult)\
                    .then_inc(S["yT"], 1)

            def router_top(i):
                dve.wait_ge(S["lg_ps"], at("lg_ps", i))
                nc.vector.tensor_copy(lg[:], bank["C"][:, 0:NT * E].rearrange("p (t e) -> p t e", t=NT)).then_inc(S["top"], 1)
                wait_apart(dve, "top", at("top", i, 1))
                for t in range(NT):
                    last = nc.vector.max(m8[:, t, :], lg[:, t, :])
                last.then_inc(S["top"], 1)
                dve.wait_ge(S["top"], at("top", i, 2))
                nc.vector.tensor_scalar(nm[:], m8[:, :, 0], -1.0, None, ALU.mult).then_inc(S["top"], 1)

            def router_weights(i):
                dve.wait_ge(S["el"], at("el", i))
                for t in range(NT):
                    last = nc.vector.scalar_tensor_tensor(out=em[:, t, :], in0=lg[:, t, :], scalar=m8[:, t, 1:2], in1=el[:, t, :],
                                                          op0=ALU.is_ge, op1=ALU.mult)
                last.then_inc(S["top"], 1)
                dve.wait_ge(S["top"], at("top", i, 4))
                nc.vector.tensor_reduce(es[:], em[:], AX.X, ALU.add).then_inc(S["top"], 1)
                dve.wait_ge(S["top"], at("top", i, 5))
                nc.vector.reciprocal(er[:], es[:]).then_inc(S["top"], 1)
                dve.wait_ge(S["top"], at("top", i, 6))
                for t in range(NT):
                    last = nc.vector.tensor_scalar(wx[:, t, :, :], em[:, t, :].unsqueeze(2).broadcast_to((P, E, R)),
                                                   er[:, t:t + 1], 2.0, ALU.mult, ALU.mult)
                last.then_inc(S["wx"], 1)

            def expert_weights(i):
                dve.wait_ge(S["wT"], at("wT", i))
                dve.wait_ge(S["ax_ps"], at("ax_ps", i))
                nc.vector.tensor_tensor(axw[:], bank["B"][:, 0:T], wT[:], ALU.mult).then_inc(S["axw"], 1)

            def qkv(i):
                for t in range(NT):
                    dve.wait_ge(S["sq"], at("sq", i, 3 * t + 3))
                    nc.vector.tensor_reduce(rv[:, 0, t, :], sq[:, t, :, :], AX.X, ALU.add).then_inc(S["ssq"], 1)
                    nc.vector.tensor_tensor(qc[:, t, :, :], qs[:, t, :, :], rot_c[:, t, :, :], ALU.mult).then_inc(S["rotc"], 1)
                dve.wait_ge(S["ssq"], at("ssq", i))
                v, y, a = rv[:, 1, :, :], rv[:, 2, :, :], rv[:, 3, :, :]
                nc.vector.tensor_scalar(v, rv[:, 0, :, :], 1.0 / DH, RMS_EPS, ALU.mult, ALU.add).then_inc(S["rms"], 1)
                dve.wait_ge(S["rms"], at("rms", i, 1))
                rsqrt(y, v, a, "rms", i, 1)
                for t in range(NT):
                    dve.wait_ge(S["rots"], at("rots", i, t + 1))
                    nc.vector.tensor_tensor(qc[:, t, :, :], qc[:, t, :, :], qn[:, t, :, :], ALU.add).then_inc(S["rsum"], 1)
                for t in range(NT):
                    dve.wait_ge(S["rsum"], at("rsum", i, t + 1))
                    nc.vector.tensor_tensor(qr[:, t, 0:H, :], qc[:, t, 0:H, :], y[:, t, 0:H].unsqueeze(2).broadcast_to((P, H, DH)),
                                            ALU.mult).then_inc(S["qr"], 1)
                    dst = qr[:, t, H:, :].rearrange("p (k c) f -> p c k f", c=2)
                    for c in range(2):
                        last = nc.vector.tensor_tensor(dst[:, c, :, :], qc[:, t, H:HK, :],
                                                       y[:, t, H:HK].unsqueeze(2).broadcast_to((P, KV, DH)), ALU.mult)
                    last.then_inc(S["qr"], 1)
                for n in range(6):
                    dve.wait_ge(S["qT"], at("qT", i, n + 1))
                    nc.vector.tensor_copy(qTb[:, 2 * n:2 * n + 2, :], qT[:, 2 * n:2 * n + 2, :]).then_inc(S["qTb"], 1)
                for n, (hp, q, t) in enumerate(MAX_STEPS):
                    dve.wait_ge(S["ms_ps"], at("ms_ps", i, n + 1))
                    dst = mx[:, t, :].rearrange("p (f c) -> p c f", c=2)[:, hp, 2 * q:2 * q + 2]
                    nc.vector.tensor_reduce(dst, halves(MAX_BANKS[n % 4]), AX.X, ALU.max).then_inc(S["mx"], 1)
                dve.wait_ge(S["mx"], at("mx", i))
                for a in (0, 64):
                    nc.vector.tensor_scalar(mn[:, :, a:a + H], mx[:], -1.0, None, ALU.mult).then_inc(S["mn"], 1)

            def turn(i, prev, cur, nxt):
                if cur:
                    inject(i, 0)
                for p in range(8):
                    if cur:
                        if p < 7:
                            inject(i, p + 1)
                        scan(i, p)
                    if prev and p >= 1:
                        weigh(i - 1, p - 1)
                if prev:
                    weigh(i - 1, 7)
                if cur:
                    scan_out(i)
                if nxt:
                    dve.wait_ge(S["x_in"], at("x_in", i + 1))
                    moments(i + 1, 0, xa)
                if cur:
                    dve.wait_ge(S["o0_ps"], at("o0_ps", i))
                    dve.wait_ge(S["x0"], at("x0", i))
                    residual(i, halves("B", P), 0, 0, x0, x1, "g0", "x1")
                    moments(i, 1, x1)
                if prev:
                    dve.wait_ge(S["o1_ps"], at("o1_ps", i - 1))
                    residual(i - 1, halves("M", P), 1, 0, x2, x3, "g2", "x3")
                    moments(i - 1, 2, x3)
                deviations(0 if nxt else 1 if cur else 2, 3 if prev else 2 if cur else 1, "norms", i + 1)
                if cur:
                    normed(i, 1, 1, x1)
                if prev:
                    normed(i - 1, 3, 2, x3)
                if nxt:
                    normed(i + 1, 0, 0, xa)
                if cur:
                    router_top(i)
                if prev:
                    shift_mix(i - 1)
                if cur:
                    router_weights(i)
                if prev:
                    relu_squared(i - 1)
                if cur:
                    expert_weights(i)
                if nxt:
                    gate_of_y(i + 1)
                if prev:
                    finish(i - 1)
                if cur:
                    dve.wait_ge(S["f0_ps"], at("f0_ps", i))
                    residual(i, halves("C", P), 0, 1, x1, x2, "g1", "x2")
                    moments(i, 3, x2)
                    deviations(3, 4, "ln2", i)
                    normed(i, 2, 3, x2)
                if nxt:
                    split_bc(i + 1)
                    step_size(i + 1)
                if cur:
                    qkv(i)

            turn(-1, False, False, True)
            dve.wait_ge(s_gates, 32)
            turn(0, False, True, True)
            with dve.Fori(1, B - 1) as i:
                turn(i, True, True, True)
            turn(B - 1, True, True, False)
            turn(B, True, False, False)

        @block.tensor
        def _(pe):
            pe.wait_ge(s_pre_dve, 2)
            pe.wait_ge(s_w0, EARLY)
            mod_ps = bank["M"][:, 0:64].rearrange("p (l j b) -> p l j b", l=2, j=4)
            for l in range(2):
                nc.tensor.matmul(bank["B"][0:B, 256 * l:256 * l + 256], csil[:, l, :],
                                 w_mod[:, l, 2:6:3, :], start=True, stop=True)
                for j, part in enumerate((0, 1, 3, 4)):
                    last = nc.tensor.matmul(mod_ps[:, l, j, :], w_mod[:, l, part, :], csil[:, l, :], start=True, stop=True)
            last.then_inc(s_pre_pe, 1)
            for j in range(2):
                for tap in (2 * j, 2 * j + 1):
                    for c in range(ND):
                        last = nc.tensor.matmul(halves(("S0", "S1")[j])[:, tap % 2, :], w_inx[:, c, :], w_conv[:, c, tap, :],
                                                start=(c == 0), stop=(c == ND - 1))
                last.then_inc(s_pre_pe, 1)
            pe.wait_ge(s_consts, 8)

            def turn_xn(i, n, ps):
                pe.wait_ge(S[f"xn{n}"], at(f"xn{n}", i))
                for t in range(NT):
                    last = nc.tensor.transpose(bank[ps][:, t * P:(t + 1) * P], xn[n][:, t, :], ident[:])
                last.then_inc(S[f"h_ps{n}"], 1)

            def conv(b):
                pe.wait_ge(S["h1"], at("h1", b))
                for c in range(ND):
                    for tap in range(TAPS):
                        last = nc.tensor.matmul(halves("O1")[:, c, :], w_cin[:, tap, c * P:(c + 1) * P], h1[:, tap:tap + T],
                                                start=(tap == 0), stop=(tap == TAPS - 1))
                last.then_inc(S["u_ps"], 1)

            def z_proj(b):
                for c in range(ND):
                    last = nc.tensor.matmul(halves("O0")[:, c, :], w_z[:, c * P:(c + 1) * P], h1[:, PAD:PAD + T], start=True, stop=True)
                last.then_inc(S["z_ps"], 1)

            def scan_inputs(b):
                pe.wait_ge(S["uT"], at("uT", b))
                for k in range(ND):
                    last = nc.tensor.matmul(bank["O1"][0:96, 0:T], w_bc[:, k, :], uT[:, k, :], start=(k == 0), stop=(k == ND - 1))
                last.then_inc(S["bc_ps"], 1)
                pe.wait_ge(S["y1"], at("y1", b, 0))
                for c in range(ND):
                    for k in range(ND):
                        last = nc.tensor.matmul(halves("Y")[:, c, :], w_dt[:, k, c * P:(c + 1) * P], uT[:, k, :],
                                                start=(k == 0), stop=(k == ND - 1))
                last.then_inc(S["dt_ps"], 1)

            def spread_b(i, p):
                if p > 0:
                    pe.wait_ge(S["db"], at("db", i, p))
                for m in range(2):
                    last = nc.tensor.matmul(halves("B")[:, m, :], sel[:, 2 * p + m, :], bc3[:], start=True, stop=True)
                last.then_inc(S["bb_ps"], 1)

            def spread_c(i, p):
                if p > 0:
                    pe.wait_ge(S["ys"], at("ys", i, p))
                for m in range(2):
                    last = nc.tensor.matmul(halves("C")[:, m, :], sel[:, NS + 2 * p + m, :], bc3[:], start=True, stop=True)
                last.then_inc(S["cb_ps"], 1)

            def first_spread(b):
                pe.wait_ge(S["bc3"], at("bc3", b))
                spread_b(b, 0)
                spread_c(b, 0)

            def sum_states(i, p):
                pe.wait_ge(S["ys"], at("ys", i, p + 1))
                if p == 0:
                    pe.wait_ge(S["thd"], at("thd", i))
                for m in range(2):
                    last = nc.tensor.matmul(halves("Y"), ident[:], st[p % 2][:, :, m, :],
                                            start=(p == 0 and m == 0), stop=(p == 7 and m == 1))
                last.then_inc(S["y_ps"], 1)

            def scores(j, h):
                f, a, g = h // 2, DH * (h % 2), h // REP
                if h >= 2:
                    pe.wait_ge(S["pt"], at("pt", j, h - 1))
                if h == 0:
                    pe.wait_ge(S["negm"], at("negm", j))
                for kt in range(NT):
                    dst = halves(f"S{h % 2}")[:, kt, :]
                    nc.tensor.matmul(dst, qT[a:a + DH, NF + g, kt * P:(kt + 1) * P], qT[a:a + DH, f, :], start=True, stop=False)
                    last = nc.tensor.matmul(dst, onehot[a:a + DH, h, :], negm[a:a + DH, :], start=False, stop=True)
                last.then_inc(S["sc_ps"], 1)

            def weighted(j, h):
                pe.wait_ge(S["pt"], at("pt", j, h + 1))
                if h % 2 == 0 and h >= 4:
                    pe.wait_ge(S["on"], at("on", j, h // 2 - 1))
                for qt in range(NT):
                    c = (DH + 1) * (2 * (h % 2) + qt)
                    for kt in range(NT):
                        last = nc.tensor.matmul(bank[f"O{h // 2 % 2}"][:, c:c + DH + 1], pt[h % 2][:, kt, qt * P:(qt + 1) * P],
                                                va[:, kt, h // REP, :], start=(kt == 0), stop=(kt == NT - 1))
                last.then_inc(S["av"], 1)

            def heads_to_T(j, g):
                pe.wait_ge(S["on"], at("on", j, 2 * g + 2))
                if g > 0:
                    pe.wait_ge(S["ot"], at("ot", j, g))
                for f in range(2):
                    for t in range(NT):
                        src = on[:, t, 4 * g + 2 * f:4 * g + 2 * f + 2, :].rearrange("p h f -> p (h f)")
                        last = nc.tensor.transpose(halves("M")[:, f, t * P:(t + 1) * P], src, ident[:])
                last.then_inc(S["ot_ps"], 1)

            def attention_out(j):
                pe.wait_ge(S["ot"], at("ot", j))
                for t in range(NT):
                    for f in range(NF):
                        last = nc.tensor.matmul(halves("M", P)[:, t, :], oT[:, f, t * P:(t + 1) * P], w_o[:, f, :],
                                                start=(f == 0), stop=(f == NF - 1))
                last.then_inc(S["o1_ps"], 1)

            def keys_and_receptance(j):
                pe.wait_ge(S["xk"], at("xk", j))
                nc.tensor.matmul(bank["S0"][:, 0:T], w_k[:], xk[:], start=True, stop=True).then_inc(S["kk_ps"], 1)
                pe.wait_ge(S["xr"], at("xr", j))
                for t in range(NT):
                    last = nc.tensor.matmul(halves("S1", P)[:, t, :], xr[:, t * P:(t + 1) * P], w_r[:], start=True, stop=True)
                last.then_inc(S["rr_ps"], 1)

            def values(j):
                pe.wait_ge(S["ka"], at("ka", j))
                for t in range(NT):
                    last = nc.tensor.matmul(halves("S0", P)[:, t, :], ka[:, t * P:(t + 1) * P], w_v[:], start=True, stop=True)
                last.then_inc(S["vv_ps"], 1)

            def scan_proj(i):
                pe.wait_ge(S["yT"], at("yT", i))
                for t in range(NT):
                    for k in range(ND):
                        last = nc.tensor.matmul(halves("B", P)[:, t, :], yT[:, k, t * P:(t + 1) * P], w_out[:, k, :],
                                                start=(k == 0), stop=(k == ND - 1))
                last.then_inc(S["o0_ps"], 1)

            def router_and_lora_a(i):
                pe.wait_ge(S["h2"], at("h2", i))
                for t in range(NT):
                    dst = bank["C"][:, t * E:(t + 1) * E]
                    nc.tensor.matmul(dst, h2[:, t * P:(t + 1) * P], w_rt[:], start=True, stop=False)
                    last = nc.tensor.matmul(dst, ones_row[:], rows[:, P:P + E], start=False, stop=True)
                last.then_inc(S["lg_ps"], 1)
                nc.tensor.matmul(bank["B"][:, 0:T], w_la[:], h2[:], start=True, stop=True).then_inc(S["ax_ps"], 1)

            def weights_to_T(i):
                pe.wait_ge(S["wx"], at("wx", i))
                for t in range(NT):
                    last = nc.tensor.transpose(bank["C"][:, t * P:(t + 1) * P], wx[:, t, :, :].rearrange("p e r -> p (e r)"), ident[:])
                last.then_inc(S["wt_ps"], 1)

            def experts_out(i):
                pe.wait_ge(S["axw"], at("axw", i))
                for t in range(NT):
                    dst = halves("C", P)[:, t, :]
                    nc.tensor.matmul(dst, h2[:, t * P:(t + 1) * P], w_base[:], start=True, stop=False)
                    nc.tensor.matmul(dst, ones_row[:], rows[:, 0:P], start=False, stop=False)
                    last = nc.tensor.matmul(dst, axw[:, t * P:(t + 1) * P], w_lb[:], start=False, stop=True)
                last.then_inc(S["f0_ps"], 1)

            def qkv(i, prev, nxt):
                turn_xn(i, 2, "B")
                pe.wait_ge(S["h3"], at("h3", i))
                pe.wait_ge(S["x2"], at("x2", i))
                if prev:
                    pe.wait_ge(S["t4"], at("t4", i - 1, 1))
                    pe.wait_ge(S["thr"], at("thr", i - 1))
                if nxt:
                    pe.wait_ge(S["gz"], at("gz", i + 1))
                    pe.wait_ge(S["bc_rest"], at("bc_rest", i + 1, 1))
                for t in range(NT):
                    for n in range(3):
                        nc.tensor.matmul(bank[QKV_BANKS[t][n]][:], h3[:, t * P:(t + 1) * P], w_qkv[:, 512 * n:512 * n + 512],
                                         start=True, stop=True).then_inc(S["qkv_ps"], 1)
                pe.wait_ge(S["qr"], at("qr", i))
                pe.wait_ge(S["va"], at("va", i))
                for n in range(6):
                    for f in range(2):
                        for t in range(NT):
                            src = qr[:, t, 2 * (2 * n + f):2 * (2 * n + f) + 2, :].rearrange("p h f -> p (h f)")
                            last = nc.tensor.transpose(halves(QT_BANKS[n])[:, f, t * P:(t + 1) * P], src, ident[:])
                    last.then_inc(S["qT_ps"], 1)
                if nxt:
                    pe.wait_ge(S["qT"], at("qT", i, 2))
                    first_spread(i + 1)
                pe.wait_ge(S["qTb"], at("qTb", i))
                for n, (hp, q, t) in enumerate(MAX_STEPS):
                    if n >= 4:
                        pe.wait_ge(S["mx"], at("mx", i, n - 3))
                    for m in range(2):
                        f, a = 2 * q + m, DH * hp
                        last = nc.tensor.matmul(halves(MAX_BANKS[n % 4])[:, m, :], qTb[a:a + DH, f, t * P:(t + 1) * P],
                                                qTb[a:a + DH, NF + 2 * f // REP, :], start=True, stop=True)
                    last.then_inc(S["ms_ps"], 1)
                pe.wait_ge(S["mn"], at("mn", i))
                for t in range(NT):
                    last = nc.tensor.transpose(bank["M"][:, t * P // 2:(t + 1) * P // 2].bitcast(BF16), mn[:, t, :], identb[:])
                last.then_inc(S["mn_ps"], 1)

            def turn(i, prev, cur, nxt):
                if prev:
                    scores(i - 1, 0)
                if cur:
                    spread_b(i, 1)
                for p in range(8):
                    if cur and p > 0:
                        spread_c(i, p)
                        sum_states(i, p - 1)
                    if prev:
                        scores(i - 1, 2 * p + 1)
                        weighted(i - 1, 2 * p)
                    if cur and p < 6:
                        spread_b(i, p + 2)
                    if prev:
                        if p < 7:
                            scores(i - 1, 2 * p + 2)
                        weighted(i - 1, 2 * p + 1)
                        if p in (3, 5, 7):
                            heads_to_T(i - 1, (p - 3) // 2)
                if cur:
                    sum_states(i, 7)
                if prev:
                    heads_to_T(i - 1, 3)
                if cur:
                    scan_proj(i)
                if prev:
                    attention_out(i - 1)
                if cur:
                    turn_xn(i, 1, "B")
                if prev:
                    turn_xn(i - 1, 3, "M")
                if nxt:
                    pe.wait_ge(S["gz"], at("gz", i + 1, 0))
                    turn_xn(i + 1, 0, "O0")
                if cur:
                    router_and_lora_a(i)
                if prev:
                    keys_and_receptance(i - 1)
                if nxt:
                    conv(i + 1)
                if cur:
                    weights_to_T(i)
                if nxt:
                    z_proj(i + 1)
                if prev:
                    values(i - 1)
                if cur:
                    experts_out(i)
                if nxt:
                    scan_inputs(i + 1)
                if cur:
                    qkv(i, prev, nxt)

            pe.wait_ge(s_pre_dve, 4)
            pe.wait_ge(s_pre_act, 6)
            turn(-1, False, False, True)
            first_spread(0)
            pe.wait_ge(s_w1, LATE)
            turn(0, False, True, True)
            with pe.Fori(1, B - 1) as i:
                turn(i, True, True, True)
            turn(B - 1, True, True, False)
            turn(B, True, False, False)


QKV_BANKS = (("B", "C", "S0"), ("S1", "O0", "O1"))
QT_BANKS = ("B", "C", "S0", "S1", "O0", "O1")
MAX_BANKS = ("S0", "S1", "O0", "O1")
MAX_STEPS = [(hp, q, t) for q in range(NF // 2) for t in range(NT) for hp in range(2)]


def kernel(**inputs):
    import numpy as np
    import concourse.bacc as bacc
    from concourse.bass_utils import run_bass_kernel_spmd as run

    a = {k: np.asarray(v) for k, v in inputs.items()}
    m0, m1, f0, f1 = "L0_attn_", "L1_attn_", "L0_ffn_", "L1_ffn_"

    def tiles(w):
        w = w.reshape((w.shape[0] // P, P) + w.shape[1:])
        return np.moveaxis(w, 0, 1)

    in_w = a[m0 + "in_proj_w"]
    bc = np.concatenate([a[m0 + "B_w"], a[m0 + "C_w"]]).T
    mod = np.stack([a["L0_wmod"], a["L1_wmod"]]).reshape(2, P, 6, P)
    pos = np.maximum(np.arange(T, dtype=np.float32) - 1, 0)
    inv_freq = (1.0 / np.float32(10000.0) ** (np.arange(0, DH, 2, dtype=np.float32) / DH)).astype(np.float32)
    angle = np.concatenate([pos[:, None] * inv_freq[None, :]] * 2, axis=1).astype(np.float32)
    sign = np.where(np.arange(DH) < DH // 2, -1.0, 1.0).astype(np.float32)
    cs = np.stack([np.cos(angle), np.sin(angle) * sign], axis=1).astype(np.float32)
    pick = np.zeros((P, 32 + H), np.float32)
    for p in range(P):
        pick[p, p % 32] = 1.0
        if p % 64 < H:
            pick[p, 32 + p % 64] = 1.0
    arrays = {
        "x": a[m0 + "x"],
        "cT": np.stack([a["L0_c"].T, a["L1_c"].T], axis=1),
        "wmod": np.moveaxis(mod, 0, 1),
        "w_inx": tiles(in_w[:DI]),
        "w_conv": tiles(a[m0 + "conv_w"].transpose(1, 2, 0)),
        "w_z": in_w[DI:].T,
        "cols": np.concatenate([tiles(a[m0 + "conv_b"]), tiles(a[m0 + "dt_b"]), tiles(a[m0 + "D"]),
                                a[f1 + "mu_r"][:, None], a[f1 + "mu_k"][:, None]], axis=1),
        "a_log": tiles(a[m0 + "A_log"]),
        "pick": pick,
        "w_dt": tiles(a[m0 + "dt_w"].T),
        "w_bc": tiles(np.concatenate([bc, bc, bc], axis=1)),
        "cs": tiles(cs),
        "w_out": tiles(a[m0 + "out_w"].T),
        "w_base": a[f0 + "base_w"].T,
        "w_la": a[f0 + "lora_A"].transpose(1, 0, 2).reshape(P, E * R),
        "w_lb": a[f0 + "lora_B"].reshape(E * R, P),
        "w_rt": a[f0 + "router_w"].T,
        "rows": np.concatenate([a[f0 + "base_b"], a[f0 + "router_b"]])[None, :],
        "norm_w": np.broadcast_to(np.stack([a[m1 + "q_norm_w"], a[m1 + "k_norm_w"]]), (P, 2, DH)),
        "w_qkv": np.concatenate([a[m1 + "Wq"], a[m1 + "Wk"], a[m1 + "Wv"]]).T,
        "w_o": tiles(a[m1 + "Wo"].T),
        "w_r": a[f1 + "W_r"].T,
        "w_k": a[f1 + "W_k"].T,
        "w_v": a[f1 + "W_v"].T,
    }
    arrays = {k: np.ascontiguousarray(v) for k, v in arrays.items()}
    nc = bacc.Bacc("TRN2", target_bir_lowering=False, num_devices=1)
    d = {k: nc.dram_tensor(f"in_{k}", v.shape, mybir.dt.from_np(v.dtype), kind="ExternalInput").ap()
         for k, v in arrays.items()}
    out = nc.dram_tensor("out", (B, T, P), F32, kind="ExternalOutput").ap()
    build(nc, d, out)
    r = run(nc, [{f"in_{k}": v for k, v in arrays.items()}], core_ids=[0])
    return r.results[0]["out"]
```

```python
from contextlib import ExitStack

import concourse.bass as bass
from concourse import mybir

F32 = mybir.dt.float32
BF16 = mybir.dt.bfloat16
I32 = mybir.dt.int32
ALU = mybir.AluOpType
ACT = mybir.ActivationFunctionType
AX = mybir.AxisListType

P = 128
B, T = 8, 256
NT = T // P
DI = 256
ND = DI // P
NS = 16
TAPS = 4
PAD = TAPS - 1
E, R = 8, 16
LORA_SCALE = 2.0
H, KV, DH = 16, 4, 64
REP = H // KV
HK = H + KV
NF = H * DH // P
LN_EPS, RMS_EPS, STATE_EPS = 1e-5, 1e-6, 1e-6
CLIP = 5.0
RSQRT_SEED = 0x5F1FFFF9
RSQRT_A, RSQRT_B, RSQRT_C = 0.703952253, 2.38924456, 0.375
RSQRT_PARTS = 7
LN_STEPS = 2 + RSQRT_PARTS

EVENTS = dict(
    x_in=16, x0=1, mom0=2, mom1=2, mom2=2, mom3=2, ln0=LN_STEPS, ln1=LN_STEPS, ln23=LN_STEPS, rms=2 + RSQRT_PARTS,
    xn0=1, xn1=1, xn2=1, xn3=1, h_ps0=1, h_ps1=1, h_ps2=1, h_ps3=1, h1=1, h2=1, h3=1, h4=1,
    u_ps=2, z_ps=1, uT=1, thz=1, gz=2, dt_ps=1, thd=1, dt=3, bc_ps=1, bc_hi=1, bc_rest=3, bc3=1,
    bb_ps=8, cb_ps=8, dAx=8, dA=8, db=8, dbe=8, scan=9, ys=7, ys7=2, sum7=2, pair_sum=7, acc=7, du=1, y_ps=2, yT=2,
    o0_ps=1, g0=1, x1=1, ax_ps=1, lg_ps=1, top=5, el=1, wx=1, wt_ps=1, axw=1, f0_ps=1, g1=1, x2=1,
    qkv_ps=6, qs=6, sq=6, va=2, ssq=6, rotc=6, rots=6, rsum=6, qr=4, qr1=2, qT_ps=6, qT=6, qTb=6,
    ms_ps=16, mx=16, mn=2, mn_ps=1, negm=1,
    sc_ps=16, pt=16, av=16, rinv=8, on=8, ot_ps=4, ot=4, o1_ps=1, g2=1, x3=1,
    dd=1, xk=1, xr=1, kk_ps=1, rr_ps=1, kr=1, ka=1, thr=1, vv_ps=1, t4=1, t4g=1, x4=1, out=16,
)


def build(nc, d, out):
    ctx = ExitStack()
    with ctx:
        def sb(name, shape, dt=F32):
            return ctx.enter_context(nc.sbuf_tensor(name, shape, dt))

        def sem(name):
            return ctx.enter_context(nc.semaphore(name))

        w_inx = sb("w_inx", [P, ND, P])
        w_cin = sb("w_cin", [P, TAPS, DI])
        w_z = sb("w_z", [P, DI])
        w_dt = sb("w_dt", [P, ND, DI])
        w_bc = sb("w_bc", [P, ND, 96])
        w_out = sb("w_out", [P, ND, P])
        w_base = sb("w_base", [P, P])
        w_la = sb("w_la", [P, E * R])
        w_lb = sb("w_lb", [E * R, P])
        w_rt = sb("w_rt", [P, E])
        w_qkv = sb("w_qkv", [P, (H + 2 * KV) * DH])
        w_o = sb("w_o", [P, NF, P])
        w_r = sb("w_r", [P, P])
        w_k = sb("w_k", [P, P])
        w_v = sb("w_v", [P, P])
        cT = sb("cT", [P, 2, B])
        cols = sb("cols", [P, 3 * ND + 2])
        a_log = sb("a_log", [P, ND, NS])
        neg_a = sb("neg_a", [P, ND, NS])
        hdtb = sb("hdtb", [P, ND])
        rows = sb("rows", [P, P + E])
        norm_w = sb("norm_w", [P, 2, DH])
        cs = sb("cs", [P, NT, 2, DH])
        rot_c = sb("rot_c", [P, NT, HK, DH])
        rot_s = sb("rot_s", [P, NT, HK, DH])
        ident = sb("ident", [P, P])
        identb = sb("identb", [P, P], BF16)
        sel = sb("sel", [96, 2 * NS, P], BF16)
        onehot = sb("onehot", [P, H, P], BF16)
        pick = sb("pick", [P, 32 + H])
        ones_row = sb("ones_row", [1, P])
        clip = sb("clip", [P, 2])
        cth = sb("cth", [P, 2, B])
        csil = sb("csil", [P, 2, B])
        mod_t = sb("mod_t", [P, 2, 4, B])
        gate = sb("gate", [B, 2, 2, P])
        gabs = sb("gabs", [B, 2, 2, P])
        gates = sb("gates", [P, B, 2, 2, P])
        gate_dram = nc.dram_tensor("gate_scratch", (B, 2, 2, P), F32, kind="Internal").ap()

        xa = sb("xa", [P, NT, P])
        x0 = sb("x0", [P, NT, P])
        x1 = sb("x1", [P, NT, P])
        x2 = sb("x2", [P, NT, P])
        x3 = sb("x3", [P, NT, P])
        x4 = sb("x4", [P, NT, P])
        tmp_g = sb("tmp_g", [P, NT, P])
        stats = sb("stats", [P, 4, NT, 6])
        mv = sb("mv", [P, 4, NT, 2])
        lnv = sb("lnv", [P, 3, 4, NT])
        xn = [sb(f"xn{n}", [P, NT, P]) for n in range(4)]
        h1 = sb("h1", [P, PAD + T])
        h2 = sb("h2", [P, T])
        h3 = sb("h3", [P, T])
        h4 = sb("h4", [P, 1 + T])
        uT = sb("uT", [P, ND, T])
        thz = sb("thz", [P, ND, T])
        gz = sb("gz", [P, ND, T])
        thd = sb("thd", [P, ND, T])
        dt = sb("dt", [P, ND, T])
        dtu = sb("dtu", [P, ND, T])
        bc3 = sb("bc3", [96, T], BF16)
        bc_r = sb("bc_r", [96, T])
        bc_m = sb("bc_m", [96, T], BF16)
        scan_mem = sb("scan_mem", [P, 6, ND * 2 * T])
        dA, dB, st = ([scan_mem[:, 2 * k + n, :].rearrange("p (c m t) -> p c m t", c=ND, m=2) for n in range(2)]
                      for k in range(3))
        scan_flat = scan_mem[:].rearrange("p k x -> p (k x)")
        qn = scan_flat[:, 0:NT * HK * DH].rearrange("p (t h f) -> p t h f", t=NT, h=HK)
        sq = scan_flat[:, NT * HK * DH:2 * NT * HK * DH].rearrange("p (t h f) -> p t h f", t=NT, h=HK)
        w_conv = scan_flat[:, 0:ND * TAPS * DI].rearrange("p (c j o) -> p c j o", c=ND, j=TAPS)
        w_mod = scan_flat[:, ND * TAPS * DI:ND * TAPS * DI + 12 * P].rearrange("p (l j f) -> p l j f", l=2, j=6)
        du = sb("du", [P, ND, T])
        acc = sb("acc", [P, ND, T])
        yT = sb("yT", [P, ND, T])
        m8 = sb("m8", [P, NT, 8])
        nm = sb("nm", [P, NT])
        el = sb("el", [P, NT, E])
        em = sb("em", [P, NT, E])
        es = sb("es", [P, NT])
        er = sb("er", [P, NT])
        wx = sb("wx", [P, NT, E, R])
        axw = sb("axw", [P, T])
        qs = sb("qs", [P, NT * HK * DH])
        dA += [qs[:, n * ND * 2 * T:(n + 1) * ND * 2 * T].rearrange("p (c m t) -> p c m t", c=ND, m=2) for n in range(2)]
        qs = qs[:].rearrange("p (t h f) -> p t h f", t=NT, h=HK)
        qc = sb("qc", [P, NT * HK * DH])
        oT = qc[:, 0:NF * T].rearrange("p (f t) -> p f t", f=NF)
        qc = qc[:].rearrange("p (t h f) -> p t h f", t=NT, h=HK)
        rv = sb("rv", [P, 4, NT, HK])
        qr = sb("qr", [P, NT, H + 2 * KV, DH])
        on = qr[:, :, 0:H, :]
        qT = sb("qT", [P, NF + KV, T])
        qTb = sb("qTb", [P, NF + KV, T], BF16)
        va = sb("va", [P, NT, KV, DH + 1])
        mx = sb("mx", [P, NT, H])
        mn = sb("mn", [P, NT, P], BF16)
        negm = sb("negm", [P, T], BF16)
        pt = [sb(f"pt{n}", [P, NT, T]) for n in range(2)]
        rinv = sb("rinv", [P, 2, 4])
        dd = sb("dd", [P, T])
        xk = sb("xk", [P, T])
        xr = sb("xr", [P, T])
        kr = sb("kr", [P, T])
        ka = sb("ka", [P, T])
        thr = sb("thr", [P, NT, P])
        t4 = sb("t4", [P, NT, P])

        bank = {n: ctx.enter_context(nc.psum_tensor(f"ps_{n}", [P, 512], F32))
                for n in ("B", "C", "Y", "S0", "S1", "O0", "O1", "M")}
        S = {name: sem(f"s_{name}") for name in EVENTS}
        s_wc, s_w0, s_w1, s_const, s_consts, s_onehot = (
            sem(n) for n in ("s_wc", "s_w0", "s_w1", "s_const", "s_consts", "s_onehot"))
        s_pre_act, s_pre_dve, s_pre_pe, s_gate, s_gates, s_rot = (
            sem(n) for n in ("s_pre_act", "s_pre_dve", "s_pre_pe", "s_gate", "s_gates", "s_rot"))

        s_passed = sem("s_passed")

        def at(name, i, k=None):
            n = EVENTS[name]
            return i * n + (n if k is None else k)

        def wait_apart(eng, name, value):
            eng.wait_ge(S[name], value)
            eng.sem_inc(s_passed, 1)

        def halves(bk, n=256):
            return bank[bk][:, 0:2 * n].rearrange("p (a b) -> p a b", a=2)

        lg = halves("M", E)

        def quarters(bk):
            return bank[bk][:].rearrange("p (a b) -> p a b", a=4)

        loads_conv = [(w_inx[:], d["w_inx"]), (w_conv, d["w_conv"])]
        loads_early = [
            (cT[:], d["cT"]), (w_mod, d["wmod"]), (cols[:], d["cols"]), (pick[:], d["pick"]), (a_log[:], d["a_log"]),
            (w_z[:], d["w_z"]), (w_bc[:], d["w_bc"]), (w_dt[:], d["w_dt"]), (cs[:], d["cs"]),
        ]
        loads_late = [
            (w_out[:], d["w_out"]), (w_base[:], d["w_base"]), (w_la[:], d["w_la"]), (w_lb[:], d["w_lb"]),
            (w_rt[:], d["w_rt"]), (rows[:], d["rows"]), (norm_w[:], d["norm_w"]), (w_qkv[:], d["w_qkv"]),
            (w_o[:], d["w_o"]), (w_r[:], d["w_r"]), (w_k[:], d["w_k"]), (w_v[:], d["w_v"]),
        ]
        CONSTS = 9
        CONV, EARLY, LATE = 16 * len(loads_conv), 16 * len(loads_early), 16 * len(loads_late)
        x_view = d["x"].rearrange("b (t p) f -> b p t f", p=P)
        out_view = out.rearrange("b (t p) f -> b p t f", p=P)
        block = ctx.enter_context(nc.Block())

        @block.sync
        def _(sp):
            for dst, src in loads_conv:
                sp.dma_start(dst, src).then_inc(s_wc, 16)
            sp.dma_start(xa[:], x_view[0]).then_inc(S["x_in"], 16)
            for dst, src in loads_early:
                sp.dma_start(dst, src).then_inc(s_w0, 16)
            for dst, src in loads_late:
                sp.dma_start(dst, src).then_inc(s_w1, 16)
            sp.wait_ge(s_gate, 1)
            sp.dma_start(gate_dram, gate[:]).then_inc(s_gates, 16)
            sp.wait_ge(s_gates, 16)
            sp.dma_start(gates[:].rearrange("p b l g f -> p (b l g f)"),
                         gate_dram.rearrange("b l g f -> (b l g f)").partition_broadcast(P)).then_inc(s_gates, 16)

            def load(b):
                sp.wait_ge(S["x0"], at("x0", b, 0))
                sp.wait_ge(S["xn0"], at("xn0", b, 0))
                sp.dma_start(xa[:], x_view[b]).then_inc(S["x_in"], 16)

            def store(b):
                sp.wait_ge(S["x4"], at("x4", b))
                sp.dma_start(out_view[b], x4[:]).then_inc(S["out"], 16)

            load(1)
            with sp.Fori(1, B - 1) as i:
                load(i + 1)
                store(i - 1)
            store(B - 2)
            store(B - 1)
            sp.wait_ge(S["out"], 16 * B)

        @block.gpsimd
        def _(pool):
            nc.gpsimd.memset(ident[:], 0.0).then_inc(s_const, 1)
            nc.gpsimd.memset(ones_row[:], 1.0).then_inc(s_consts, 1)
            nc.gpsimd.memset(h1[:, 0:PAD], 0.0).then_inc(s_consts, 1)
            nc.gpsimd.memset(h4[:, 0:1], 0.0).then_inc(s_consts, 1)
            nc.gpsimd.memset(va[:, :, :, DH:DH + 1], 1.0).then_inc(s_consts, 1)
            nc.gpsimd.memset(mn[:], 0.0).then_inc(s_consts, 1)
            nc.gpsimd.memset(clip[:, 0:1], CLIP).then_inc(s_consts, 1)
            nc.gpsimd.memset(clip[:, 1:2], -CLIP).then_inc(s_consts, 1)
            pool.wait_ge(s_const, 1)
            nc.gpsimd.affine_select(out=ident[:], in_=ident[:], compare_op=ALU.not_equal, fill=1.0, base=0,
                                    pattern=[[-1, P]], channel_multiplier=1).then_inc(s_const, 1)
            pool.wait_ge(s_const, 2)
            nc.gpsimd.tensor_copy(identb[:], ident[:]).then_inc(s_consts, 1)
            pool.wait_ge(s_w0, EARLY)
            nc.gpsimd.tensor_copy(onehot[:], pick[:, 32:32 + H].unsqueeze(2).broadcast_to((P, H, P))).then_inc(s_onehot, 1)
            pool.wait_ge(s_w1, LATE)
            for which, (lo, n) in enumerate(((0, H), (H, KV))):
                for t in range(NT):
                    nc.gpsimd.tensor_tensor(
                        rot_c[:, t, lo:lo + n, :], cs[:, t, 0, :].unsqueeze(1).broadcast_to((P, n, DH)),
                        norm_w[:, which, :].unsqueeze(1).broadcast_to((P, n, DH)), ALU.mult).then_inc(s_rot, 1)
                    for a, b in ((0, DH // 2), (DH // 2, 0)):
                        m = DH // 2
                        nc.gpsimd.tensor_tensor(
                            rot_s[:, t, lo:lo + n, a:a + m], cs[:, t, 1, a:a + m].unsqueeze(1).broadcast_to((P, n, m)),
                            norm_w[:, which, b:b + m].unsqueeze(1).broadcast_to((P, n, m)), ALU.mult).then_inc(s_rot, 1)

            def add_eps(i, p):
                wait_apart(pool, "db", at("db", i, p + 1))
                nc.gpsimd.tensor_scalar(dB[p % 2], dB[p % 2], 1.0, STATE_EPS, ALU.mult, ALU.add)\
                    .then_inc(S["dbe"], 1)

            def pairs(i):
                for p in range(7):
                    add_eps(i, p + 1)
                    pool.wait_ge(S["ys"], at("ys", i, p + 1))
                    two = st[p % 2]
                    if p == 0:
                        nc.gpsimd.tensor_tensor(acc[:], two[:, :, 0, :], two[:, :, 1, :], ALU.add).then_inc(S["pair_sum"], 1)
                        pool.wait_ge(S["pair_sum"], at("pair_sum", i, 1))
                        pool.wait_ge(S["du"], at("du", i))
                        nc.gpsimd.tensor_tensor(acc[:], acc[:], du[:], ALU.add).then_inc(S["acc"], 1)
                    else:
                        nc.gpsimd.tensor_tensor(two[:, :, 0, :], two[:, :, 0, :], two[:, :, 1, :], ALU.add)\
                            .then_inc(S["pair_sum"], 1)
                        pool.wait_ge(S["pair_sum"], at("pair_sum", i, p + 1))
                        pool.wait_ge(S["acc"], at("acc", i, p))
                        nc.gpsimd.tensor_tensor(acc[:], acc[:], two[:, :, 0, :], ALU.add).then_inc(S["acc"], 1)

            def finish(j):
                pool.wait_ge(S["t4"], at("t4", j))
                gt = gates[:, bass.ds(j, 1), 1, 1, :].broadcast_to((P, NT, P))
                nc.gpsimd.tensor_tensor(t4[:], t4[:], gt, ALU.mult).then_inc(S["t4g"], 1)
                pool.wait_ge(S["t4g"], at("t4g", j))
                pool.wait_ge(S["out"], at("out", j, 0))
                nc.gpsimd.tensor_tensor(x4[:], t4[:], x3[:], ALU.add).then_inc(S["x4"], 1)

            def step_size_times_u(b):
                pool.wait_ge(S["dt"], at("dt", b, 2))
                pool.wait_ge(S["uT"], at("uT", b))
                nc.gpsimd.tensor_tensor(dtu[:], dt[:], uT[:], ALU.mult).then_inc(S["dt"], 1)

            def rotate(i):
                pool.wait_ge(S["rsum"], at("rsum", i, 0))
                for t in range(NT):
                    for n in range(3):
                        pool.wait_ge(S["qs"], at("qs", i, 3 * t + n + 1))
                        if t == 0 and n == 0:
                            pool.wait_ge(s_rot, 12)
                        m, hd = DH // 2, HEADS_OF[n]
                        nc.gpsimd.tensor_tensor(qn[:, t, hd, 0:m], qs[:, t, hd, m:DH], rot_s[:, t, hd, 0:m], ALU.mult)
                        nc.gpsimd.tensor_tensor(qn[:, t, hd, m:DH], qs[:, t, hd, 0:m], rot_s[:, t, hd, m:DH], ALU.mult)\
                            .then_inc(S["rots"], 1)

            def rms_of_q(i):
                pool.wait_ge(S["rms"], at("rms", i))
                pool.wait_ge(S["rsum"], at("rsum", i))
                for n in range(2):
                    hd = HEADS_OF[n]
                    nc.gpsimd.tensor_tensor(qr[:, 1, hd, :], qc[:, 1, hd, :], rv[:, 2, 1, hd].unsqueeze(2).broadcast_to((P, 8, DH)),
                                            ALU.mult).then_inc(S["qr1"], 1)

            def keep(b):
                pool.wait_ge(S["x_in"], at("x_in", b))
                wait_apart(pool, "x1", at("x1", b, 0))
                nc.gpsimd.tensor_copy(x0[:], xa[:]).then_inc(S["x0"], 1)

            def turn(i, prev, cur, nxt):
                if cur:
                    pairs(i)
                if nxt:
                    keep(i + 1)
                if cur:
                    rotate(i)
                if nxt:
                    step_size_times_u(i + 1)
                if cur:
                    rms_of_q(i)
                if prev:
                    finish(i - 1)
                if nxt:
                    add_eps(i + 1, 0)

            keep(0)
            step_size_times_u(0)
            add_eps(0, 0)
            turn(0, False, True, True)
            with pool.Fori(1, B - 1) as i:
                turn(i, True, True, True)
            turn(B - 1, True, True, False)
            turn(B, True, False, False)

        @block.scalar
        def _(act):
            act.wait_ge(s_w0, EARLY)
            nc.scalar.activation(cth[:], cT[:], ACT.Tanh, scale=0.5).then_inc(s_pre_act, 1)
            nc.scalar.activation(neg_a[:], a_log[:], ACT.Exp).then_inc(s_pre_act, 1)
            nc.scalar.mul(hdtb[:], cols[:, ND:2 * ND], 0.5).then_inc(s_pre_act, 1)
            act.wait_ge(s_pre_act, 2)
            nc.scalar.mul(neg_a[:], neg_a[:], -1.0).then_inc(s_pre_act, 1)
            act.wait_ge(s_pre_act, 4)
            nc.scalar.copy(sel[:], pick[0:96, 0:32].unsqueeze(2).broadcast_to((96, 32, P))).then_inc(s_consts, 1)
            for j in range(2):
                act.wait_ge(s_pre_pe, 1 + j)
                nc.scalar.copy(w_cin[:, 2 * j:2 * j + 2, :], halves(("S0", "S1")[j])).then_inc(s_pre_act, 1)

            def modulate(i, n, ps, dst, done):
                l, j = n // 2, 2 * (n % 2)
                act.wait_ge(S[f"h_ps{n}"], at(f"h_ps{n}", i))
                nc.scalar.activation(dst, bank[ps][:, 0:T], ACT.Identity, scale=mod_t[:, l, j + 1, bass.ds(i, 1)],
                                     bias=mod_t[:, l, j, bass.ds(i, 1)]).then_inc(S[done], 1)

            def conv_out(b):
                act.wait_ge(S["du"], at("du", b, 0))
                act.wait_ge(S["dt"], at("dt", b, 0))
                act.wait_ge(S["u_ps"], at("u_ps", b))
                for c in range(ND):
                    last = nc.scalar.activation(uT[:, c, :], halves("O1")[:, c, :], ACT.Identity, bias=cols[:, c:c + 1])
                last.then_inc(S["uT"], 1)

            def gate_of_y(b):
                act.wait_ge(S["z_ps"], at("z_ps", b))
                nc.scalar.activation(thz[:], halves("O0"), ACT.Tanh, scale=0.5).then_inc(S["thz"], 1)

            def d_times_u(b):
                act.wait_ge(S["acc"], at("acc", b, 0))
                act.wait_ge(S["uT"], at("uT", b))
                for c in range(ND):
                    last = nc.scalar.mul(du[:, c, :], uT[:, c, :], cols[:, 2 * ND + c:2 * ND + c + 1])
                last.then_inc(S["du"], 1)

            def b_and_c(b):
                act.wait_ge(S["bc_ps"], at("bc_ps", b))
                nc.scalar.copy(bc3[:], bank["O1"][0:96, 0:T]).then_inc(S["bc_hi"], 1)

            def step_size(b):
                act.wait_ge(S["dt_ps"], at("dt_ps", b))
                for c in range(ND):
                    last = nc.scalar.activation(thd[:, c, :], halves("Y")[:, c, :], ACT.Tanh, scale=0.5, bias=hdtb[:, c:c + 1])
                last.then_inc(S["thd"], 1)

            def decay(i, p, c):
                k = DECAYS.index(p)
                if k == 0 and c == 0:
                    act.wait_ge(S["dt"], at("dt", i, 2))
                    act.wait_ge(S["rotc"], at("rotc", i, 0))
                    act.wait_ge(S["rots"], at("rots", i, 0))
                if p == 0 and c == 0:
                    act.wait_ge(S["ssq"], at("ssq", i, 0))
                    act.wait_ge(S["rsum"], at("rsum", i, 0))
                if p >= 4 and c == 0:
                    act.wait_ge(S["scan"], at("scan", i, p - 3))
                for m in range(2):
                    n = 2 * p + m
                    last = nc.scalar.activation(dA[p % 4][:, c, m, :], dt[:, c, :], ACT.Relu, scale=neg_a[:, c, n:n + 1],
                                                bias=clip[:, 0:1])
                if c == ND - 1:
                    last.then_inc(S["dAx"], 1)
                    act.wait_ge(S["dAx"], at("dAx", i, k + 1))
                    nc.scalar.activation(dA[p % 4], dA[p % 4], ACT.Exp, bias=clip[:, 1:2]).then_inc(S["dA"], 1)

            def probs(j, h):
                act.wait_ge(S["sc_ps"], at("sc_ps", j, h + 1))
                if h >= 2:
                    act.wait_ge(S["av"], at("av", j, h - 1))
                nc.scalar.activation(pt[h % 2][:], halves(f"S{h % 2}"), ACT.Exp).then_inc(S["pt"], 1)

            def heads_to_T(j, g):
                act.wait_ge(S["ot_ps"], at("ot_ps", j, g + 1))
                nc.scalar.copy(oT[:, 2 * g:2 * g + 2, :], halves(HEADS_BANKS[g])).then_inc(S["ot"], 1)

            def relu_squared(j):
                act.wait_ge(S["kk_ps"], at("kk_ps", j))
                nc.scalar.activation(kr[:], bank["M"][:, 0:T], ACT.Relu).then_inc(S["kr"], 1)
                act.wait_ge(S["kr"], at("kr", j))
                nc.scalar.activation(ka[:], kr[:], ACT.Square).then_inc(S["ka"], 1)

            def receptance(j):
                act.wait_ge(S["rr_ps"], at("rr_ps", j))
                nc.scalar.activation(thr[:].rearrange("p t f -> p (t f)"), bank["Y"][:, 0:T], ACT.Tanh, scale=0.5)\
                    .then_inc(S["thr"], 1)

            def router_exp(i):
                act.wait_ge(S["top"], at("top", i, 2))
                for t in range(NT):
                    last = nc.scalar.activation(el[:, t, :], lg[:, t, :], ACT.Exp, bias=nm[:, t:t + 1])
                last.then_inc(S["el"], 1)

            def weighted_a(i):
                act.wait_ge(S["wt_ps"], at("wt_ps", i))
                nc.scalar.mul(axw[:], bank["B"][:, 0:T], LORA_SCALE).then_inc(S["axw"], 1)

            def qkv(i, t):
                if t == 0:
                    act.wait_ge(S["scan"], at("scan", i, 4))
                for n in range(3):
                    act.wait_ge(S["qkv_ps"], at("qkv_ps", i, 3 * t + n + 1))
                    hd = HEADS_OF[n]
                    src = bank[QKV_BANKS[t][n]][:, 0:(hd.stop - hd.start) * DH].rearrange("p (h f) -> p h f", f=DH)
                    nc.scalar.copy(qs[:, t, hd, :], src).then_inc(S["qs"], 1)
                    nc.scalar.activation(sq[:, t, hd, :], src, ACT.Square).then_inc(S["sq"], 1)
                src = bank[QKV_BANKS[t][2]][:, KV * DH:2 * KV * DH].rearrange("p (h f) -> p h f", f=DH)
                nc.scalar.copy(va[:, t, :, 0:DH], src).then_inc(S["va"], 1)

            def qk_copies(i):
                for n, wide in QT_COPIES:
                    f, t = QT_GROUPS[n]
                    act.wait_ge(S["qT_ps"], at("qT_ps", i, n + 1))
                    dst, done = (qT, "qT") if wide else (qTb, "qTb")
                    nc.scalar.copy(dst[:, f:f + 4, t * P:(t + 1) * P], quarters(QT_BANKS[n])).then_inc(S[done], 1)

            def largest_scores(i):
                act.wait_ge(S["mn_ps"], at("mn_ps", i))
                nc.scalar.copy(negm[:], bank["M"][:, 0:T // 2].bitcast(BF16)).then_inc(S["negm"], 1)

            def turn(i, prev, cur, nxt):
                for p in range(8):
                    if prev:
                        probs(i - 1, 2 * p)
                    if cur and p in DECAY_AT:
                        decay(i, DECAY_AT[p], 0)
                    if prev:
                        probs(i - 1, 2 * p + 1)
                    if nxt and p == 7:
                        modulate(i + 1, 0, "M", h1[:, PAD:PAD + T], "h1")
                    if cur and p in DECAY_AT:
                        decay(i, DECAY_AT[p], 1)
                    if prev and p in (3, 5):
                        heads_to_T(i - 1, (p - 3) // 2)
                if prev:
                    heads_to_T(i - 1, 2)
                    heads_to_T(i - 1, 3)
                if nxt:
                    gate_of_y(i + 1)
                if cur:
                    modulate(i, 1, "B", h2[:], "h2")
                    router_exp(i)
                    weighted_a(i)
                if nxt:
                    conv_out(i + 1)
                    b_and_c(i + 1)
                if cur:
                    modulate(i, 2, "B", h3[:], "h3")
                if prev:
                    modulate(i - 1, 3, "M", h4[:, 1:1 + T], "h4")
                if cur:
                    qkv(i, 0)
                if prev:
                    relu_squared(i - 1)
                    receptance(i - 1)
                if cur:
                    qkv(i, 1)
                if nxt:
                    d_times_u(i + 1)
                    step_size(i + 1)
                    for c in range(ND):
                        decay(i + 1, 2, c)
                if cur:
                    qk_copies(i)
                if nxt:
                    for p in range(2):
                        for c in range(ND):
                            decay(i + 1, p, c)
                if cur:
                    largest_scores(i)

            act.wait_ge(s_pre_dve, 4)
            act.wait_ge(s_consts, CONSTS)
            turn(-1, False, False, True)
            turn(0, False, True, True)
            with act.Fori(1, B - 1) as i:
                turn(i, True, True, True)
            turn(B - 1, True, True, False)
            turn(B, True, False, False)

        @block.vector
        def _(dve):
            dve.wait_ge(s_w0, EARLY)
            dve.wait_ge(s_pre_act, 1)
            nc.vector.scalar_tensor_tensor(out=csil[:], in0=cth[:], scalar=1.0, in1=cT[:], op0=ALU.add, op1=ALU.mult)\
                .then_inc(s_pre_dve, 1)
            dve.wait_ge(s_pre_dve, 1)
            nc.vector.tensor_scalar(csil[:], csil[:], 0.5, None, ALU.mult).then_inc(s_pre_dve, 1)
            dve.wait_ge(s_pre_pe, 3)
            mod_ps = bank["M"][:, 0:64].rearrange("p (l j b) -> p l j b", l=2, j=4)
            for l in range(2):
                nc.vector.tensor_copy(mod_t[:, l, 0:4:2, :], mod_ps[:, l, 0:4:2, :])
                nc.vector.tensor_scalar(mod_t[:, l, 1:4:2, :], mod_ps[:, l, 1:4:2, :], 1.0, None, ALU.add)\
                    .then_inc(s_pre_dve, 1)
            def rsqrt_seed(y, v, s):
                nc.vector.tensor_scalar(y.bitcast(I32), v.bitcast(I32), -0.5, float(RSQRT_SEED), ALU.mult, ALU.add)\
                    .then_inc(S[s], 1)

            def rsqrt_part(n, y, v, a, s, i):
                dve.wait_ge(S[s], at(s, i, 2 + n))
                if n in (0, 3):
                    last = nc.vector.tensor_tensor(a, y, y, ALU.mult)
                elif n == 1:
                    last = nc.vector.scalar_tensor_tensor(out=a, in0=a, scalar=-RSQRT_A * RSQRT_C, in1=v, op0=ALU.mult, op1=ALU.mult)
                elif n == 2:
                    last = nc.vector.scalar_tensor_tensor(out=y, in0=a, scalar=RSQRT_A * RSQRT_B * RSQRT_C, in1=y,
                                                          op0=ALU.add, op1=ALU.mult)
                elif n == 4:
                    last = nc.vector.scalar_tensor_tensor(out=a, in0=a, scalar=RSQRT_C ** -2, in1=v, op0=ALU.mult, op1=ALU.mult)
                elif n == 5:
                    last = nc.vector.scalar_tensor_tensor(out=a, in0=a, scalar=-10 / 3, in1=a, op0=ALU.add, op1=ALU.mult)
                else:
                    last = nc.vector.scalar_tensor_tensor(out=y, in0=a, scalar=5.0, in1=y, op0=ALU.add, op1=ALU.mult)
                last.then_inc(S[s], 1)

            def moments(b, slot, x):
                mom = f"mom{slot}"
                for t in range(NT):
                    last = nc.vector.bn_stats(stats[:, slot, t, :], x[:, t, :])
                last.then_inc(S[mom], 1)
                wait_apart(dve, mom, at(mom, b, 1))
                for t in range(NT):
                    last = nc.vector.bn_aggr(mv[:, slot, t, :], stats[:, slot, t, :])
                last.then_inc(S[mom], 1)
                dve.wait_ge(S[mom], at(mom, b, 2))

            def norm_vars(lo, hi):
                return tuple(lnv[:, k, lo:hi, :] for k in (1, 0, 2))

            def deviations_start(lo, hi, s, i):
                y, v, a = norm_vars(lo, hi)
                nc.vector.tensor_scalar(v, mv[:, lo:hi, :, 1], LN_EPS, None, ALU.add).then_inc(S[s], 1)
                dve.wait_ge(S[s], at(s, i, 1))
                rsqrt_seed(y, v, s)

            def deviations_parts(lo, hi, s, i, parts):
                for n in parts:
                    rsqrt_part(n, *norm_vars(lo, hi), s, i)

            def deviations(lo, hi, s, i):
                deviations_start(lo, hi, s, i)
                deviations_parts(lo, hi, s, i, range(RSQRT_PARTS))
                dve.wait_ge(S[s], at(s, i, LN_STEPS))

            def normed(b, n, slot, x):
                for t in range(NT):
                    last = nc.vector.tensor_scalar(xn[n][:, t, :], x[:, t, :], mv[:, slot, t, 0:1], lnv[:, 1, slot, t:t + 1],
                                                   ALU.subtract, ALU.mult)
                last.then_inc(S[f"xn{n}"], 1)

            def residual(i, banks, l, g, x, y, step, done):
                gt = gates[:, bass.ds(i, 1), l, g, :].broadcast_to((P, NT, P))
                for t in range(NT):
                    last = nc.vector.tensor_tensor(tmp_g[:, t, :], bank[banks[t]][:, 0:P], gt[:, t, :], ALU.mult)
                last.then_inc(S[step], 1)
                dve.wait_ge(S[step], at(step, i))
                nc.vector.tensor_tensor(y[:], tmp_g[:], x[:], ALU.add).then_inc(S[done], 1)
                dve.wait_ge(S[done], at(done, i))

            def split_bc_rest(b):
                dve.wait_ge(S["bc_hi"], at("bc_hi", b))
                nc.vector.tensor_tensor(bc_r[:], bank["O1"][0:96, 0:T], bc3[:], ALU.subtract).then_inc(S["bc_rest"], 1)

            def split_bc_middle(b):
                dve.wait_ge(S["bc_rest"], at("bc_rest", b, 1))
                nc.vector.tensor_copy(bc_m[:], bc_r[:]).then_inc(S["bc_rest"], 1)

            def split_bc_parts(b):
                dve.wait_ge(S["bc_rest"], at("bc_rest", b, 2))
                nc.vector.tensor_copy(bc3[32:64, :], bc_m[32:64, :]).then_inc(S["bc_rest"], 1)
                nc.vector.tensor_tensor(bc3[64:96, :], bc_r[64:96, :], bc_m[64:96, :], ALU.subtract).then_inc(S["bc3"], 1)

            def gate_of_y(b, c):
                dve.wait_ge(S["thz"], at("thz", b))
                nc.vector.scalar_tensor_tensor(out=gz[:, c, :], in0=thz[:, c, :], scalar=1.0, in1=halves("O0")[:, c, :],
                                               op0=ALU.add, op1=ALU.mult).then_inc(S["gz"], 1)

            def step_size_sigmoid(b):
                dve.wait_ge(S["thd"], at("thd", b))
                nc.vector.tensor_scalar(dt[:], thd[:], 0.5, 0.5, ALU.mult, ALU.add).then_inc(S["dt"], 1)

            def step_size_clip(b):
                dve.wait_ge(S["dt"], at("dt", b, 1))
                nc.vector.tensor_scalar(dt[:], dt[:], 1e-4, 1.0, ALU.max, ALU.min).then_inc(S["dt"], 1)

            def inject(i, p):
                if p == 0:
                    dve.wait_ge(S["dt"], at("dt", i))
                dve.wait_ge(S["bb_ps"], at("bb_ps", i, p + 1))
                nc.vector.tensor_tensor(dB[p % 2], halves("B").unsqueeze(1).broadcast_to((P, ND, 2, T)),
                                        dtu[:].unsqueeze(2).broadcast_to((P, ND, 2, T)), ALU.mult).then_inc(S["db"], 1)

            def scan(i, p, tiles=range(ND)):
                dve.wait_ge(S["dA"], at("dA", i, DECAYS.index(p) + 1))
                dve.wait_ge(S["dbe"], at("dbe", i, p + 1))
                if p >= 2:
                    dve.wait_ge(S["acc"], at("acc", i, p - 1))
                for c in tiles:
                    for m in range(2):
                        last = nc.vector.tensor_tensor_scan(st[p % 2][:, c, m, :], dA[p % 4][:, c, m, :],
                                                            dB[p % 2][:, c, m, :], 0.0, ALU.mult, ALU.add)
                last.then_inc(S["scan"], 1)

            def times_c(i, p):
                dve.wait_ge(S["scan"], at("scan", i, p + 1))
                dve.wait_ge(S["cb_ps"], at("cb_ps", i, p + 1))
                nc.vector.tensor_tensor(st[p % 2], halves("C").unsqueeze(1).broadcast_to((P, ND, 2, T)), st[p % 2],
                                        ALU.mult).then_inc(S["ys"], 1)

            def last_times_c(i, c):
                dve.wait_ge(S["scan"], at("scan", i, 8 + c))
                dve.wait_ge(S["cb_ps"], at("cb_ps", i))
                nc.vector.tensor_tensor(st[1][:, c, :, :], halves("C"), st[1][:, c, :, :], ALU.mult).then_inc(S["ys7"], 1)

            def last_sum(i, c):
                dve.wait_ge(S["ys7"], at("ys7", i, c + 1))
                nc.vector.tensor_tensor(st[1][:, c, 0, :], st[1][:, c, 0, :], st[1][:, c, 1, :], ALU.add).then_inc(S["sum7"], 1)

            def weigh(j, n):
                dve.wait_ge(S["av"], at("av", j, 2 * n + 2))
                o = bank[f"O{n % 2}"][:, 0:4 * (DH + 1)].rearrange("p (a f) -> p a f", a=4)
                nc.vector.reciprocal(rinv[:, n % 2, :], o[:, :, DH]).then_inc(S["rinv"], 1)
                dve.wait_ge(S["rinv"], at("rinv", j, n + 1))
                for hh in range(2):
                    last = nc.vector.tensor_tensor(on[:, :, 2 * n + hh, :], o[:, 2 * hh:2 * hh + 2, 0:DH],
                                                   rinv[:, n % 2, 2 * hh:2 * hh + 2].unsqueeze(2).broadcast_to((P, NT, DH)), ALU.mult)
                last.then_inc(S["on"], 1)

            def shift_mix(j):
                dve.wait_ge(S["h4"], at("h4", j))
                nc.vector.tensor_tensor(dd[:], h4[:, 1:1 + T], h4[:, 0:T], ALU.subtract).then_inc(S["dd"], 1)
                dve.wait_ge(S["dd"], at("dd", j))
                for n, dst, done in ((1, xk, "xk"), (0, xr, "xr")):
                    nc.vector.scalar_tensor_tensor(out=dst[:], in0=dd[:], scalar=cols[:, 3 * ND + n:3 * ND + n + 1],
                                                   in1=h4[:, 0:T], op0=ALU.mult, op1=ALU.add).then_inc(S[done], 1)

            def finish(j):
                dve.wait_ge(S["thr"], at("thr", j))
                dve.wait_ge(S["vv_ps"], at("vv_ps", j))
                nc.vector.scalar_tensor_tensor(out=t4[:], in0=thr[:], scalar=1.0, in1=halves("M", P), op0=ALU.add, op1=ALU.mult)\
                    .then_inc(S["t4"], 1)

            def scan_out(i):
                for c in range(ND):
                    dve.wait_ge(S["y_ps"], at("y_ps", i, c + 1))
                    nc.vector.scalar_tensor_tensor(out=yT[:, c, :], in0=bank[Y_BANKS[c]][:, 0:T], scalar=0.5, in1=gz[:, c, :],
                                                   op0=ALU.mult, op1=ALU.mult).then_inc(S["yT"], 1)

            def router_top(i):
                wait_apart(dve, "lg_ps", at("lg_ps", i))
                for t in range(NT):
                    last = nc.vector.max(m8[:, t, :], lg[:, t, :])
                last.then_inc(S["top"], 1)
                dve.wait_ge(S["top"], at("top", i, 1))
                nc.vector.tensor_scalar(nm[:], m8[:, :, 0], -1.0, None, ALU.mult).then_inc(S["top"], 1)

            def router_weights(i):
                dve.wait_ge(S["el"], at("el", i))
                for t in range(NT):
                    last = nc.vector.scalar_tensor_tensor(out=em[:, t, :], in0=lg[:, t, :], scalar=m8[:, t, 1:2], in1=el[:, t, :],
                                                          op0=ALU.is_ge, op1=ALU.mult)
                last.then_inc(S["top"], 1)
                dve.wait_ge(S["top"], at("top", i, 3))
                nc.vector.tensor_reduce(es[:], em[:], AX.X, ALU.add).then_inc(S["top"], 1)
                dve.wait_ge(S["top"], at("top", i, 4))
                nc.vector.reciprocal(er[:], es[:]).then_inc(S["top"], 1)
                dve.wait_ge(S["top"], at("top", i, 5))
                dve.wait_ge(S["ax_ps"], at("ax_ps", i))
                for t in range(NT):
                    last = nc.vector.scalar_tensor_tensor(
                        out=wx[:, t, :, :], in0=em[:, t, :].unsqueeze(2).broadcast_to((P, E, R)), scalar=er[:, t:t + 1],
                        in1=bank["B"][:, t * P:(t + 1) * P].rearrange("p (e r) -> p e r", e=E), op0=ALU.mult, op1=ALU.mult)
                last.then_inc(S["wx"], 1)

            def rotate_and_square(i, t, n):
                hd = HEADS_OF[n]
                k = 3 * t + n + 1
                dve.wait_ge(S["qs"], at("qs", i, k))
                nc.vector.tensor_tensor(qc[:, t, hd, :], qs[:, t, hd, :], rot_c[:, t, hd, :], ALU.mult).then_inc(S["rotc"], 1)
                dve.wait_ge(S["sq"], at("sq", i, k))
                nc.vector.tensor_reduce(rv[:, 0, t, hd], sq[:, t, hd, :], AX.X, ALU.add).then_inc(S["ssq"], 1)

            def rotated(i, k):
                t, hd = k // 3, HEADS_OF[k % 3]
                dve.wait_ge(S["rotc"], at("rotc", i, k + 1))
                dve.wait_ge(S["rots"], at("rots", i, k + 1))
                nc.vector.tensor_tensor(qc[:, t, hd, :], qc[:, t, hd, :], qn[:, t, hd, :], ALU.add).then_inc(S["rsum"], 1)

            def qkv(i, prev, nxt):
                for t in range(NT):
                    for n in range(3):
                        rotate_and_square(i, t, n)
                if prev:
                    finish(i - 1)
                v, y, a = rv[:, 1, :, :], rv[:, 2, :, :], rv[:, 3, :, :]
                args = (y, v, a, "rms", i)
                dve.wait_ge(S["ssq"], at("ssq", i))
                nc.vector.tensor_scalar(v, rv[:, 0, :, :], 1.0 / DH, RMS_EPS, ALU.mult, ALU.add).then_inc(S["rms"], 1)
                rotated(i, 0)
                dve.wait_ge(S["rms"], at("rms", i, 1))
                rsqrt_seed(y, v, "rms")
                rotated(i, 1)
                for n in range(4):
                    rsqrt_part(n, *args)
                    if nxt and n == 0:
                        step_size_sigmoid(i + 1)
                    rotated(i, 2 + n)
                    if nxt and n == 0:
                        step_size_clip(i + 1)
                for n in range(4, RSQRT_PARTS):
                    rsqrt_part(n, *args)
                dve.wait_ge(S["rms"], at("rms", i))
                dve.wait_ge(S["rsum"], at("rsum", i))
                for t in range(NT):
                    nc.vector.tensor_tensor(qr[:, t, H:, :].rearrange("p (k c) f -> p k c f", c=2),
                                            qc[:, t, H:HK, :].unsqueeze(2).broadcast_to((P, KV, 2, DH)),
                                            y[:, t, H:HK].unsqueeze(2).unsqueeze(3).broadcast_to((P, KV, 2, DH)),
                                            ALU.mult).then_inc(S["qr"], 1)
                for n in range(2):
                    hd = HEADS_OF[n]
                    nc.vector.tensor_tensor(qr[:, 0, hd, :], qc[:, 0, hd, :], y[:, 0, hd].unsqueeze(2).broadcast_to((P, 8, DH)),
                                            ALU.mult).then_inc(S["qr"], 1)
                if nxt:
                    inject(i + 1, 0)
                for n, (hp, q, t) in enumerate(MAX_STEPS):
                    dve.wait_ge(S["ms_ps"], at("ms_ps", i, n + 1))
                    dst = mx[:, t, :].rearrange("p (f c) -> p c f", c=2)[:, hp, 2 * q:2 * q + 2]
                    nc.vector.tensor_reduce(dst, halves(MAX_BANKS[n % 4]), AX.X, ALU.max).then_inc(S["mx"], 1)
                    if nxt and n == 12:
                        inject(i + 1, 1)
                dve.wait_ge(S["mx"], at("mx", i))
                for a in (0, 64):
                    nc.vector.tensor_scalar(mn[:, :, a:a + H], mx[:], -1.0, None, ALU.mult).then_inc(S["mn"], 1)

            def turn(i, prev, cur, nxt):
                for p in range(8):
                    if cur and 0 < p < 7:
                        inject(i, p + 1)
                    if nxt and p == 1:
                        dve.wait_ge(S["x_in"], at("x_in", i + 1))
                        moments(i + 1, 0, xa)
                    if nxt and p == 2:
                        deviations_start(0, 1, "ln0", i + 1)
                    if nxt and 3 <= p < 7:
                        deviations_parts(0, 1, "ln0", i + 1, (2 * p - 6,))
                    if cur and p < 7:
                        scan(i, p)
                    if cur and p == 7:
                        scan(i, p, (0,))
                    if nxt and 3 <= p < 6:
                        deviations_parts(0, 1, "ln0", i + 1, (2 * p - 5,))
                    if prev and 1 <= p < 7:
                        weigh(i - 1, p - 1)
                    if cur and p < 7:
                        times_c(i, p)
                if nxt:
                    dve.wait_ge(S["ln0"], at("ln0", i + 1))
                    normed(i + 1, 0, 0, xa)
                if cur:
                    last_times_c(i, 0)
                    scan(i, 7, (1,))
                    last_sum(i, 0)
                    last_times_c(i, 1)
                    last_sum(i, 1)
                if prev:
                    weigh(i - 1, 6)
                if cur:
                    scan_out(i)
                    dve.wait_ge(S["o0_ps"], at("o0_ps", i))
                    dve.wait_ge(S["x0"], at("x0", i))
                    residual(i, OUT0_BANKS, 0, 0, x0, x1, "g0", "x1")
                    moments(i, 1, x1)
                    deviations_start(1, 2, "ln1", i)
                if prev:
                    weigh(i - 1, 7)
                if cur:
                    deviations_parts(1, 2, "ln1", i, range(RSQRT_PARTS))
                    dve.wait_ge(S["ln1"], at("ln1", i))
                    normed(i, 1, 1, x1)
                if nxt:
                    gate_of_y(i + 1, 0)
                    gate_of_y(i + 1, 1)
                if cur:
                    router_top(i)
                    router_weights(i)
                if prev:
                    dve.wait_ge(S["o1_ps"], at("o1_ps", i - 1))
                    dve.wait_ge(S["x4"], at("x4", i - 1, 0))
                    residual(i - 1, O_BANKS, 1, 0, x2, x3, "g2", "x3")
                    moments(i - 1, 2, x3)
                if cur:
                    dve.wait_ge(S["f0_ps"], at("f0_ps", i))
                    residual(i, FFN_BANKS, 0, 1, x1, x2, "g1", "x2")
                    moments(i, 3, x2)
                if cur or prev:
                    deviations(2 if prev else 3, 4 if cur else 3, "ln23", i)
                if cur:
                    normed(i, 2, 3, x2)
                if prev:
                    normed(i - 1, 3, 2, x3)
                if nxt:
                    split_bc_rest(i + 1)
                    split_bc_middle(i + 1)
                    split_bc_parts(i + 1)
                if prev:
                    shift_mix(i - 1)
                if prev and not cur:
                    finish(i - 1)
                if cur:
                    qkv(i, prev, nxt)

            dve.wait_ge(S["x_in"], at("x_in", 0))
            moments(0, 0, xa)
            deviations(0, 1, "ln0", 0)
            normed(0, 0, 0, xa)
            dve.wait_ge(s_pre_pe, 4)
            gate_ps = bank["B"][0:B, :].rearrange("p (l g f) -> p l g f", l=2, g=2)
            nc.vector.tensor_copy(gate[:], gate_ps).then_inc(s_pre_dve, 1)
            dve.wait_ge(s_pre_dve, 5)
            nc.vector.scalar_tensor_tensor(out=gabs[:], in0=gate[:], scalar=-1.0, in1=gate[:], op0=ALU.mult, op1=ALU.max)\
                .then_inc(s_pre_dve, 1)
            dve.wait_ge(s_pre_dve, 6)
            nc.vector.tensor_scalar(gabs[:], gabs[:], 0.25, None, ALU.max).then_inc(s_pre_dve, 1)
            nc.vector.tensor_scalar(gate[:], gate[:], 0.0, 2.0, ALU.is_ge, ALU.mult).then_inc(s_pre_dve, 1)
            dve.wait_ge(s_pre_dve, 8)
            nc.vector.scalar_tensor_tensor(out=gate[:], in0=gate[:], scalar=-1.0, in1=gabs[:], op0=ALU.add, op1=ALU.mult)\
                .then_inc(s_pre_dve, 1)
            dve.wait_ge(s_pre_dve, 9)
            nc.vector.tensor_scalar(gate[:, 1, 1, :], gate[:, 1, 1, :], 0.5, None, ALU.mult).then_inc(s_gate, 1)
            gate_of_y(0, 0)
            gate_of_y(0, 1)
            split_bc_rest(0)
            split_bc_middle(0)
            split_bc_parts(0)
            step_size_sigmoid(0)
            step_size_clip(0)
            inject(0, 0)
            inject(0, 1)
            dve.wait_ge(s_gates, 32)
            turn(0, False, True, True)
            with dve.Fori(1, B - 1) as i:
                turn(i, True, True, True)
            turn(B - 1, True, True, False)
            turn(B, True, False, False)

        @block.tensor
        def _(pe):
            pe.wait_ge(s_wc, CONV)
            for j in range(2):
                for tap in (2 * j, 2 * j + 1):
                    for c in range(ND):
                        last = nc.tensor.matmul(halves(("S0", "S1")[j])[:, tap % 2, :], w_inx[:, c, :], w_conv[:, c, tap, :],
                                                start=(c == 0), stop=(c == ND - 1))
                last.then_inc(s_pre_pe, 1)
            pe.wait_ge(s_pre_dve, 2)
            pe.wait_ge(s_w0, EARLY)
            mod_ps = bank["M"][:, 0:64].rearrange("p (l j b) -> p l j b", l=2, j=4)
            for l in range(2):
                for j, part in enumerate((0, 1, 3, 4)):
                    last = nc.tensor.matmul(mod_ps[:, l, j, :], w_mod[:, l, part, :], csil[:, l, :], start=True, stop=True)
            last.then_inc(s_pre_pe, 1)
            for l in range(2):
                last = nc.tensor.matmul(bank["B"][0:B, 256 * l:256 * l + 256], csil[:, l, :],
                                        w_mod[:, l, 2:6:3, :], start=True, stop=True)
            last.then_inc(s_pre_pe, 1)
            pe.wait_ge(s_consts, CONSTS)

            def keep_warm(ps, n):
                for _ in range(n):
                    nc.tensor.matmul(bank[ps][:], identb[:], onehot[:, 0:4, :].rearrange("p h f -> p (h f)"), start=True, stop=True)

            def turn_xn(i, n, ps):
                pe.wait_ge(S[f"xn{n}"], at(f"xn{n}", i))
                for t in range(NT):
                    last = nc.tensor.transpose(bank[ps][:, t * P:(t + 1) * P], xn[n][:, t, :], ident[:])
                last.then_inc(S[f"h_ps{n}"], 1)

            def conv(b, c, part):
                for tap in range(part * TAPS // 2, (part + 1) * TAPS // 2):
                    last = nc.tensor.matmul(halves("O1")[:, c, :], w_cin[:, tap, c * P:(c + 1) * P], h1[:, tap:tap + T],
                                            start=(tap == 0), stop=(tap == TAPS - 1))
                if part == 1:
                    last.then_inc(S["u_ps"], 1)

            def z_proj(b):
                for c in range(ND):
                    last = nc.tensor.matmul(halves("O0")[:, c, :], w_z[:, c * P:(c + 1) * P], h1[:, PAD:PAD + T], start=True, stop=True)
                last.then_inc(S["z_ps"], 1)

            def bc_proj(b):
                pe.wait_ge(S["uT"], at("uT", b))
                for k in range(ND):
                    last = nc.tensor.matmul(bank["O1"][0:96, 0:T], w_bc[:, k, :], uT[:, k, :], start=(k == 0), stop=(k == ND - 1))
                last.then_inc(S["bc_ps"], 1)

            def dt_proj(b):
                for c in range(ND):
                    for k in range(ND):
                        last = nc.tensor.matmul(halves("Y")[:, c, :], w_dt[:, k, c * P:(c + 1) * P], uT[:, k, :],
                                                start=(k == 0), stop=(k == ND - 1))
                last.then_inc(S["dt_ps"], 1)

            def spread_b(i, p):
                if p > 0:
                    pe.wait_ge(S["db"], at("db", i, p))
                for m in range(2):
                    last = nc.tensor.matmul(halves("B")[:, m, :], sel[:, 2 * p + m, :], bc3[:], start=True, stop=True)
                last.then_inc(S["bb_ps"], 1)

            def spread_c(i, p):
                if p > 0:
                    pe.wait_ge(S["ys"], at("ys", i, p))
                for m in range(2):
                    last = nc.tensor.matmul(halves("C")[:, m, :], sel[:, NS + 2 * p + m, :], bc3[:], start=True, stop=True)
                last.then_inc(S["cb_ps"], 1)

            def first_spread_b(b):
                pe.wait_ge(S["bc3"], at("bc3", b))
                spread_b(b, 0)

            def sum_states(i):
                pe.wait_ge(S["thd"], at("thd", i))
                pe.wait_ge(S["db"], at("db", i))
                pe.wait_ge(S["acc"], at("acc", i))
                for c in range(ND):
                    nc.tensor.matmul(bank[Y_BANKS[c]][:, 0:T], ident[:], acc[:, c, :], start=True, stop=False)
                for c in range(ND):
                    pe.wait_ge(S["sum7"], at("sum7", i, c + 1))
                    nc.tensor.matmul(bank[Y_BANKS[c]][:, 0:T], ident[:], st[1][:, c, 0, :], start=False, stop=True)\
                        .then_inc(S["y_ps"], 1)

            def scores(j, h):
                f, a, g = h // 2, DH * (h % 2), h // REP
                if h >= 2:
                    pe.wait_ge(S["pt"], at("pt", j, h - 1))
                if h == 0:
                    pe.wait_ge(S["negm"], at("negm", j))
                for kt in range(NT):
                    dst = halves(f"S{h % 2}")[:, kt, :]
                    nc.tensor.matmul(dst, qT[a:a + DH, NF + g, kt * P:(kt + 1) * P], qT[a:a + DH, f, :], start=True, stop=False)
                    last = nc.tensor.matmul(dst, onehot[a:a + DH, h, :], negm[a:a + DH, :], start=False, stop=True)
                last.then_inc(S["sc_ps"], 1)

            def weighted(j, h):
                pe.wait_ge(S["pt"], at("pt", j, h + 1))
                if h % 2 == 0 and h >= 4:
                    pe.wait_ge(S["on"], at("on", j, h // 2 - 1))
                for qt in range(NT):
                    c = (DH + 1) * (2 * (h % 2) + qt)
                    for kt in range(NT):
                        last = nc.tensor.matmul(bank[f"O{h // 2 % 2}"][:, c:c + DH + 1], pt[h % 2][:, kt, qt * P:(qt + 1) * P],
                                                va[:, kt, h // REP, :], start=(kt == 0), stop=(kt == NT - 1))
                last.then_inc(S["av"], 1)

            def heads_to_T(j, g):
                pe.wait_ge(S["on"], at("on", j, 2 * g + 2))
                if 0 < g < 3:
                    pe.wait_ge(S["ot"], at("ot", j, g))
                for f in range(2):
                    for t in range(NT):
                        src = on[:, t, 4 * g + 2 * f:4 * g + 2 * f + 2, :].rearrange("p h f -> p (h f)")
                        last = nc.tensor.transpose(halves(HEADS_BANKS[g])[:, f, t * P:(t + 1) * P], src, ident[:])
                last.then_inc(S["ot_ps"], 1)

            def attention_out(j, g, features):
                pe.wait_ge(S["ot"], at("ot", j, g))
                pe.wait_ge(S["pt"], at("pt", j))
                for t in range(NT):
                    for f in features:
                        last = nc.tensor.matmul(bank[O_BANKS[t]][:, 0:P], oT[:, f, t * P:(t + 1) * P], w_o[:, f, :],
                                                start=(f == 0), stop=(f == NF - 1))
                if g == 4:
                    last.then_inc(S["o1_ps"], 1)

            def keys_and_receptance(j):
                pe.wait_ge(S["xk"], at("xk", j))
                nc.tensor.matmul(bank["M"][:, 0:T], w_k[:], xk[:], start=True, stop=True).then_inc(S["kk_ps"], 1)
                pe.wait_ge(S["xr"], at("xr", j))
                for t in range(NT):
                    last = nc.tensor.matmul(halves("Y", P)[:, t, :], xr[:, t * P:(t + 1) * P], w_r[:], start=True, stop=True)
                last.then_inc(S["rr_ps"], 1)

            def values(j):
                pe.wait_ge(S["ka"], at("ka", j))
                for t in range(NT):
                    last = nc.tensor.matmul(halves("M", P)[:, t, :], ka[:, t * P:(t + 1) * P], w_v[:], start=True, stop=True)
                last.then_inc(S["vv_ps"], 1)

            def scan_proj(i):
                for k in range(ND):
                    pe.wait_ge(S["yT"], at("yT", i, k + 1))
                    for t in range(NT):
                        last = nc.tensor.matmul(bank[OUT0_BANKS[t]][:, 0:P], yT[:, k, t * P:(t + 1) * P], w_out[:, k, :],
                                                start=(k == 0), stop=(k == ND - 1))
                last.then_inc(S["o0_ps"], 1)

            def router_and_lora_a(i):
                pe.wait_ge(S["h2"], at("h2", i))
                for t in range(NT):
                    nc.tensor.matmul(lg[:, t, :], h2[:, t * P:(t + 1) * P], w_rt[:], start=True, stop=False)
                    last = nc.tensor.matmul(lg[:, t, :], ones_row[:], rows[0:1, P:P + E], start=False, stop=True)
                last.then_inc(S["lg_ps"], 1)
                for t in range(NT):
                    last = nc.tensor.matmul(halves("B", P)[:, t, :], h2[:, t * P:(t + 1) * P], w_la[:], start=True, stop=True)
                last.then_inc(S["ax_ps"], 1)

            def base_out(i):
                for t in range(NT):
                    dst = bank[FFN_BANKS[t]][:, 0:P]
                    nc.tensor.matmul(dst, h2[:, t * P:(t + 1) * P], w_base[:], start=True, stop=False)
                    nc.tensor.matmul(dst, ones_row[:], rows[0:1, 0:P], start=False, stop=False)

            def weighted_a_to_T(i):
                pe.wait_ge(S["wx"], at("wx", i))
                for t in range(NT):
                    last = nc.tensor.transpose(bank["B"][:, t * P:(t + 1) * P], wx[:, t, :, :].rearrange("p e r -> p (e r)"), ident[:])
                last.then_inc(S["wt_ps"], 1)

            def lora_out(i):
                pe.wait_ge(S["axw"], at("axw", i))
                for t in range(NT):
                    last = nc.tensor.matmul(bank[FFN_BANKS[t]][:, 0:P], axw[:, t * P:(t + 1) * P], w_lb[:], start=False, stop=True)
                last.then_inc(S["f0_ps"], 1)

            def qk_to_T(i, n):
                f, t = QT_GROUPS[n]
                done, k = QT_NEEDS[n]
                pe.wait_ge(S[done], at(done, i, k))
                if n >= 4:
                    pe.wait_ge(S["qT"], at("qT", i, n - 3))
                for k in range(4):
                    src = qr[:, t, 2 * (f + k):2 * (f + k) + 2, :].rearrange("p h f -> p (h f)")
                    last = nc.tensor.transpose(quarters(QT_BANKS[n])[:, k, :], src, ident[:])
                last.then_inc(S["qT_ps"], 1)

            def largest(i, n):
                hp, q, t = MAX_STEPS[n]
                if n in MAX_NEEDS:
                    pe.wait_ge(S["qTb"], at("qTb", i, MAX_NEEDS[n]))
                if n >= 4:
                    pe.wait_ge(S["mx"], at("mx", i, n - 3))
                for m in range(2):
                    f, a = 2 * q + m, DH * hp
                    last = nc.tensor.matmul(halves(MAX_BANKS[n % 4])[:, m, :], qTb[a:a + DH, f, t * P:(t + 1) * P],
                                            qTb[a:a + DH, NF + 2 * f // REP, :], start=True, stop=True)
                last.then_inc(S["ms_ps"], 1)

            def qkv(i, t):
                for n in range(3):
                    nc.tensor.matmul(bank[QKV_BANKS[t][n]][:], h3[:, t * P:(t + 1) * P], w_qkv[:, 512 * n:512 * n + 512],
                                     start=True, stop=True).then_inc(S["qkv_ps"], 1)

            def largest_scores(i, nxt):
                pe.wait_ge(S["va"], at("va", i))
                if nxt:
                    first_spread_b(i + 1)
                for name, k in (("rotc", 5), ("rotc", 6), ("rsum", 1), ("rsum", 2), ("rsum", 4), ("rms", 5)):
                    pe.wait_ge(S[name], at(name, i, k))
                    keep_warm("S0", 3)
                for n in range(4):
                    qk_to_T(i, n)
                for n in range(4):
                    if n == 3:
                        pe.wait_ge(S["qT"], at("qT", i, 3))
                    largest(i, n)
                qk_to_T(i, 4)
                qk_to_T(i, 5)
                for n in range(4, 16):
                    largest(i, n)
                    if nxt and n == 4:
                        pe.wait_ge(S["db"], at("db", i + 1, 1))
                    if 4 <= n < 12:
                        keep_warm("B", 1)
                    if n == 13:
                        pe.wait_ge(S["qT"], at("qT", i, 5))
                    if n >= 13:
                        keep_warm("Y", 1)
                    if nxt and n == 12:
                        spread_b(i + 1, 1)
                        spread_c(i + 1, 0)
                pe.wait_ge(S["qT"], at("qT", i))
                keep_warm("Y", 8)
                pe.wait_ge(S["mn"], at("mn", i))
                for t in range(NT):
                    last = nc.tensor.transpose(bank["M"][:, t * P // 2:(t + 1) * P // 2].bitcast(BF16), mn[:, t, :], identb[:])
                last.then_inc(S["mn_ps"], 1)
                keep_warm("Y", 3)

            def turn(i, prev, cur, nxt):
                if cur:
                    spread_b(i, 2)
                if prev:
                    scores(i - 1, 0)
                for p in range(8):
                    if cur and 0 < p < 7:
                        spread_c(i, p)
                    if cur and 0 < p < 6:
                        spread_b(i, p + 2)
                    if prev:
                        scores(i - 1, 2 * p + 1)
                    if nxt and p == 7:
                        if prev:
                            pe.wait_ge(S["ot"], at("ot", i - 1, 2))
                        turn_xn(i + 1, 0, "M")
                    if prev and p < 7:
                        weighted(i - 1, 2 * p)
                        scores(i - 1, 2 * p + 2)
                    if cur and p == 6:
                        spread_c(i, 7)
                    if prev and p < 7:
                        weighted(i - 1, 2 * p + 1)
                        if p in (3, 5):
                            heads_to_T(i - 1, (p - 3) // 2)
                if cur:
                    sum_states(i)
                    scan_proj(i)
                if prev:
                    weighted(i - 1, 14)
                    weighted(i - 1, 15)
                    if nxt:
                        pe.wait_ge(S["h1"], at("h1", i + 1))
                    heads_to_T(i - 1, 2)
                    attention_out(i - 1, 2, range(0, 4))
                    if cur:
                        pe.wait_ge(S["yT"], at("yT", i))
                    heads_to_T(i - 1, 3)
                if nxt:
                    pe.wait_ge(S["h1"], at("h1", i + 1))
                    if cur:
                        pe.wait_ge(S["gz"], at("gz", i))
                    if prev:
                        pe.wait_ge(S["on"], at("on", i - 1, 7))
                    z_proj(i + 1)
                if cur:
                    if prev:
                        pe.wait_ge(S["ot"], at("ot", i - 1))
                    turn_xn(i, 1, "B")
                if prev:
                    attention_out(i - 1, 3, range(4, NF - 2))
                if cur:
                    router_and_lora_a(i)
                if prev:
                    attention_out(i - 1, 4, range(NF - 2, NF))
                if cur:
                    pe.wait_ge(S["x1"], at("x1", i))
                    base_out(i)
                    weighted_a_to_T(i)
                if nxt:
                    if cur:
                        pe.wait_ge(S["bc3"], at("bc3", i))
                    conv(i + 1, 0, 0)
                if cur:
                    lora_out(i)
                if nxt:
                    conv(i + 1, 0, 1)
                    conv(i + 1, 1, 0)
                    conv(i + 1, 1, 1)
                    bc_proj(i + 1)
                if cur and not nxt:
                    for k in (2, 5, 8):
                        pe.wait_ge(S["ln23"], at("ln23", i, k))
                        keep_warm("M", 2)
                if cur:
                    turn_xn(i, 2, "B")
                if prev:
                    turn_xn(i - 1, 3, "M")
                if cur:
                    pe.wait_ge(S["h3"], at("h3", i))
                    pe.wait_ge(S["x2"], at("x2", i))
                    if prev:
                        pe.wait_ge(S["x3"], at("x3", i - 1))
                    qkv(i, 0)
                if nxt:
                    pe.wait_ge(S["gz"], at("gz", i + 1))
                    pe.wait_ge(S["bc_rest"], at("bc_rest", i + 1, 1))
                if prev:
                    keys_and_receptance(i - 1)
                if cur:
                    qkv(i, 1)
                if prev:
                    values(i - 1)
                    pe.wait_ge(S["thr"], at("thr", i - 1))
                if nxt:
                    dt_proj(i + 1)
                    pe.wait_ge(S["thd"], at("thd", i + 1))
                if cur:
                    largest_scores(i, nxt)

            pe.wait_ge(s_pre_dve, 4)
            pe.wait_ge(s_pre_act, 6)
            turn(-1, False, False, True)
            pe.wait_ge(s_pre_dve, 5)
            first_spread_b(0)
            spread_c(0, 0)
            spread_b(0, 1)
            pe.wait_ge(s_w1, LATE)
            pe.wait_ge(s_onehot, 1)
            turn(0, False, True, True)
            with pe.Fori(1, B - 1) as i:
                turn(i, True, True, True)
            turn(B - 1, True, True, False)
            turn(B, True, False, False)


Y_BANKS = ("Y", "B")
OUT0_BANKS = ("Y", "C")
FFN_BANKS = ("C", "Y")
DECAYS = (2, 0, 1, 3, 4, 5, 6, 7)
DECAY_AT = {0: 3, 1: 4, 2: 5, 4: 6, 5: 7}
HEADS_BANKS = "MMMB"
O_BANKS = ("S0", "S1")
QKV_BANKS = (("B", "C", "S0"), ("S1", "O0", "O1"))
HEADS_OF = (slice(0, 8), slice(8, H), slice(H, HK))
QT_GROUPS = ((NF, 0), (NF, 1), (0, 0), (4, 0), (0, 1), (4, 1))
QT_COPIES = ((0, 0), (1, 0), (2, 0), (0, 1), (1, 1), (2, 1), (3, 0), (3, 1), (4, 0), (4, 1), (5, 0), (5, 1))
QT_NEEDS = (("qr", 1), ("qr", 2), ("qr", 3), ("qr", 4), ("qr1", 1), ("qr1", 2))
QT_BANKS = ("Y", "M", "O1", "C", "Y", "M")
MAX_BANKS = ("S0", "S1", "O0", "O1")
MAX_STEPS = [(hp, q, t) for t in range(NT) for q in range(NF // 2) for hp in range(2)]
MAX_NEEDS = {0: 3, 4: 4, 8: 5, 12: 6}


def kernel(**inputs):
    import numpy as np
    import concourse.bacc as bacc
    from concourse.bass_utils import run_bass_kernel_spmd as run

    a = {k: np.asarray(v) for k, v in inputs.items()}
    m0, m1, f0, f1 = "L0_attn_", "L1_attn_", "L0_ffn_", "L1_ffn_"

    def tiles(w):
        w = w.reshape((w.shape[0] // P, P) + w.shape[1:])
        return np.moveaxis(w, 0, 1)

    in_w = a[m0 + "in_proj_w"]
    bc = np.concatenate([a[m0 + "B_w"], a[m0 + "C_w"]]).T
    mod = np.stack([a["L0_wmod"], a["L1_wmod"]]).reshape(2, P, 6, P)
    pos = np.maximum(np.arange(T, dtype=np.float32) - 1, 0)
    inv_freq = (1.0 / np.float32(10000.0) ** (np.arange(0, DH, 2, dtype=np.float32) / DH)).astype(np.float32)
    angle = np.concatenate([pos[:, None] * inv_freq[None, :]] * 2, axis=1).astype(np.float32)
    sign = np.where(np.arange(DH) < DH // 2, -1.0, 1.0).astype(np.float32)
    cs = np.stack([np.cos(angle), np.sin(angle) * sign], axis=1).astype(np.float32)
    pick = np.zeros((P, 32 + H), np.float32)
    for p in range(P):
        pick[p, p % 32] = 1.0
        if p % 64 < H:
            pick[p, 32 + p % 64] = 1.0
    arrays = {
        "x": a[m0 + "x"],
        "cT": np.stack([a["L0_c"].T, a["L1_c"].T], axis=1),
        "wmod": np.moveaxis(mod, 0, 1),
        "w_inx": tiles(in_w[:DI]),
        "w_conv": tiles(a[m0 + "conv_w"].transpose(1, 2, 0)),
        "w_z": in_w[DI:].T,
        "cols": np.concatenate([tiles(a[m0 + "conv_b"]), tiles(a[m0 + "dt_b"]), tiles(a[m0 + "D"]),
                                a[f1 + "mu_r"][:, None], a[f1 + "mu_k"][:, None]], axis=1),
        "a_log": tiles(a[m0 + "A_log"]),
        "pick": pick,
        "w_dt": tiles(a[m0 + "dt_w"].T),
        "w_bc": tiles(np.concatenate([bc, bc, bc], axis=1)),
        "cs": tiles(cs),
        "w_out": tiles(a[m0 + "out_w"].T),
        "w_base": a[f0 + "base_w"].T,
        "w_la": a[f0 + "lora_A"].transpose(1, 0, 2).reshape(P, E * R),
        "w_lb": a[f0 + "lora_B"].reshape(E * R, P),
        "w_rt": a[f0 + "router_w"].T,
        "rows": np.broadcast_to(np.concatenate([a[f0 + "base_b"], a[f0 + "router_b"]]), (P, P + E)),
        "norm_w": np.broadcast_to(np.stack([a[m1 + "q_norm_w"], a[m1 + "k_norm_w"]]), (P, 2, DH)),
        "w_qkv": np.concatenate([a[m1 + "Wq"], a[m1 + "Wk"], a[m1 + "Wv"]]).T,
        "w_o": tiles(a[m1 + "Wo"].T),
        "w_r": a[f1 + "W_r"].T,
        "w_k": a[f1 + "W_k"].T,
        "w_v": a[f1 + "W_v"].T,
    }
    arrays = {k: np.ascontiguousarray(v) for k, v in arrays.items()}
    nc = bacc.Bacc("TRN2", target_bir_lowering=False, num_devices=1)
    d = {k: nc.dram_tensor(f"in_{k}", v.shape, mybir.dt.from_np(v.dtype), kind="ExternalInput").ap()
         for k, v in arrays.items()}
    out = nc.dram_tensor("out", (B, T, P), F32, kind="ExternalOutput").ap()
    build(nc, d, out)
    r = run(nc, [{f"in_{k}": v for k, v in arrays.items()}], core_ids=[0])
    return r.results[0]["out"]
```
